# Optimizing a Trainium2 kernel written in Bass

```python
import numpy as np
import jax
import jax.numpy as jnp

def _softmax(x, axis=-1):
    return jax.nn.softmax(x, axis=axis)

def _gelu(x):
    return jax.nn.gelu(x, approximate=True)

def _silu(x):
    return jax.nn.silu(x)

def _sigmoid(x):
    return jax.nn.sigmoid(x)

def _layernorm(x, axis=-1, eps=1e-05):
    m = jnp.mean(x, axis=axis, keepdims=True)
    v = jnp.var(x, axis=axis, keepdims=True)
    return (x - m) / jnp.sqrt(v + eps)

def _scatter_add(tgt, idx, src, axis=0):
    return tgt.at[idx].add(src)

def _segment_sum(src, seg, n):
    return jax.ops.segment_sum(src, seg, n)
kernel_name = 'mk_perceiver_d1_seqx_r8_f0644d'

def setup_inputs(seed: int=0):
    np.random.seed(seed)
    _w = jnp.asarray

    def _rec_inputs():
        import jax
        import jax.numpy as jnp
        _rk = jax.random.key(seed)
        x = 7.22e-05 + 1 * jax.random.normal(jax.random.fold_in(_rk, 1), (32, 64, 256), jnp.float32)
        _lenS = 64 - jax.random.randint(jax.random.fold_in(_rk, 7), (32,), 0, max(1, 64 // 4) + 1, jnp.int32)
        _lenS2 = 128 - jax.random.randint(jax.random.fold_in(_rk, 8), (32,), 0, max(1, 128 // 4) + 1, jnp.int32)
        _ctx_2048P = jax.random.normal(jax.random.fold_in(_rk, 11), (32, 16, 256), jnp.float32)
        _ctx_2048c = jax.random.dirichlet(jax.random.fold_in(_rk, 511), 0.3 * jnp.ones((16,), jnp.float32), (32, 128))
        _ctx_2048t = jnp.einsum('bsk,bkd->bsd', _ctx_2048c, _ctx_2048P)
        _ctx_2048t = _ctx_2048t * jax.lax.rsqrt(jnp.mean(jnp.square(_ctx_2048t)) + 1e-12) * 0.953939
        ctx_2048 = -0.000514642 + 1.00011 * (_ctx_2048t + 0.3 * jax.random.normal(jax.random.fold_in(_rk, 611), (32, 128, 256), jnp.float32))
        return (x, ctx_2048)
    x, ctx_2048 = _rec_inputs()

    def _L0_xattn_setup():
        import jax, jax.numpy as jnp
        import numpy as np
        HIDDEN = 256
        NUM_HEADS = 16
        NUM_KV_HEADS = 4
        HEAD_DIM = 128
        ROPE_THETA = 10000.0
        EPS = 1e-06

        def rms_norm(x, w, eps=EPS):
            var = jnp.mean(jnp.square(x), axis=-1, keepdims=True)
            return x * jax.lax.rsqrt(var + eps) * w

        def rope_cache(L, head_dim, theta, dtype):
            inv_freq = 1.0 / theta ** (jnp.arange(0, head_dim, 2, dtype=jnp.float32) / head_dim)
            t = jnp.arange(L, dtype=jnp.float32)
            freqs = jnp.outer(t, inv_freq)
            emb = jnp.concatenate([freqs, freqs], -1)
            cos = jnp.cos(emb).astype(dtype)[None, :, None, :]
            sin = jnp.sin(emb).astype(dtype)[None, :, None, :]
            return (cos, sin)

        def rotate_half(x):
            x1, x2 = jnp.split(x, 2, axis=-1)
            return jnp.concatenate([-x2, x1], axis=-1)
        key = jax.random.key(seed)
        ks = jax.random.split(key, 10)
        B, L, T = (2, 256, 64)
        q_out = NUM_HEADS * HEAD_DIM
        kv_out = NUM_KV_HEADS * HEAD_DIM
        s = lambda fan_in: 1.0 / np.sqrt(fan_in)
        return {'x': jax.random.normal(ks[0], (B, L, HIDDEN), jnp.float32), 'h_ctx_kv': jax.random.normal(ks[1], (B, T, HIDDEN), jnp.float32), 'wq': jax.random.normal(ks[2], (HIDDEN, q_out), jnp.float32) * s(HIDDEN), 'wk': jax.random.normal(ks[3], (HIDDEN, kv_out), jnp.float32) * s(HIDDEN), 'wv': jax.random.normal(ks[4], (HIDDEN, kv_out), jnp.float32) * s(HIDDEN), 'wo': jax.random.normal(ks[5], (q_out, HIDDEN), jnp.float32) * s(q_out), 'wk_ctx': jax.random.normal(ks[6], (HIDDEN, kv_out), jnp.float32) * s(HIDDEN), 'wv_ctx': jax.random.normal(ks[7], (HIDDEN, kv_out), jnp.float32) * s(HIDDEN), 'q_norm_w': jnp.ones((HEAD_DIM,), jnp.float32), 'k_norm_w': jnp.ones((HEAD_DIM,), jnp.float32)}
    _L0_xattn_all = _L0_xattn_setup()
    _L0_xattn_in = {k: v for k, v in _L0_xattn_all.items() if k in ('wq', 'wk', 'wv', 'wo', 'wk_ctx', 'wv_ctx', 'q_norm_w', 'k_norm_w')}
    del _L0_xattn_all

    def _L0_attn_setup():
        import jax, jax.numpy as jnp
        import numpy as np
        D_INNER, D_STATE, DT_RANK = (256, 16, 128)
        BATCH, SEQ_LEN = (2, 256)

        def _selective_scan(x, dt, A, B, C):
            dA = jnp.exp(dt[..., None] * A[None, None])
            dBx = dt[..., None] * B[:, :, None, :] * x[..., None]
            dA_t = jnp.moveaxis(dA, 1, 0)
            dBx_t = jnp.moveaxis(dBx, 1, 0)
            C_t = jnp.moveaxis(C, 1, 0)

            def step(h, inputs):
                a, bx, c = inputs
                h = a * h + bx
                y = jnp.einsum('bdn,bn->bd', h, c)
                return (h, y)
            h0 = jnp.zeros((x.shape[0], x.shape[2], A.shape[1]), dtype=x.dtype)
            _, ys = jax.lax.scan(step, h0, (dA_t, dBx_t, C_t))
            return jnp.moveaxis(ys, 0, 1)
        key = jax.random.key(seed)
        ks = jax.random.split(key, 6)
        x = jax.random.normal(ks[0], (BATCH, SEQ_LEN, D_INNER), dtype=jnp.float32)
        x_proj_w = jax.random.normal(ks[1], (DT_RANK + 2 * D_STATE, D_INNER), dtype=jnp.float32) * D_INNER ** (-0.5)
        dt_init_std = DT_RANK ** (-0.5)
        dt_proj_w = jax.random.uniform(ks[2], (D_INNER, DT_RANK), dtype=jnp.float32, minval=-dt_init_std, maxval=dt_init_std)
        dt = jnp.exp(jax.random.uniform(ks[3], (D_INNER,), dtype=jnp.float32) * (np.log(0.1) - np.log(0.001)) + np.log(0.001))
        dt_proj_b = dt + jnp.log(-jnp.expm1(-dt))
        A_log = jnp.broadcast_to(jnp.log(jnp.arange(1, D_STATE + 1, dtype=jnp.float32))[None, :], (D_INNER, D_STATE))
        D = jnp.ones((D_INNER,), dtype=jnp.float32)
        return {'x': x, 'x_proj_w': x_proj_w, 'dt_proj_w': dt_proj_w, 'dt_proj_b': dt_proj_b, 'A_log': A_log, 'D': D}
    _L0_attn_all = _L0_attn_setup()
    _L0_attn_in = {k: v for k, v in _L0_attn_all.items() if k in ('x_proj_w', 'dt_proj_w', 'dt_proj_b', 'A_log', 'D')}
    del _L0_attn_all

    def _L0_ffn_setup():
        import jax, jax.numpy as jnp
        import numpy as np
        B, S, D = (2, 256, 256)
        H, HD = (16, 128)
        E, K, I = (16, 6, 176)
        SI = 352
        EPS = 1e-06

        def rmsnorm(x, w):
            v = jnp.mean(jnp.square(x), axis=-1, keepdims=True)
            return x * jax.lax.rsqrt(v + EPS) * w
        key = jax.random.key(seed)
        ks = jax.random.split(key, 14)
        s = 0.02
        return {'hidden_states': jax.random.normal(ks[0], (B, S, D), jnp.float32), 'ln1_w': jnp.ones((D,), jnp.float32), 'ln2_w': jnp.ones((D,), jnp.float32), 'wq': jax.random.normal(ks[1], (D, H * HD), jnp.float32) * s, 'wk': jax.random.normal(ks[2], (D, H * HD), jnp.float32) * s, 'wv': jax.random.normal(ks[3], (D, H * HD), jnp.float32) * s, 'wo': jax.random.normal(ks[4], (H * HD, D), jnp.float32) * s, 'gate_w': jax.random.normal(ks[5], (E, D), jnp.float32) * s, 'eg_w': jax.random.normal(ks[6], (E, I, D), jnp.float32) * s, 'eu_w': jax.random.normal(ks[7], (E, I, D), jnp.float32) * s, 'ed_w': jax.random.normal(ks[8], (E, D, I), jnp.float32) * s, 'sg_w': jax.random.normal(ks[9], (SI, D), jnp.float32) * s, 'su_w': jax.random.normal(ks[10], (SI, D), jnp.float32) * s, 'sd_w': jax.random.normal(ks[11], (D, SI), jnp.float32) * s}
    _L0_ffn_all = _L0_ffn_setup()
    _L0_ffn_in = {k: v for k, v in _L0_ffn_all.items() if k in ('ln1_w', 'ln2_w', 'wq', 'wk', 'wv', 'wo', 'gate_w', 'eg_w', 'eu_w', 'ed_w', 'sg_w', 'su_w', 'sd_w')}
    del _L0_ffn_all
    return {'x': x, 'ctx_2048': ctx_2048, 'L0_xattn_wq': _L0_xattn_in['wq'], 'L0_xattn_wk': _L0_xattn_in['wk'], 'L0_xattn_wv': _L0_xattn_in['wv'], 'L0_xattn_wo': _L0_xattn_in['wo'], 'L0_xattn_wk_ctx': _L0_xattn_in['wk_ctx'], 'L0_xattn_wv_ctx': _L0_xattn_in['wv_ctx'], 'L0_xattn_q_norm_w': _L0_xattn_in['q_norm_w'], 'L0_xattn_k_norm_w': _L0_xattn_in['k_norm_w'], 'L0_attn_x_proj_w': _L0_attn_in['x_proj_w'], 'L0_attn_dt_proj_w': _L0_attn_in['dt_proj_w'], 'L0_attn_dt_proj_b': _L0_attn_in['dt_proj_b'], 'L0_attn_A_log': _L0_attn_in['A_log'], 'L0_attn_D': _L0_attn_in['D'], 'L0_ffn_ln1_w': _L0_ffn_in['ln1_w'], 'L0_ffn_ln2_w': _L0_ffn_in['ln2_w'], 'L0_ffn_wq': _L0_ffn_in['wq'], 'L0_ffn_wk': _L0_ffn_in['wk'], 'L0_ffn_wv': _L0_ffn_in['wv'], 'L0_ffn_wo': _L0_ffn_in['wo'], 'L0_ffn_gate_w': _L0_ffn_in['gate_w'], 'L0_ffn_eg_w': _L0_ffn_in['eg_w'], 'L0_ffn_eu_w': _L0_ffn_in['eu_w'], 'L0_ffn_ed_w': _L0_ffn_in['ed_w'], 'L0_ffn_sg_w': _L0_ffn_in['sg_w'], 'L0_ffn_su_w': _L0_ffn_in['su_w'], 'L0_ffn_sd_w': _L0_ffn_in['sd_w']}

def reference(x, ctx_2048, L0_xattn_wq, L0_xattn_wk, L0_xattn_wv, L0_xattn_wo, L0_xattn_wk_ctx, L0_xattn_wv_ctx, L0_xattn_q_norm_w, L0_xattn_k_norm_w, L0_attn_x_proj_w, L0_attn_dt_proj_w, L0_attn_dt_proj_b, L0_attn_A_log, L0_attn_D, L0_ffn_ln1_w, L0_ffn_ln2_w, L0_ffn_wq, L0_ffn_wk, L0_ffn_wv, L0_ffn_wo, L0_ffn_gate_w, L0_ffn_eg_w, L0_ffn_eu_w, L0_ffn_ed_w, L0_ffn_sg_w, L0_ffn_su_w, L0_ffn_sd_w):
    import jax
    import jax.numpy as jnp

    def _L0_xattn_ref(x, h_ctx_kv, wq, wk, wv, wo, wk_ctx, wv_ctx, q_norm_w, k_norm_w):
        import jax, jax.numpy as jnp
        import numpy as np
        HIDDEN = 256
        NUM_HEADS = 16
        NUM_KV_HEADS = 4
        HEAD_DIM = 128
        ROPE_THETA = 10000.0
        EPS = 1e-06

        def rms_norm(x, w, eps=EPS):
            var = jnp.mean(jnp.square(x), axis=-1, keepdims=True)
            return x * jax.lax.rsqrt(var + eps) * w

        def rope_cache(L, head_dim, theta, dtype):
            inv_freq = 1.0 / theta ** (jnp.arange(0, head_dim, 2, dtype=jnp.float32) / head_dim)
            t = jnp.arange(L, dtype=jnp.float32)
            freqs = jnp.outer(t, inv_freq)
            emb = jnp.concatenate([freqs, freqs], -1)
            cos = jnp.cos(emb).astype(dtype)[None, :, None, :]
            sin = jnp.sin(emb).astype(dtype)[None, :, None, :]
            return (cos, sin)

        def rotate_half(x):
            x1, x2 = jnp.split(x, 2, axis=-1)
            return jnp.concatenate([-x2, x1], axis=-1)
        B, L, _ = x.shape
        T = h_ctx_kv.shape[1]
        rep = NUM_HEADS // NUM_KV_HEADS
        q = (x @ wq).reshape(B, L, NUM_HEADS, HEAD_DIM)
        k = (x @ wk).reshape(B, L, NUM_KV_HEADS, HEAD_DIM)
        v = (x @ wv).reshape(B, L, NUM_KV_HEADS, HEAD_DIM)
        q = rms_norm(q, q_norm_w)
        k = rms_norm(k, k_norm_w)
        k_ctx = (h_ctx_kv @ wk_ctx).reshape(B, T, NUM_KV_HEADS, HEAD_DIM)
        v_ctx = (h_ctx_kv @ wv_ctx).reshape(B, T, NUM_KV_HEADS, HEAD_DIM)
        k_ctx = rms_norm(k_ctx, k_norm_w)
        cos, sin = rope_cache(L, HEAD_DIM, ROPE_THETA, x.dtype)
        q = q * cos + rotate_half(q) * sin
        k = k * cos + rotate_half(k) * sin
        k_full = jnp.concatenate([k_ctx, k], axis=1)
        v_full = jnp.concatenate([v_ctx, v], axis=1)
        k_full = jnp.repeat(k_full, rep, axis=2)
        v_full = jnpp_repeat = jnp.repeat(v_full, rep, axis=2)
        i = jnp.arange(L)[:, None]
        j = jnp.arange(L)[None, :]
        causal = jnp.where(j > i, -jnp.inf, 0.0).astype(x.dtype)
        mask = jnp.concatenate([jnp.zeros((L, T), x.dtype), causal], axis=1)
        scale = 1.0 / np.sqrt(HEAD_DIM)
        scores = jnp.einsum('blhd,bmhd->bhlm', q, k_full) * scale + mask
        probs = jax.nn.softmax(scores, axis=-1)
        out = jnp.einsum('bhlm,bmhd->blhd', probs, v_full)
        out = out.reshape(B, L, NUM_HEADS * HEAD_DIM)
        return out @ wo

    def _L0_attn_ref(x, x_proj_w, dt_proj_w, dt_proj_b, A_log, D):
        import jax, jax.numpy as jnp
        import numpy as np
        D_INNER, D_STATE, DT_RANK = (256, 16, 128)
        BATCH, SEQ_LEN = (2, 256)

        def _selective_scan(x, dt, A, B, C):
            dA = jnp.exp(dt[..., None] * A[None, None])
            dBx = dt[..., None] * B[:, :, None, :] * x[..., None]
            dA_t = jnp.moveaxis(dA, 1, 0)
            dBx_t = jnp.moveaxis(dBx, 1, 0)
            C_t = jnp.moveaxis(C, 1, 0)

            def step(h, inputs):
                a, bx, c = inputs
                h = a * h + bx
                y = jnp.einsum('bdn,bn->bd', h, c)
                return (h, y)
            h0 = jnp.zeros((x.shape[0], x.shape[2], A.shape[1]), dtype=x.dtype)
            _, ys = jax.lax.scan(step, h0, (dA_t, dBx_t, C_t))
            return jnp.moveaxis(ys, 0, 1)
        x_dbl = jnp.einsum('bld,ed->ble', x, x_proj_w)
        dt_low, B, C = jnp.split(x_dbl, [DT_RANK, DT_RANK + D_STATE], axis=-1)
        dt = jax.nn.softplus(jnp.einsum('blr,dr->bld', dt_low, dt_proj_w) + dt_proj_b)
        A = -jnp.exp(A_log)
        y = _selective_scan(x, dt, A, B, C)
        return y + D[None, None, :] * x

    def _L0_ffn_ref(hidden_states, ln1_w, ln2_w, wq, wk, wv, wo, gate_w, eg_w, eu_w, ed_w, sg_w, su_w, sd_w):
        import jax, jax.numpy as jnp
        import numpy as np
        B, S, D = (2, 256, 256)
        H, HD = (16, 128)
        E, K, I = (16, 6, 176)
        SI = 352
        EPS = 1e-06

        def rmsnorm(x, w):
            v = jnp.mean(jnp.square(x), axis=-1, keepdims=True)
            return x * jax.lax.rsqrt(v + EPS) * w
        b, s, d = hidden_states.shape
        x = hidden_states
        h = rmsnorm(x, ln1_w)
        q = (h @ wq).reshape(b, s, H, HD)
        k = (h @ wk).reshape(b, s, H, HD)
        v = (h @ wv).reshape(b, s, H, HD)
        scores = jnp.einsum('bqhd,bkhd->bhqk', q, k) / np.sqrt(HD).astype(np.float32)
        causal = jnp.tril(jnp.ones((s, s), bool))
        scores = jnp.where(causal, scores, jnp.float32(-1000000000.0))
        attn = jax.nn.softmax(scores, axis=-1)
        ao = jnp.einsum('bhqk,bkhd->bqhd', attn, v).reshape(b, s, H * HD) @ wo
        x = x + ao
        h = rmsnorm(x, ln2_w)
        t = h.reshape(-1, d)
        T = t.shape[0]
        logits = t @ gate_w.T
        probs = jax.nn.softmax(logits, axis=-1)
        topv, topi = jax.lax.top_k(probs, K)
        topv = topv / jnp.sum(topv, axis=-1, keepdims=True)
        cw = jnp.zeros((T, E), t.dtype).at[jnp.arange(T)[:, None], topi].add(topv)
        g = jnp.einsum('td,eid->eti', t, eg_w)
        u = jnp.einsum('td,eid->eti', t, eu_w)
        hh = jax.nn.silu(g) * u
        routed = jnp.einsum('eti,edi,te->td', hh, ed_w, cw)
        shared = jax.nn.silu(t @ sg_w.T) * (t @ su_w.T) @ sd_w.T
        out = x + (routed + shared).reshape(b, s, d)
        return out
    x = x + _L0_xattn_ref(_layernorm(x, axis=-1), ctx_2048, L0_xattn_wq, L0_xattn_wk, L0_xattn_wv, L0_xattn_wo, L0_xattn_wk_ctx, L0_xattn_wv_ctx, L0_xattn_q_norm_w, L0_xattn_k_norm_w)
    x = x + _L0_attn_ref(_layernorm(x, axis=-1), L0_attn_x_proj_w, L0_attn_dt_proj_w, L0_attn_dt_proj_b, L0_attn_A_log, L0_attn_D)
    x = x + _L0_ffn_ref(_layernorm(x, axis=-1), L0_ffn_ln1_w, L0_ffn_ln2_w, L0_ffn_wq, L0_ffn_wk, L0_ffn_wv, L0_ffn_wo, L0_ffn_gate_w, L0_ffn_eg_w, L0_ffn_eu_w, L0_ffn_ed_w, L0_ffn_sg_w, L0_ffn_su_w, L0_ffn_sd_w)
    return x

_drawn_inputs = setup_inputs


def setup_inputs(seed=0):
    import zlib

    import numpy as np

    out = dict(_drawn_inputs(seed))
    spreads = {'L0_xattn_q_norm_w': (1.0, 0.2),
     'L0_xattn_k_norm_w': (1.0, 0.2),
     'L0_attn_D': (1.0, 0.2),
     'L0_ffn_ln1_w': (1.0, 0.6),
     'L0_ffn_ln2_w': (1.0, 0.6)}
    factors = {'L0_ffn_wq': 8.0,
     'L0_ffn_wk': 8.0,
     'L0_ffn_gate_w': 8.0,
     'L0_ffn_eg_w': 8.0,
     'L0_ffn_eu_w': 8.0,
     'L0_ffn_ed_w': 8.0,
     'L0_ffn_sg_w': 8.0,
     'L0_ffn_su_w': 8.0,
     'L0_ffn_sd_w': 7.973}
    for name, (base, spread) in spreads.items():
        noise = np.random.default_rng([zlib.crc32(name.encode()), seed]).standard_normal(out[name].shape)
        drawn = base * np.exp(spread * noise) if base else spread * noise
        out[name] = jnp.asarray(drawn.astype(out[name].dtype))
    for name, factor in factors.items():
        out[name] = (out[name] * factor).astype(out[name].dtype)
    return out
```

```python
from contextlib import ExitStack

import numpy as np

import concourse.bass as bass
from concourse import mybir

F32 = mybir.dt.float32
F32R = mybir.dt.float32r
ALU = mybir.AluOpType
ACT = mybir.ActivationFunctionType
AX = mybir.AxisListType

P = 128
BATCH, LEN, DIM = 32, 64, 256
CTX = 128
NT = BATCH * LEN // P
KD = DIM // P
HD = 128
NEG = -1.0e30

HI, LO = 0, 1
THREE = ((HI, HI), (HI, LO), (LO, HI))


class Kit:

    def __init__(self, nc, ctx, tag):
        self.nc, self.ctx, self.tag = nc, ctx, tag

    def sb(self, name, shape, dt=F32):
        return self.ctx.enter_context(self.nc.sbuf_tensor(f"{self.tag}_{name}", shape, dt))

    def ps(self, name, shape):
        return self.ctx.enter_context(self.nc.psum_tensor(f"{self.tag}_{name}", shape, F32))

    def sem(self, name):
        return self.ctx.enter_context(self.nc.semaphore(f"{self.tag}_{name}"))

    def sems(self, name, n=2):
        return [self.sem(f"{name}{j}") for j in range(n)]


def product(pe, out, lhs, rhs, start, stop, **kw):
    for n, (a, b) in enumerate(THREE):
        last = pe.matmul(out, lhs(a), rhs(b), start=start and n == 0, stop=stop and n == 2, **kw)
    return last


NQ, NG, REP = 16, 4, 4
KEYS = CTX + LEN


def cross_attention(nc, X, xd, d):
    with ExitStack() as ctx:
        k = Kit(nc, ctx, "xa")
        sb, sem, sems = k.sb, k.sem, k.sems
        WQ = sb("WQ", [P, 2, KD, NQ * HD], F32R)
        WKV = sb("WKV", [P, 2, KD, NG, 2 * HD], F32R)
        WKVC = sb("WKVC", [P, 2, KD, NG, 2 * HD], F32R)
        WO = sb("WO", [P, 2, NQ, DIM], F32R)
        stage = [sb(f"stage{j}", [P, 2048]) for j in range(2)]
        ident = sb("ident", [P, P])
        cosw = [sb(f"cosw{j}", [P, HD]) for j in range(2)]
        sinw = [sb(f"sinw{j}", [P, HD]) for j in range(2)]
        normw = [sb(f"normw{j}", [P, HD]) for j in range(2)]
        cos, sin = sb("cos", [P, HD]), sb("sin", [P, HD])
        mask = sb("mask", [P, LEN])
        mhalf, lneps = sb("mhalf", [P, 8]), sb("lneps", [P, 1])
        stats, mv, rstd, xn = sb("stats", [P, 6]), sb("mv", [P, 2]), sb("rstd", [P, 1]), sb("xn", [P, DIM])
        XT = sb("XT", [P, 2, KD, P], F32R)
        ctx_raw = sb("ctx_raw", [P, KD, 2 * CTX])
        CT = sb("CT", [P, 2, KD, 2 * CTX], F32R)
        sq, t1, t2, qn = sb("sq", [P, 7, HD]), sb("t1", [P, 7, HD]), sb("t2", [P, 5, HD]), sb("qn", [P, 7, HD])
        ss, var, rs = sb("ss", [P, 8]), sb("var", [P, 8]), sb("rs", [P, 8])
        QT = [sb(f"QT{j}", [P, 2, 2, REP * LEN], F32R) for j in range(2)]
        KT = [sb(f"KT{j}", [P, 2, 2, KEYS], F32R) for j in range(2)]
        VS = [sb(f"VS{j}", [P, 2, HD], F32R) for j in range(2)]
        VC = [sb(f"VC{j}", [P, 2, 2, HD], F32R) for j in range(2)]
        PR = [sb(f"PR{b}", [P, 2, KEYS]) for b in range(2)]
        nmax = [sb(f"nmax{b}", [P, 2]) for b in range(2)]
        rsum = [sb(f"rsum{b}", [P, 2]) for b in range(2)]
        rinv = [sb(f"rinv{b}", [P, 2]) for b in range(2)]
        PT = [sb(f"PT{b}", [P, 2, 2, REP * LEN], F32R) for b in range(2)]
        OT = sb("OT", [P, 2, REP, P], F32R)
        J = [k.ps(f"J{j}", [P, 512]) for j in range(2)]
        T = [k.ps(f"T{j}", [P, 512]) for j in range(2)]
        S = [k.ps(f"S{b}", [P, 2, KEYS]) for b in range(2)]
        PO = k.ps("PO", [P, 2, REP * LEN])
        ACC = k.ps("ACC", [P, DIM])

        x_in, tab_in, staged = sem("x_in"), sem("tab_in"), sems("staged")
        w_hi, w_lo, tabs = sem("w_hi"), sem("w_lo"), sem("tabs")
        ctx_in, ct_hi, ct_full = sem("ctx_in"), sem("ct_hi"), sem("ct_full")
        stat_full, mv_full, rstd_full, xn_full = sem("stat_full"), sem("mv_full"), sem("rstd_full"), sem("xn_full")
        J_full = sems("J_full")
        J_act, J_dve = sems("J_act"), sems("J_dve")
        T_full, T_act, T_dve = sems("T_full"), sems("T_act"), sems("T_dve")
        S_full, S_mask = sems("S_full"), sems("S_mask")
        nmax_full, exp_full, rinv_full, pr_full = sems("nmax_full"), sems("exp_full"), sems("rinv_full"), sems("pr_full")
        ss_full, var_full, rs_full, t_sum, qn_full = (sem(n) for n in ("ss_full", "var_full", "rs_full", "t_sum", "qn_full"))
        pv_done, ot_hi, ot_full = sems("pv_done"), sem("ot_hi"), sem("ot_full")
        wo_done, acc_read = sem("wo_done"), sem("acc_read")

        pieces = [(d["wq"].rearrange("(k p) n -> p k n", p=P)[:, c, :], lambda a, c=c: WQ[:, a, c, :]) for c in range(KD)]
        pieces += [(src, lambda a, W=W: W[:, a].rearrange("p k g n -> p (k g n)")) for src, W in ((d["wkv"], WKV), (d["wkvc"], WKVC))]
        pieces += [(d["wo"].rearrange("(h p) n -> p h n", p=P)[:, 8 * c:8 * c + 8, :],
                    lambda a, c=c: WO[:, a, 8 * c:8 * c + 8, :]) for c in range(2)]

        def staging(j):
            view = stage[j % 2][:, :]
            return view.rearrange("p (a n) -> p a n", n=DIM) if len(pieces[j][0].shape) == 3 else view

        def use(n, per, i):
            return n % 2, i * (per // 2) + n // 2

        def j_use(i, g, u):
            return use(5 + 3 * g + (2 if g == 3 else 0) + u, 14, i)

        def j_x(i, c):
            return use(14 + c, 14, i)

        def t_use(i, g, u):
            return use(2 + 4 * g + u, 16, i)

        J_FIRST = [use(n, 14, 0) for n in range(5)]
        T_FIRST = [use(n, 16, 0) for n in range(2)]
        SELF = (slice(0, LEN), slice(CTX, KEYS))
        CKEY = (slice(LEN, KEYS), slice(0, CTX))

        block = ctx.enter_context(nc.Block())

        @block.sync
        def _(sp):
            xt = xd.rearrange("(t p) n -> p t n", p=P)
            sp.dma_start(X[:, 0:2, :], xt[:, 0:2, :]).then_inc(x_in, 16)
            sp.dma_start(ctx_raw[:], d["ctxT"][0]).then_inc(ctx_in, 16)
            for dst, src in ((ident, d["ident"]), (cos, d["cos"]), (sin, d["sin"]), (mask, d["xmask"]),
                             (normw[0], d["qnorm"].partition_broadcast(P)), (normw[1], d["knorm"].partition_broadcast(P))):
                sp.dma_start(dst[:, :], src).then_inc(tab_in, 16)
            for j, (src, _) in enumerate(pieces):
                if j >= 2:
                    sp.wait_ge(w_lo, j - 1)
                sp.dma_start(staging(j), src).then_inc(staged[j % 2], 16)
            sp.wait_ge(x_in, 16)
            sp.dma_start(X[:, 2:, :], xt[:, 2:, :]).then_inc(x_in, 16)
            with sp.Fori(1, NT) as t:
                sp.wait_ge(ct_full, t)
                sp.dma_start(ctx_raw[:].rearrange("p k n -> p (k n)").unsqueeze(1),
                             d["ctxT"].rearrange("t p k n -> p t (k n)")[:, bass.ds(t, 1), :]).then_inc(ctx_in, 16)

        @block.scalar
        def _(act):
            for j, (_, dst) in enumerate(pieces):
                act.wait_ge(staged[j % 2], 16 * (j // 2 + 1))
                act.activation(dst(HI), staging(j), ACT.Copy).then_inc(w_hi, 1)

            def context_split(t):
                act.wait_ge(ctx_in, 16 * t + 16)
                act.activation(CT[:, HI], ctx_raw[:], ACT.Copy).then_inc(ct_hi, 1)

            def x_split(uses):
                for c, (bank, n) in enumerate(uses):
                    act.wait_ge(J_full[bank], n + 1)
                    act.activation(XT[:, HI, c, :], J[bank][:, 0:P], ACT.Copy).then_inc(J_act[bank], 1)

            def project(uses, par):
                (bq, nq), (bc, n_c), (bs, n_s) = uses
                act.wait_ge(J_full[bq], nq + 1)
                act.activation(sq[:, 0:4, :], J[bq][:, :].rearrange("p (h e) -> p h e", h=4), ACT.Square).then_inc(J_act[bq], 1)
                act.wait_ge(J_full[bc], n_c + 1)
                kv = J[bc][:, :].rearrange("p (b n) -> p b n", b=2)
                act.activation(sq[:, 5:7, :], kv[:, :, 0:HD], ACT.Square)
                act.activation(VC[par][:, HI], kv[:, :, HD:], ACT.Copy).then_inc(J_act[bc], 1)
                act.wait_ge(J_full[bs], n_s + 1)
                act.activation(sq[:, 4, :], J[bs][:, 0:HD], ACT.Square)
                act.activation(VS[par][:, HI], J[bs][:, HD:2 * HD], ACT.Copy).then_inc(J_act[bs], 1)

            def qk_split(uses, par):
                (bq, nq), (bk, nk) = uses
                act.wait_ge(T_full[bq], nq + 1)
                act.activation(QT[par][:, HI].rearrange("p b (h l) -> p h b l", h=REP),
                               T[bq][:, :].rearrange("p (h b l) -> p h b l", h=REP, b=2), ACT.Copy).then_inc(T_act[bq], 1)
                act.wait_ge(T_full[bk], nk + 1)
                act.activation(KT[par][:, HI], T[bk][:, 0:2 * KEYS].rearrange("p (b n) -> p b n", b=2),
                               ACT.Copy).then_inc(T_act[bk], 1)

            def slot(i, g, last=False):
                s, par, more = 4 * i + g, (g + 1) % 2, not (last and g == 3)
                for b in range(2):
                    act.wait_ge(nmax_full[b], s + 1)
                    act.wait_ge(pv_done[b], s + 1)
                    for pair in range(2):
                        act.activation(PR[b][:, pair, :], S[b][:, pair, :], ACT.Exp, bias=nmax[b][:, pair:pair + 1],
                                       accum_out=rsum[b][:, pair:pair + 1]).then_inc(exp_full[b], 1)
                if more:
                    act.wait_ge(ss_full, s + 1)
                    act.wait_ge(pv_done[1], s + 1)
                    project([j_use(i, g, u) for u in range(3)], par)
                    if g == 2 and not last:
                        context_split(i + 1)
                for b in range(2):
                    bank, n = t_use(i, g, b)
                    act.wait_ge(T_full[bank], n + 1)
                    act.activation(PT[b][:, HI], T[bank][:, :].rearrange("p (a n) -> p a n", a=2),
                                   ACT.Copy).then_inc(T_act[bank], 1)
                if more:
                    if g == 2 and not last:
                        x_split([j_x(i, c) for c in range(KD)])
                    act.wait_ge(S_full[1], s + 1)
                    qk_split([t_use(i, g, u) for u in (2, 3)], par)
                act.wait_ge(pv_done[1], s + 2)
                act.wait_ge(wo_done, s + 1)
                act.activation(OT[:, HI].rearrange("p h (b l) -> p b h l", b=2),
                               PO[:, :, :].rearrange("p b (h l) -> p b h l", h=REP), ACT.Copy).then_inc(ot_hi, 1)

            context_split(0)
            x_split(J_FIRST[0:2])
            project(J_FIRST[2:5], 0)
            qk_split(T_FIRST, 0)
            with act.Fori(0, NT - 1) as i:
                for g in range(NG):
                    slot(i, g)
            for g in range(NG):
                slot(NT - 1, g, last=True)

        @block.vector
        def _(dve):
            for unused in (ot_full, acc_read):
                dve.sem_inc(unused, 1)
            dve.wait_ge(tab_in, 6 * 16)
            half = HD // 2
            for j, scale in enumerate((HD ** -0.5, 1.0)):
                dve.scalar_tensor_tensor(cosw[j][:], cos[:], scale, normw[j][:], ALU.mult, ALU.mult)
                dve.scalar_tensor_tensor(sinw[j][:, :half], sin[:, :half], scale, normw[j][:, half:], ALU.mult, ALU.mult)
                dve.scalar_tensor_tensor(sinw[j][:, half:], sin[:, half:], scale, normw[j][:, :half], ALU.mult, ALU.mult).then_inc(tabs, 1)

            def norm_stats(x):
                dve.bn_stats(stats[:], x).then_inc(stat_full, 1)

            def norm_var():
                dve.bn_aggr(mv[:], stats[:]).then_inc(mv_full, 1)

            def norm_apply(x, t):
                dve.wait_ge(rstd_full, t + 1)
                dve.tensor_scalar(xn[:], x, mv[:, 0:1], rstd[:, 0:1], ALU.subtract, ALU.mult).then_inc(xn_full, 1)

            dve.wait_ge(x_in, 16)
            norm_stats(X[:, 0, :])
            dve.wait_ge(stat_full, 1)
            norm_var()
            for j, (_, dst) in enumerate(pieces):
                dve.wait_ge(w_hi, j + 1)
                dve.tensor_tensor(dst(LO), staging(j), dst(HI), ALU.subtract).then_inc(w_lo, 1)
            norm_apply(X[:, 0, :], 0)

            def context_split(t):
                dve.wait_ge(ct_hi, t + 1)
                dve.tensor_tensor(CT[:, LO], ctx_raw[:], CT[:, HI], ALU.subtract).then_inc(ct_full, 1)

            def x_split(uses):
                for c, (bank, n) in enumerate(uses):
                    dve.wait_ge(J_act[bank], n + 1)
                    dve.tensor_tensor(XT[:, LO, c, :], J[bank][:, 0:P], XT[:, HI, c, :], ALU.subtract).then_inc(J_dve[bank], 1)

            def rope(src, first, heads, j):
                v = src.rearrange("p (h e) -> p h e", h=heads)
                half = HD // 2
                dve.tensor_tensor(t1[:, first:first + heads, :], v, cosw[j][:, None, :].broadcast_to([P, heads, HD]), ALU.mult)
                dve.tensor_tensor(t2[:, first:first + heads, :half], v[:, :, half:],
                                  sinw[j][:, None, :half].broadcast_to([P, heads, half]), ALU.mult)
                return dve.tensor_tensor(t2[:, first:first + heads, half:], v[:, :, :half],
                                         sinw[j][:, None, half:].broadcast_to([P, heads, half]), ALU.mult)

            def project(uses, par):
                (bq, nq), (bc, n_c), (bs, n_s) = uses
                dve.wait_ge(J_act[bq], nq + 1)
                rope(J[bq][:, :], 0, 4, 0).then_inc(J_dve[bq], 1)
                kv = J[bc][:, :].rearrange("p (b n) -> p b n", b=2)
                dve.wait_ge(J_act[bc], n_c + 1)
                dve.tensor_tensor(t1[:, 5:7, :], kv[:, :, 0:HD], normw[1][:, None, :].broadcast_to([P, 2, HD]), ALU.mult)
                dve.tensor_tensor(VC[par][:, LO], kv[:, :, HD:], VC[par][:, HI], ALU.subtract).then_inc(J_dve[bc], 1)
                dve.wait_ge(J_act[bs], n_s + 1)
                rope(J[bs][:, 0:HD], 4, 1, 1)
                dve.tensor_tensor(VS[par][:, LO], J[bs][:, HD:2 * HD], VS[par][:, HI], ALU.subtract).then_inc(J_dve[bs], 1)
                dve.tensor_reduce(ss[:, 0:7], sq[:, :, :], AX.X, ALU.add).then_inc(ss_full, 1)

            def qk_split(uses, par):
                (bq, nq), (bk, nk) = uses
                dve.wait_ge(T_act[bq], nq + 1)
                dve.tensor_tensor(QT[par][:, LO].rearrange("p b (h l) -> p h b l", h=REP),
                                  T[bq][:, :].rearrange("p (h b l) -> p h b l", h=REP, b=2),
                                  QT[par][:, HI].rearrange("p b (h l) -> p h b l", h=REP), ALU.subtract).then_inc(T_dve[bq], 1)
                dve.wait_ge(T_act[bk], nk + 1)
                dve.tensor_tensor(KT[par][:, LO], T[bk][:, 0:2 * KEYS].rearrange("p (b n) -> p b n", b=2),
                                  KT[par][:, HI], ALU.subtract).then_inc(T_dve[bk], 1)

            def slot(i, g, last=False):
                s, par, more = 4 * i + g, (g + 1) % 2, not (last and g == 3)
                for b in range(2):
                    dve.wait_ge(S_full[b], s + 2)
                    own = S[b][:, :, SELF[b]]
                    dve.tensor_tensor(own, own, mask[:, None, :].broadcast_to([P, 2, LEN]), ALU.add).then_inc(S_mask[b], 1)
                    dve.wait_ge(S_mask[b], s + 1)
                    dve.tensor_reduce(nmax[b][:], S[b][:, :, :], AX.X, ALU.max, negate=True).then_inc(nmax_full[b], 1)
                if g == 1 and not last:
                    norm_stats(X[:, bass.ds(i + 1, 1), :].rearrange("p a n -> p (a n)"))
                if g == 1 and not last:
                    dve.wait_ge(stat_full, i + 2)
                for b in range(2):
                    dve.wait_ge(exp_full[b], 2 * s + 2)
                    dve.reciprocal(rinv[b][:], rsum[b][:]).then_inc(rinv_full[b], 1)
                if g == 1 and not last:
                    norm_var()
                for b in range(2):
                    dve.wait_ge(rinv_full[b], s + 1)
                    for pair in range(2):
                        done = dve.tensor_scalar(PR[b][:, pair, :], PR[b][:, pair, :], rinv[b][:, pair:pair + 1], None, ALU.mult)
                    done.then_inc(pr_full[b], 1)
                if more:
                    dve.wait_ge(qn_full, s + 1)
                    project([j_use(i, g, u) for u in range(3)], par)
                if g == 1 and not last:
                    norm_apply(X[:, bass.ds(i + 1, 1), :].rearrange("p a n -> p (a n)"), i + 1)
                if g == 2 and not last:
                    context_split(i + 1)
                for b in range(2):
                    bank, n = t_use(i, g, b)
                    dve.wait_ge(T_act[bank], n + 1)
                    dve.tensor_tensor(PT[b][:, LO], T[bank][:, :].rearrange("p (a n) -> p a n", a=2),
                                      PT[b][:, HI], ALU.subtract).then_inc(T_dve[bank], 1)
                if more:
                    if g == 2 and not last:
                        x_split([j_x(i, c) for c in range(KD)])
                    qk_split([t_use(i, g, u) for u in (2, 3)], par)
                dve.wait_ge(ot_hi, s + 1)
                dve.tensor_tensor(OT[:, LO].rearrange("p h (b l) -> p b h l", b=2),
                                  PO[:, :, :].rearrange("p b (h l) -> p b h l", h=REP),
                                  OT[:, HI].rearrange("p h (b l) -> p b h l", b=2), ALU.subtract).then_inc(ot_full, 1)
                if g == 3:
                    dve.wait_ge(wo_done, s + 2)
                    x = X[:, bass.ds(i, 1), :].rearrange("p a n -> p (a n)") if not last else X[:, i, :]
                    dve.tensor_tensor(x, ACC[:, :], x, ALU.add).then_inc(acc_read, 1)

            dve.wait_ge(tabs, 2)
            context_split(0)
            x_split(J_FIRST[0:2])
            project(J_FIRST[2:5], 0)
            qk_split(T_FIRST, 0)
            dve.wait_ge(x_in, 32)
            with dve.Fori(0, NT - 1) as i:
                for g in range(NG):
                    slot(i, g)
            for g in range(NG):
                slot(NT - 1, g, last=True)

        @block.gpsimd
        def _(pool):
            pool.memset(lneps[:], 1e-5)
            pool.memset(mhalf[:], -0.5).then_inc(var_full, 1)
            pool.wait_ge(var_full, 1)

            def ln_rstd(t, n):
                pool.wait_ge(mv_full, t + 1)
                pool.tensor_tensor(rstd[:], mv[:, 1:2], lneps[:], ALU.add).then_inc(var_full, 1)
                pool.wait_ge(var_full, n + 1)
                pool.tensor_tensor(rstd[:], rstd[:], mhalf[:, 0:1], ALU.pow).then_inc(rstd_full, 1)

            def norms(s, n):
                pool.wait_ge(ss_full, s + 1)
                pool.tensor_tensor(t1[:, 0:5, :], t1[:, 0:5, :], t2[:, :, :], ALU.add).then_inc(t_sum, 1)
                pool.tensor_scalar(var[:, 0:7], ss[:, 0:7], 1.0 / HD, 1e-6, ALU.mult, ALU.add).then_inc(var_full, 1)
                pool.wait_ge(var_full, n + 1)
                pool.tensor_tensor(rs[:, 0:7], var[:, 0:7], mhalf[:, 0:7], ALU.pow).then_inc(rs_full, 1)
                pool.wait_ge(rs_full, s + 1)
                pool.wait_ge(t_sum, s + 1)
                if not isinstance(s, int) or s > 0:
                    pool.wait_ge(S_full[0], s + 1)
                pool.tensor_tensor(qn[:], t1[:], rs[:, 0:7, None].broadcast_to([P, 7, HD]), ALU.mult).then_inc(qn_full, 1)

            ln_rstd(0, 1)
            norms(0, 2)
            with pool.Fori(0, NT - 1) as i:
                for g in range(NG):
                    if g == 1:
                        ln_rstd(i + 1, 5 * i + 4)
                    norms(4 * i + g + 1, 5 * i + 3 + g + (1 if g >= 1 else 0))
            for g in range(NG - 1):
                norms(4 * (NT - 1) + g + 1, 5 * (NT - 1) + 3 + g)

        @block.tensor
        def _(pe):
            def fill_j(bank, n):
                pe.wait_ge(J_dve[bank], n)

            def x_turn(uses, t):
                pe.wait_ge(xn_full, t + 1)
                for c, (bank, n) in enumerate(uses):
                    fill_j(bank, n)
                    pe.transpose(J[bank][:, 0:P], xn[:, c * P:(c + 1) * P], ident[:]).then_inc(J_full[bank], 1)

            def project(uses, g, t):
                (bq, nq), (bc, n_c), (bs, n_s) = uses
                fill_j(bq, nq)
                if g == 0:
                    fill_j(bc, n_c)
                for c in range(KD):
                    mm = product(pe, J[bq][:, :], lambda a: XT[:, a, c, :], lambda a: WQ[:, a, c, g * 512:(g + 1) * 512],
                                 c == 0, c == KD - 1)
                mm.then_inc(J_full[bq], 1)
                fill_j(bc, n_c)
                if g == 0:
                    pe.wait_ge(ct_full, t + 1)
                for b in range(2):
                    for c in range(KD):
                        mm = product(pe, J[bc][:, b * 256:(b + 1) * 256], lambda a: CT[:, a, c, b * CTX:(b + 1) * CTX],
                                     lambda a: WKVC[:, a, c, g, :], c == 0, c == KD - 1)
                mm.then_inc(J_full[bc], 1)
                fill_j(bs, n_s)
                for c in range(KD):
                    mm = product(pe, J[bs][:, 0:256], lambda a: XT[:, a, c, :], lambda a: WKV[:, a, c, g, :], c == 0, c == KD - 1)
                mm.then_inc(J_full[bs], 1)

            def qk_turn(uses, s):
                (bq, nq), (bk, nk) = uses
                pe.wait_ge(qn_full, s + 1)
                pe.wait_ge(T_dve[bq], nq)
                for h in range(REP):
                    mm = pe.transpose(T[bq][:, h * P:(h + 1) * P], qn[:, h, :], ident[:])
                mm.then_inc(T_full[bq], 1)
                pe.wait_ge(T_dve[bk], nk)
                for b in range(2):
                    mm = pe.transpose(T[bk][:, b * KEYS + CKEY[b].start:b * KEYS + CKEY[b].stop], qn[:, 5 + b, :], ident[:])
                own = T[bk][:, 0:2 * KEYS].rearrange("p (r l) -> p r l", l=LEN)[:, ::5, :]
                mm = pe.transpose(own, qn[:, 4, :], ident[:])
                mm.then_inc(T_full[bk], 1)

            def scores(uses, s, par):
                (bq, nq), (bk, nk) = uses
                pe.wait_ge(T_dve[bq], nq + 1)
                pe.wait_ge(T_dve[bk], nk + 1)
                for b in range(2):
                    pe.wait_ge(exp_full[b], 2 * s)
                    for pair in range(2):
                        mm = product(pe, S[b][:, pair, :], lambda a: QT[par][:, a, b, pair * P:(pair + 1) * P],
                                     lambda a: KT[par][:, a, b, :], True, True)
                    mm.then_inc(S_full[b], 1)

            def slot(i, g, last=False):
                s, par, more = 4 * i + g, g % 2, not (last and g == 3)
                if more:
                    project([j_use(i, g, u) for u in range(3)], (g + 1) % NG, i + 1)
                for b in range(2):
                    bank, n = t_use(i, g, b)
                    pe.wait_ge(pr_full[b], s + 1)
                    pe.wait_ge(T_dve[bank], n)
                    at_own = (0, LEN)[b]
                    for part, col in ((0, CKEY[b].start), (1, at_own)):
                        for pair in range(2):
                            mm = pe.transpose(T[bank][:, part * 256 + pair * P:part * 256 + (pair + 1) * P],
                                              PR[b][:, pair, col:col + P], ident[:])
                    mm.then_inc(T_full[bank], 1)
                for b in range(2):
                    bank, n = t_use(i, g, b)
                    pe.wait_ge(T_dve[bank], n + 1)
                    if b == 0:
                        pe.wait_ge(ot_full, s + 1)
                    product(pe, PO[:, b, :], lambda a: VC[par][:, a, b, :], lambda a: PT[b][:, a, 0, :], True, False)
                    own = slice(b * LEN, (b + 1) * LEN)
                    if b == 1:
                        pe.wait_ge(pv_done[0], s + 2)
                    product(pe, PO[:, b, :], lambda a: VS[par][own, a, :], lambda a: PT[b][own, a, 1, :], False, True)\
                        .then_inc(pv_done[b], 1)
                if g == 2 and not last:
                    x_turn([j_x(i, c) for c in range(KD)], i + 1)
                if more:
                    uses = [t_use(i, g, u) for u in (2, 3)]
                    qk_turn(uses, s + 1)
                    scores(uses, s + 1, 1 - par)
                pe.wait_ge(ot_full, s + 2)
                if g == 0:
                    pe.wait_ge(acc_read, i + 1)
                for h in range(REP):
                    mm = product(pe, ACC[:, :], lambda a: OT[:, a, h, :], lambda a: WO[:, a, REP * g + h, :],
                                 g == 0 and h == 0, g == NG - 1 and h == REP - 1)
                mm.then_inc(wo_done, 1)

            for unused in (*pv_done, *S_full, wo_done):
                pe.sem_inc(unused, 1)
            pe.wait_ge(tab_in, 6 * 16)
            x_turn(J_FIRST[0:2], 0)
            pe.wait_ge(w_lo, len(pieces))
            project(J_FIRST[2:5], 0, 0)
            qk_turn(T_FIRST, 0)
            scores(T_FIRST, 0, 0)
            with pe.Fori(0, NT - 1) as i:
                for g in range(NG):
                    slot(i, g)
            for g in range(NG):
                slot(NT - 1, g, last=True)


DSTATE, DTRANK = 16, 128
CT4 = 4
NC = NT // CT4
CHUNK = CT4 * P


def tokens(X, c, first=0, n=CT4):
    return X[:, bass.ds(c * CT4 + first, n), :]


def tile_of(X, c, t):
    return tokens(X, c, t, 1).rearrange("p a n -> p (a n)")


def selective_scan(nc, X, d):
    with ExitStack() as ctx:
        k = Kit(nc, ctx, "ss")
        sb, sem, sems = k.sb, k.sem, k.sems
        ident, scrap, lneps, mhalf = sb("ident", [P, P]), sb("scrap", [P, 1]), sb("lneps", [P, CT4]), sb("mhalf", [P, CT4])
        w_raw = sb("w_raw", [P, KD, DTRANK + 2 * DSTATE])
        W = sb("W", [P, 2, KD, DTRANK + 2 * DSTATE], F32R)
        dt_raw, DTW = sb("dt_raw", [P, DIM]), sb("DTW", [P, 2, DIM], F32R)
        sel_raw = sb("sel_raw", [64, 2 * DSTATE, P])
        SEL = sb("SEL", [64, 2 * DSTATE, P], F32R)
        bias, alog, A, skip = sb("bias", [P, KD]), sb("alog", [P, KD, DSTATE]), sb("A", [P, KD, DSTATE]), sb("skip", [P, KD])
        stats, mv, rstd = sb("stats", [P, CT4, 6]), sb("mv", [P, CT4, 2]), sb("rstd", [P, CT4])
        xn = sb("xn", [P, CT4, DIM])
        XT, XF = sb("XT", [P, 2, KD, CHUNK], F32R), sb("XF", [P, KD, CHUNK])
        DL, BC = sb("DL", [P, 2, CHUNK], F32R), sb("BC", [64, CHUNK], F32R)
        az, rz, ez, lz = (sb(n, [P, KD, CHUNK]) for n in ("az", "rz", "ez", "lz"))
        dt, u, y = (sb(n, [P, KD, CHUNK]) for n in ("dt", "u", "y"))
        decay = [sb(f"decay{j}", [P, CHUNK // LEN, LEN]) for j in range(2)]
        bx, state = sb("bx", [P, CHUNK]), sb("state", [P, CHUNK])
        cy = [sb(f"cy{j}", [P, CHUNK]) for j in range(2)]
        M = [k.ps(f"M{j}", [P, CHUNK]) for j in range(2)]
        BB = [k.ps(f"BB{j}", [P, CHUNK]) for j in range(2)]
        CB = [k.ps(f"CB{j}", [P, CHUNK]) for j in range(2)]
        YT = [k.ps(f"YT{j}", [P, 2, DIM]) for j in range(2)]

        w_in, w_hi, w_full, decay_zero = sem("w_in"), sem("w_hi"), sem("w_full"), sem("decay_zero")
        stat_full, mv_full, var_full, rstd_full, xn_full = (sem(n) for n in ("stat_full", "mv_full", "var_full", "rstd_full", "xn_full"))
        M_full, M_act, M_dve = sems("M_full"), sems("M_act"), sems("M_dve")
        ez_full, lz_full, dt_full, du_full = (sem(n) for n in ("ez_full", "lz_full", "dt_full", "du_full"))
        decay_full, bb_full, cb_full = sem("decay_full"), sem("bb_full"), sem("cb_full")
        bx_full, state_full, cy_full, y_sum = sem("bx_full"), sem("state_full"), sem("cy_full"), sem("y_sum")
        yt_full, x_sum = sem("yt_full"), sem("x_sum")
        Q = KD * DSTATE

        def step(c, q):
            return c * Q + (q + 3)

        block = ctx.enter_context(nc.Block())

        @block.sync
        def _(sp):
            for dst, src in ((ident, d["ident"]), (w_raw, d["xproj"].rearrange("(k p) n -> p k n", p=P)), (dt_raw, d["dtproj"]),
                             (sel_raw, d["sel_bc"]), (bias, d["dtbias"]),
                             (alog, d["alog"].rearrange("(k p) n -> p k n", p=P)), (skip, d["skip"])):
                sp.dma_start(dst[:], src).then_inc(w_in, 16)

        @block.scalar
        def _(act):
            act.wait_ge(w_in, 7 * 16)
            act.activation(W[:, HI], w_raw[:], ACT.Copy)
            act.activation(DTW[:, HI], dt_raw[:], ACT.Copy)
            act.activation(SEL[:], sel_raw[:], ACT.Copy)
            act.activation(A[:], alog[:], ACT.Exp).then_inc(w_hi, 1)
            act.wait_ge(decay_zero, 1)

            def chunk(c):
                for j in range(KD):
                    act.wait_ge(M_full[j], 3 * c + 1)
                    act.activation(XT[:, HI, j, :], M[j][:, :], ACT.Copy)
                    act.activation(XF[:, j, :], M[j][:, :], ACT.Copy).then_inc(M_act[j], 1)
                act.wait_ge(M_full[0], 3 * c + 2)
                act.activation(DL[:, HI], M[0][:, :], ACT.Copy).then_inc(M_act[0], 1)
                act.wait_ge(M_full[1], 3 * c + 2)
                act.activation(BC[0:32, :], M[1][0:32, :], ACT.Copy).then_inc(M_act[1], 1)
                for j in range(KD):
                    act.wait_ge(M_full[j], 3 * c + 3)
                    act.activation(az[:, j, :], M[j][:, :], ACT.Abs, bias=bias[:, j:j + 1]).then_inc(M_act[j], 1)
                for j in range(KD):
                    act.wait_ge(M_act[j], 3 * c + 3)
                    act.activation(ez[:, j, :], az[:, j, :], ACT.Exp, scale=-1.0).then_inc(ez_full, 1)
                act.wait_ge(ez_full, 2 * c + 2)
                for j in range(KD):
                    act.activation(lz[:, j, :], ez[:, j, :], ACT.Ln, bias=1.0).then_inc(lz_full, 1)
                for q in range(Q):
                    half, n = divmod(q, DSTATE)
                    if n == 0:
                        act.wait_ge(du_full, 2 * c + half + 1)
                    act.wait_ge(state_full, step(c, q - 2))
                    act.activation(decay[q % 2][:, :, 1:], dt[:, half, :].rearrange("p (b l) -> p b l", l=LEN)[:, :, 1:],
                                   ACT.Exp, scale=A[:, half, n:n + 1]).then_inc(decay_full, 1)

            with act.Fori(0, NC) as c:
                chunk(c)

        @block.vector
        def _(dve):
            for used in (bx_full, state_full, cy_full):
                dve.sem_inc(used, 2)
            dve.memset(decay[0][:], 0.0)
            dve.memset(decay[1][:], 0.0).then_inc(decay_zero, 1)
            dve.wait_ge(w_hi, 1)
            dve.tensor_tensor(W[:, LO], w_raw[:], W[:, HI], ALU.subtract)
            dve.tensor_tensor(DTW[:, LO], dt_raw[:], DTW[:, HI], ALU.subtract)
            dve.tensor_scalar(A[:], A[:], -1.0, None, ALU.mult).then_inc(w_full, 1)

            def chunk(c):
                for t in range(CT4):
                    done = dve.bn_stats(stats[:, t, :], tile_of(X, c, t))
                done.then_inc(stat_full, 1)
                dve.wait_ge(stat_full, c + 1)
                dve.memset(scrap[:], 0.0)
                for t in range(CT4):
                    done = dve.bn_aggr(mv[:, t, :], stats[:, t, :])
                done.then_inc(mv_full, 1)
                dve.wait_ge(rstd_full, c + 1)
                dve.memset(scrap[:], 0.0)
                for t in range(CT4):
                    done = dve.tensor_scalar(xn[:, t, :], tile_of(X, c, t), mv[:, t, 0:1], rstd[:, t:t + 1], ALU.subtract, ALU.mult)
                done.then_inc(xn_full, 1)
                for j in range(KD):
                    dve.wait_ge(M_act[j], 3 * c + 1)
                    dve.tensor_tensor(XT[:, LO, j, :], M[j][:, :], XT[:, HI, j, :], ALU.subtract).then_inc(M_dve[j], 1)
                dve.wait_ge(M_act[0], 3 * c + 2)
                dve.tensor_tensor(DL[:, LO], M[0][:, :], DL[:, HI], ALU.subtract).then_inc(M_dve[0], 1)
                dve.wait_ge(M_act[1], 3 * c + 2)
                dve.tensor_tensor(BC[32:64, :], M[1][0:32, :], BC[0:32, :], ALU.subtract).then_inc(M_dve[1], 1)
                for j in range(KD):
                    dve.wait_ge(M_act[j], 3 * c + 3)
                    dve.tensor_scalar(rz[:, j, :], M[j][:, :], bias[:, j:j + 1], 0.0, ALU.add, ALU.max).then_inc(M_dve[j], 1)
                for j in range(KD):
                    dve.tensor_scalar(y[:, j, :], XF[:, j, :], skip[:, j:j + 1], None, ALU.mult)
                for j in range(KD):
                    dve.wait_ge(M_dve[j], 3 * c + 3)
                    dve.wait_ge(lz_full, 2 * c + j + 1)
                    dve.tensor_tensor(dt[:, j, :], rz[:, j, :], lz[:, j, :], ALU.add).then_inc(dt_full, 1)
                    dve.wait_ge(dt_full, 2 * c + j + 1)
                    dve.tensor_tensor(u[:, j, :], dt[:, j, :], XF[:, j, :], ALU.mult).then_inc(du_full, 1)
                for q in range(Q):
                    half, n = divmod(q, DSTATE)
                    if n == 0:
                        dve.wait_ge(du_full, 2 * c + half + 1)
                    dve.wait_ge(bb_full, c * Q + q + 1)
                    dve.wait_ge(state_full, step(c, q - 1))
                    dve.tensor_tensor(bx[:], BB[q % 2][:, :], u[:, half, :], ALU.mult).then_inc(bx_full, 1)
                    dve.wait_ge(decay_full, c * Q + q + 1)
                    dve.wait_ge(bx_full, step(c, q))
                    dve.wait_ge(cy_full, step(c, q - 1))
                    dve.tensor_tensor_scan(state[:], decay[q % 2][:].rearrange("p b l -> p (b l)"), bx[:], 0.0,
                                           ALU.mult, ALU.add).then_inc(state_full, 1)
                    dve.wait_ge(cb_full, c * Q + q + 1)
                    dve.wait_ge(state_full, step(c, q))
                    dve.wait_ge(y_sum, step(c, q - 2))
                    dve.tensor_tensor(cy[q % 2][:], CB[q % 2][:, :], state[:], ALU.mult).then_inc(cy_full, 1)
                dve.wait_ge(yt_full, c + 1)
                for t in range(0, CT4, 2):
                    done = dve.tensor_tensor(tokens(X, c, t, 2), YT[t // 2][:, :, :], tokens(X, c, t, 2), ALU.add)
                done.then_inc(x_sum, 1)

            dve.wait_ge(w_full, 1)
            with dve.Fori(0, NC) as c:
                chunk(c)

        @block.gpsimd
        def _(pool):
            pool.sem_inc(y_sum, 2)
            pool.memset(lneps[:], 1e-5)
            pool.memset(mhalf[:], -0.5).then_inc(var_full, 1)
            pool.wait_ge(var_full, 1)

            def chunk(c):
                pool.wait_ge(mv_full, c + 1)
                pool.tensor_tensor(rstd[:], mv[:, :, 1], lneps[:], ALU.add).then_inc(var_full, 1)
                pool.wait_ge(var_full, c + 2)
                pool.tensor_tensor(rstd[:], rstd[:], mhalf[:], ALU.pow).then_inc(rstd_full, 1)
                for q in range(Q):
                    half = q // DSTATE
                    pool.wait_ge(cy_full, step(c, q))
                    pool.wait_ge(y_sum, step(c, q - 1))
                    pool.tensor_tensor(y[:, half, :], y[:, half, :], cy[q % 2][:], ALU.add).then_inc(y_sum, 1)

            with pool.Fori(0, NC) as c:
                chunk(c)

        @block.tensor
        def _(pe):
            pe.wait_ge(w_full, 1)

            def spread(dst, c, q, row, free, full):
                pe.wait_ge(free, step(c, q - 2))
                pe.matmul(dst[:, :], SEL[:, row, :], BC[:, :], start=True, stop=True).then_inc(full, 1)

            def chunk(c):
                pe.wait_ge(xn_full, c + 1)
                for j in range(KD):
                    for t in range(CT4):
                        mm = pe.transpose(M[j][:, t * P:(t + 1) * P], xn[:, t, j * P:(j + 1) * P], ident[:])
                    mm.then_inc(M_full[j], 1)
                pe.wait_ge(M_dve[0], 3 * c + 1)
                pe.wait_ge(M_dve[1], 3 * c + 1)
                for m, rows in ((0, slice(0, DTRANK)), (1, slice(DTRANK, DTRANK + 2 * DSTATE))):
                    for j in range(KD):
                        mm = product(pe, M[m][0:rows.stop - rows.start, :], lambda a: W[:, a, j, rows], lambda a: XT[:, a, j, :],
                                     j == 0, j == KD - 1)
                    mm.then_inc(M_full[m], 1)
                pe.wait_ge(M_dve[0], 3 * c + 2)
                pe.wait_ge(M_dve[1], 3 * c + 2)
                for j in range(KD):
                    product(pe, M[j][:, :], lambda a: DTW[:, a, j * P:(j + 1) * P], lambda a: DL[:, a, :], True, True)\
                        .then_inc(M_full[j], 1)
                for q in range(Q):
                    n = q % DSTATE
                    spread(BB[q % 2], c, q, n, bx_full, bb_full)
                    spread(CB[q % 2], c, q, DSTATE + n, cy_full, cb_full)
                pe.wait_ge(y_sum, step(c, Q - 1))
                for t in range(CT4):
                    for j in range(KD):
                        mm = pe.transpose(YT[t // 2][:, t % 2, j * P:(j + 1) * P], y[:, j, t * P:(t + 1) * P], ident[:])
                mm.then_inc(yt_full, 1)

            with pe.Fori(0, NC) as c:
                chunk(c)


def self_attention(nc, X, x_kept, d):
    H = 16
    with ExitStack() as ctx:
        k = Kit(nc, ctx, "sa")
        sb, sem, sems = k.sb, k.sem, k.sems
        W = {n: sb(n, [P, 2, KD, H * HD], F32R) for n in ("WQ", "WK", "WV")}
        WO = sb("WO", [P, 2, H, DIM], F32R)
        ident, mask, ln1 = sb("ident", [P, P]), sb("mask", [P, P]), sb("ln1", [P, DIM])
        scrap, eps, mhalf, inv_dim = sb("scrap", [P, 1]), sb("eps", [P, 2, CT4]), sb("mhalf", [P, CT4]), sb("inv_dim", [P, CT4])
        stats, mv, rstd = sb("stats", [P, CT4, 6]), sb("mv", [P, CT4, 2]), sb("rstd", [P, CT4])
        sqs, msq, rr = sb("sqs", [P, DIM]), sb("msq", [P, CT4]), sb("rr", [P, CT4])
        xn = sb("xn", [P, CT4, DIM])
        HT = sb("HT", [P, 2, KD, CHUNK], F32R)
        QT, KT = ([sb(f"{n}{j}", [P, 2, CHUNK], F32R) for j in range(2)] for n in ("QT", "KT"))
        V = [sb(f"V{j}", [P, 2, CT4, 2 * HD], F32R) for j in range(2)]
        PRs = sb("PR", [P, 2, CT4, P])
        PR = [PRs[:, j] for j in range(2)]
        stage = [xn[:].rearrange("p a n -> p (a n)"), PRs[:].rearrange("p j a n -> p (j a n)")]
        nmax, rsum, rinv = sb("nmax", [P, CT4]), sb("rsum", [P, CT4]), sb("rinv", [P, CT4])
        PT, OT = sb("PT", [P, 2, CHUNK], F32R), sb("OT", [P, 2, CHUNK], F32R)
        out_t = xn[:].rearrange("p (k a) n -> p k (a n)", k=KD)
        J = [k.ps(f"J{j}", [P, CHUNK]) for j in range(2)]
        S = [k.ps(f"S{j}", [P, CT4, P]) for j in range(2)]
        T, PO = k.ps("T", [P, CHUNK]), k.ps("PO", [P, CHUNK])
        ACC = [k.ps(f"ACC{j}", [P, CHUNK]) for j in range(KD)]

        x_saved, tab_in, staged, w_hi, w_lo = sem("x_saved"), sem("tab_in"), sems("staged"), sem("w_hi"), sem("w_lo")
        stat_full, mv_full, var_full, rstd_full, h_full, msq_full, rr_full, xn_full = (
            sem(n) for n in ("stat_full", "mv_full", "var_full", "rstd_full", "h_full", "msq_full", "rr_full", "xn_full"))
        J_full, J_act, J_dve = sems("J_full"), sems("J_act"), sems("J_dve")
        T_full, T_act, T_dve = sem("T_full"), sem("T_act"), sem("T_dve")
        S_full, S_mask, nmax_full, exp_full, rinv_full, pr_full = (
            sem(n) for n in ("S_full", "S_mask", "nmax_full", "exp_full", "rinv_full", "pr_full"))
        pv_done, ot_hi, ot_full, wo_done = sem("pv_done"), sem("ot_hi"), sem("ot_full"), sem("wo_done")
        out_hi, x_sum = sem("out_hi"), sem("x_sum")

        pieces = []
        for n, w in (("WQ", "ffn_wq"), ("WK", "ffn_wk"), ("WV", "ffn_wv")):
            v = d[w].rearrange("(k p) n -> p k n", p=P)
            pieces += [(v[:, c, u * 1024:(u + 1) * 1024], lambda a, n=n, c=c, u=u: W[n][:, a, c, u * 1024:(u + 1) * 1024])
                       for c in range(KD) for u in range(2)]
        v = d["ffn_wo"].rearrange("(h p) n -> p h n", p=P)
        pieces += [(v[:, u * 4:(u + 1) * 4, :], lambda a, u=u: WO[:, a, u * 4:(u + 1) * 4, :]) for u in range(4)]

        def staging(j):
            view = stage[j % 2]
            return view.rearrange("p (a n) -> p a n", n=DIM) if len(pieces[j][0].shape) == 3 else view

        PER = 3 * H + KD

        def j_use(c, n):
            return n % 2, c * (PER // 2) + n // 2

        def slot_uses(c, h):
            n = 8 + 3 * h + (2 if h >= 14 else 0)
            return [j_use(c, n + u) for u in range(3)]

        def x_uses(c):
            return [j_use(c, 8 + 3 * 14 + u) for u in range(KD)]

        def qk_uses(c, h):
            return slot_uses(c, h)[0:2]

        def v_use(c, h):
            return slot_uses(c, h)[2], (h // 2 + 1) % (H // 2), 2 * (h % 2)

        def done(s):
            return s + 2

        STEP_SIGNALS = {"pe": (S_full, pv_done, wo_done), "dve": (S_mask, nmax_full, rinv_full, ot_full),
                        "act": (exp_full, ot_hi), "pool": (pr_full,)}

        def start(engine, name):
            for signal in STEP_SIGNALS[name]:
                engine.sem_inc(signal, 1)

        block = ctx.enter_context(nc.Block())

        @block.sync
        def _(sp):
            sp.dma_start(x_kept.rearrange("(t p) n -> p t n", p=P), X[:, :, :]).then_inc(x_saved, 16)
            for dst, src in ((ident, d["ident"]), (mask, d["smask"]), (ln1, d["ln1"].partition_broadcast(P))):
                sp.dma_start(dst[:], src).then_inc(tab_in, 16)
            for j, (src, _) in enumerate(pieces):
                if j >= 2:
                    sp.wait_ge(w_lo, j - 1)
                sp.dma_start(staging(j), src).then_inc(staged[j % 2], 16)

        @block.scalar
        def _(act):
            start(act, "act")

            def squares(c):
                act.wait_ge(h_full, c + 1)
                for t in range(CT4):
                    x = X[:, t, :] if isinstance(c, int) else tile_of(X, c, t)
                    act.activation(sqs[:], x, ACT.Square, accum_out=msq[:, t:t + 1]).then_inc(msq_full, 1)
                    if t < CT4 - 1:
                        act.wait_ge(msq_full, 4 * c + (t + 1))

            def x_split(uses):
                for j, (bank, n) in enumerate(uses):
                    act.wait_ge(J_full[bank], n + 1)
                    act.activation(HT[:, HI, j, :], J[bank][:, :], ACT.Copy).then_inc(J_act[bank], 1)

            def qk_split(use, u, par):
                bank, n = use
                act.wait_ge(J_full[bank], n + 1)
                act.activation((QT, KT)[u][par][:, HI], J[bank][:, :], ACT.Copy, scale=(HD ** -0.5, 1.0)[u]).then_inc(J_act[bank], 1)

            def v_split(v_use):
                (bank, n), pair, t = v_use
                act.wait_ge(J_full[bank], n + 1)
                act.activation(V[pair % 2][:, HI, t:t + 2, :], J[bank][:, :].rearrange("p (a n) -> p a n", a=2),
                               ACT.Copy).then_inc(J_act[bank], 1)

            def exps(s, par):
                act.wait_ge(nmax_full, done(s))
                for t in range(CT4):
                    last = act.activation(PR[par][:, t, :], S[par][:, t, :], ACT.Exp, bias=nmax[:, t:t + 1], accum_out=rsum[:, t:t + 1])
                last.then_inc(exp_full, 1)

            def slot(c, h, last):
                s, more = c * H + h, not (last and h >= 14)
                if h == 14 and more:
                    x_split(x_uses(c))
                if more:
                    act.wait_ge(S_full, done(s))
                    qk_split(qk_uses(c, h)[0], 0, h % 2)
                if not (last and h == 15):
                    act.wait_ge(pv_done, done(s - 1))
                    exps(s + 1, (h + 1) % 2)
                if more:
                    qk_split(qk_uses(c, h)[1], 1, h % 2)
                    v_split(v_use(c, h))
                act.wait_ge(T_full, c * (H + 1) + (h + 1))
                act.activation(PT[:, HI], T[:, :], ACT.Copy).then_inc(T_act, 1)
                if h == 11 and not last:
                    squares(c + 1)
                act.wait_ge(pv_done, done(s))
                act.wait_ge(wo_done, done(s - 1))
                act.activation(OT[:, HI], PO[:, :], ACT.Copy).then_inc(ot_hi, 1)

            def chunk(c, last=False):
                for h in range(H):
                    slot(c, h, last)
                act.wait_ge(wo_done, done(c * H + (H - 1)))
                for j in range(KD):
                    act.activation(out_t[:, j, :], ACC[j][:, :], ACT.Copy).then_inc(out_hi, 1)

            squares(0)
            for j, (_, dst) in enumerate(pieces):
                act.wait_ge(staged[j % 2], 16 * (j // 2 + 1))
                act.activation(dst(HI), staging(j), ACT.Copy).then_inc(w_hi, 1)
            x_split(x_uses(-1))
            for h in (14, 15):
                for u in range(2):
                    qk_split(qk_uses(-1, h)[u], u, h % 2)
                v_split(v_use(-1, h))
            exps(0, 0)
            with act.Fori(0, NC - 1) as c:
                chunk(c)
            chunk(NC - 1, last=True)

        @block.vector
        def _(dve):
            start(dve, "dve")

            def tile(buf, c, t):
                return buf[:, c * CT4 + t, :] if isinstance(c, int) else tile_of(buf, c, t)

            def norm_stats(c):
                for t in range(CT4):
                    last = dve.bn_stats(stats[:, t, :], tile(X, c, t))
                last.then_inc(stat_full, 1)

            def norm_var(c):
                dve.wait_ge(stat_full, c + 1)
                dve.memset(scrap[:], 0.0)
                for t in range(CT4):
                    last = dve.bn_aggr(mv[:, t, :], stats[:, t, :])
                last.then_inc(mv_full, 1)

            def norm_apply(c):
                dve.wait_ge(rstd_full, c + 1)
                dve.memset(scrap[:], 0.0)
                for t in range(CT4):
                    last = dve.tensor_scalar(tile(X, c, t), tile(X, c, t), mv[:, t, 0:1], rstd[:, t:t + 1], ALU.subtract, ALU.mult)
                last.then_inc(h_full, 1)

            def rms_apply(c):
                dve.wait_ge(rr_full, c + 1)
                dve.memset(scrap[:], 0.0)
                for t in range(CT4):
                    last = dve.scalar_tensor_tensor(xn[:, t, :], tile(X, c, t), rr[:, t:t + 1], ln1[:], ALU.mult, ALU.mult)
                last.then_inc(xn_full, 1)

            def x_split(uses):
                for j, (bank, n) in enumerate(uses):
                    dve.wait_ge(J_act[bank], n + 1)
                    dve.tensor_tensor(HT[:, LO, j, :], J[bank][:, :], HT[:, HI, j, :], ALU.subtract).then_inc(J_dve[bank], 1)

            def qk_split(uses, par):
                for u, (bank, n) in enumerate(uses):
                    buf = (QT, KT)[u][par]
                    dve.wait_ge(J_act[bank], n + 1)
                    dve.scalar_tensor_tensor(buf[:, LO], J[bank][:, :], (HD ** -0.5, 1.0)[u], buf[:, HI],
                                             ALU.mult, ALU.subtract).then_inc(J_dve[bank], 1)

            def v_split(v_use):
                (bank, n), pair, t = v_use
                dve.wait_ge(J_act[bank], n + 1)
                dve.tensor_tensor(V[pair % 2][:, LO, t:t + 2, :], J[bank][:, :].rearrange("p (a n) -> p a n", a=2),
                                  V[pair % 2][:, HI, t:t + 2, :], ALU.subtract).then_inc(J_dve[bank], 1)

            def maxima(s, par):
                dve.wait_ge(S_full, done(s))
                dve.tensor_tensor(S[par][:, :, :], S[par][:, :, :], mask[:, None, :].broadcast_to([P, CT4, P]),
                                  ALU.add).then_inc(S_mask, 1)
                dve.wait_ge(S_mask, done(s))
                dve.tensor_reduce(nmax[:], S[par][:, :, :], AX.X, ALU.max, negate=True).then_inc(nmax_full, 1)

            def inverse(s):
                dve.wait_ge(exp_full, done(s))
                dve.wait_ge(pr_full, done(s - 1))
                dve.reciprocal(rinv[:], rsum[:]).then_inc(rinv_full, 1)

            def slot(c, h, last):
                s, more = c * H + h, not (last and h >= 14)
                if not (last and h == 15):
                    maxima(s + 1, (h + 1) % 2)
                if h == 14 and more:
                    x_split(x_uses(c))
                if more:
                    qk_split(qk_uses(c, h), h % 2)
                    v_split(v_use(c, h))
                if not (last and h == 15):
                    inverse(s + 1)
                dve.wait_ge(T_act, s + 1)
                dve.tensor_tensor(PT[:, LO], T[:, :], PT[:, HI], ALU.subtract).then_inc(T_dve, 1)
                if not last:
                    for at, stage_of in ((8, norm_stats), (9, norm_var), (10, norm_apply), (12, rms_apply)):
                        if h == at:
                            stage_of(c + 1)
                dve.wait_ge(ot_hi, done(s))
                dve.tensor_tensor(OT[:, LO], PO[:, :], OT[:, HI], ALU.subtract).then_inc(ot_full, 1)

            def chunk(c, last=False):
                for h in range(H):
                    slot(c, h, last)
                dve.wait_ge(T_full, (c + 1) * (H + 1))
                for u, bank in ((0, T), (1, PO)):
                    x = X[:, c * CT4 + 2 * u:c * CT4 + 2 * u + 2, :] if last else tokens(X, c, 2 * u, 2)
                    dve.tensor_tensor(x, bank[:, :].rearrange("p (a n) -> p a n", a=2), x, ALU.add).then_inc(x_sum, 1)

            norm_stats(0)
            norm_var(0)
            dve.wait_ge(x_saved, 16)
            norm_apply(0)
            for j, (_, dst) in enumerate(pieces):
                dve.wait_ge(w_hi, j + 1)
                dve.tensor_tensor(dst(LO), staging(j), dst(HI), ALU.subtract).then_inc(w_lo, 1)
            dve.wait_ge(tab_in, 3 * 16)
            dve.wait_ge(w_lo, len(pieces))
            rms_apply(0)
            x_split(x_uses(-1))
            for h in (14, 15):
                qk_split(qk_uses(-1, h), h % 2)
                v_split(v_use(-1, h))
            maxima(0, 0)
            dve.wait_ge(exp_full, done(0))
            dve.reciprocal(rinv[:], rsum[:]).then_inc(rinv_full, 1)
            with dve.Fori(0, NC - 1) as c:
                chunk(c)
            chunk(NC - 1, last=True)

        @block.gpsimd
        def _(pool):
            start(pool, "pool")
            pool.memset(inv_dim[:], 1.0 / DIM)
            pool.memset(eps[:, 0, :], 1e-5)
            pool.memset(eps[:, 1, :], 1e-6)
            pool.memset(mhalf[:], -0.5).then_inc(var_full, 1)
            pool.wait_ge(var_full, 1)

            def ln_rstd(c):
                pool.wait_ge(mv_full, c + 1)
                pool.tensor_tensor(rstd[:], mv[:, :, 1], eps[:, 0, :], ALU.add).then_inc(var_full, 1)
                pool.wait_ge(var_full, 3 * c + 2)
                pool.tensor_tensor(rstd[:], rstd[:], mhalf[:], ALU.pow).then_inc(rstd_full, 1)

            def rms_rstd(c):
                pool.wait_ge(msq_full, 4 * c + 4)
                pool.tensor_tensor(rr[:], msq[:], inv_dim[:], ALU.mult).then_inc(var_full, 1)
                pool.wait_ge(var_full, 3 * c + 3)
                pool.tensor_tensor(rr[:], rr[:], eps[:, 1, :], ALU.add).then_inc(var_full, 1)
                pool.wait_ge(var_full, 3 * c + 4)
                pool.tensor_tensor(rr[:], rr[:], mhalf[:], ALU.pow).then_inc(rr_full, 1)

            def normalise(s, par):
                pool.wait_ge(rinv_full, done(s))
                pool.tensor_tensor(PR[par][:], PR[par][:], rinv[:, :, None].broadcast_to([P, CT4, P]), ALU.mult).then_inc(pr_full, 1)

            def chunk(c, last=False):
                for h in range(H):
                    if not (last and h == 15):
                        normalise(c * H + (h + 1), (h + 1) % 2)
                    if h == 9 and not last:
                        ln_rstd(c + 1)
                    if h == 11 and not last:
                        rms_rstd(c + 1)

            ln_rstd(0)
            rms_rstd(0)
            normalise(0, 0)
            with pool.Fori(0, NC - 1) as c:
                chunk(c)
            chunk(NC - 1, last=True)

        @block.tensor
        def _(pe):
            start(pe, "pe")

            def x_turn(uses, c):
                pe.wait_ge(xn_full, c + 1)
                for j, (bank, n) in enumerate(uses):
                    pe.wait_ge(J_dve[bank], n)
                    for t in range(CT4):
                        mm = pe.transpose(J[bank][:, t * P:(t + 1) * P], xn[:, t, j * P:(j + 1) * P], ident[:])
                    mm.then_inc(J_full[bank], 1)

            def qk_project(uses, h):
                for u, (bank, n) in enumerate(uses):
                    pe.wait_ge(J_dve[bank], n)
                    w = W[("WQ", "WK")[u]]
                    for j in range(KD):
                        mm = product(pe, J[bank][:, :], lambda a: w[:, a, j, h * HD:(h + 1) * HD], lambda a: HT[:, a, j, :],
                                     j == 0, j == KD - 1)
                    mm.then_inc(J_full[bank], 1)

            def v_project(v_use):
                (bank, n), pair, t = v_use
                pe.wait_ge(J_dve[bank], n)
                for u in range(2):
                    at = slice((t + u) * P, (t + u + 1) * P)
                    for j in range(KD):
                        mm = product(pe, J[bank][:, u * 2 * HD:(u + 1) * 2 * HD], lambda a: HT[:, a, j, at],
                                     lambda a: W["WV"][:, a, j, pair * 2 * HD:(pair + 1) * 2 * HD], j == 0, j == KD - 1)
                mm.then_inc(J_full[bank], 1)

            def scores(uses, s, par):
                for bank, n in uses:
                    pe.wait_ge(J_dve[bank], n + 1)
                for t in range(CT4):
                    mm = product(pe, S[par][:, t, :], lambda a: QT[par][:, a, t * P:(t + 1) * P],
                                 lambda a: KT[par][:, a, t * P:(t + 1) * P], True, True)
                mm.then_inc(S_full, 1)

            def begin_chunk(c, h):
                if h == 14:
                    x_turn(x_uses(c), c + 1)
                    for bank, n in x_uses(c):
                        pe.wait_ge(J_dve[bank], n + 1)
                qk_project(qk_uses(c, h), h - 14)
                v_project(v_use(c, h))

            def slot(c, h, last):
                s, par = c * H + h, h % 2
                if not (last and h == 15):
                    scores(qk_uses(c, h - 1) if h else qk_uses(c - 1, 15), s + 1, 1 - par)
                if h >= 14:
                    if not last:
                        begin_chunk(c, h)
                else:
                    qk_project(qk_uses(c, h), h + 2)
                    v_project(v_use(c, h))
                pe.wait_ge(pr_full, done(s))
                for t in range(CT4):
                    mm = pe.transpose(T[:, t * P:(t + 1) * P], PR[par][:, t, :], ident[:])
                mm.then_inc(T_full, 1)
                pe.wait_ge(T_dve, s + 1)
                pe.wait_ge(ot_full, done(s - 1))
                for t in range(CT4):
                    mm = product(pe, PO[:, t * P:(t + 1) * P], lambda a: V[h // 2 % 2][:, a, t, h % 2 * HD:(h % 2 + 1) * HD],
                                 lambda a: PT[:, a, t * P:(t + 1) * P], True, True)
                mm.then_inc(pv_done, 1)
                pe.wait_ge(ot_full, done(s))
                for j in range(KD):
                    mm = product(pe, ACC[j][:, :], lambda a: WO[:, a, h, j * P:(j + 1) * P], lambda a: OT[:, a, :], h == 0, h == H - 1)
                mm.then_inc(wo_done, 1)

            def chunk(c, last=False):
                for h in range(H):
                    slot(c, h, last)
                pe.wait_ge(out_hi, 2 * c + 2)
                for t in range(CT4):
                    for j in range(KD):
                        mm = pe.transpose((T, PO)[t // 2][:, (t % 2) * DIM + j * P:(t % 2) * DIM + (j + 1) * P],
                                          out_t[:, j, t * P:(t + 1) * P], ident[:])
                mm.then_inc(T_full, 1)
                pe.wait_ge(x_sum, 2 * c + 2)

            pe.wait_ge(tab_in, 3 * 16)
            x_turn(x_uses(-1), 0)
            pe.wait_ge(w_lo, len(pieces))
            for bank, n in x_uses(-1):
                pe.wait_ge(J_dve[bank], n + 1)
            for h in (14, 15):
                qk_project(qk_uses(-1, h), h - 14)
                v_project(v_use(-1, h))
            scores(qk_uses(-1, 14), 0, 0)
            with pe.Fori(0, NC - 1) as c:
                chunk(c)
            chunk(NC - 1, last=True)


EXPERTS, TOPK, INNER, SHARED = 16, 6, 176, 352
ROWS = EXPERTS * INNER
NE = (ROWS + SHARED + P - 1) // P


def mixture_of_experts(nc, x_kept, x2_kept, d, out):
    with ExitStack() as ctx:
        k = Kit(nc, ctx, "me")
        sb, sem, sems = k.sb, k.sem, k.sems
        WG, WU = (sb(n, [P, 2, KD, NE * P], F32R) for n in ("WG", "WU"))
        WD = sb("WD", [P, 2, NE, DIM], F32R)
        gate_raw, WR = sb("gate_raw", [P, KD, EXPERTS]), sb("WR", [P, 2, KD, EXPERTS], F32R)
        SEL = sb("SEL", [64, NE, P], F32R)
        ident, ln2, tri = sb("ident", [P, P]), sb("ln2", [P, DIM]), sb("tri", [P, EXPERTS * EXPERTS])
        eps, mhalf, inv_dim = (sb(n, [P, CT4]) for n in ("eps", "mhalf", "inv_dim"))
        x2, xk, xs, xn = (sb(n, [P, CT4, DIM]) for n in ("x2", "xk", "xs", "xn"))
        msq, rr = sb("msq", [P, CT4]), sb("rr", [P, CT4])
        HT = sb("HT", [P, 2, KD, CHUNK], F32R)
        top, total, inv = sb("top", [P, CT4]), sb("total", [P, CT4]), sb("inv", [P, CT4])
        prob, pick, rank, ties = (sb(n, [P, CT4, EXPERTS]) for n in ("prob", "pick", "rank", "ties"))
        cw = sb("cw", [P, CT4, 32])
        CWS = sb("CWS", [64, CHUNK], F32R)
        sg, hu, hw = (sb(n, [P, CHUNK]) for n in ("sg", "hu", "hw"))
        HH = [sb(f"HH{j}", [P, 2, CHUNK], F32R) for j in range(2)]
        stage = [b[:].rearrange("p a n -> p (a n)") for b in (xn, xs)]
        beats = xn[:].rearrange("p a (e f) -> p a e f", f=EXPERTS)
        out_t = xn[:].rearrange("p (k a) n -> p k (a n)", k=KD)
        G, U, C = ([k.ps(f"{n}{j}", [P, CHUNK]) for j in range(2)] for n in "GUC")
        ACC = [k.ps(f"ACC{j}", [P, CHUNK]) for j in range(KD)]

        tab_in, sel_in, staged, w_hi, w_lo = sem("tab_in"), sem("sel_in"), sems("staged"), sem("w_hi"), sem("w_lo")
        x2_in, xk_in, xs_full, res_full, stored = (sem(n) for n in ("x2_in", "xk_in", "xs_full", "res_full", "stored"))
        var_full, msq_full, rr_full, xn_full = (sem(n) for n in ("var_full", "msq_full", "rr_full", "xn_full"))
        full = {r: sems(f"{r}_full") for r in "GUC"}
        x_hi, x_lo = sem("x_hi"), sem("x_lo")
        sg_full, hu_full, hw_full, hh_hi, hh_full, down_done = (
            sem(n) for n in ("sg_full", "hu_full", "hw_full", "hh_hi", "hh_full", "down_done"))
        top_full, prob_full, router, cws_hi, cws_full = (
            sem(n) for n in ("top_full", "prob_full", "router", "cws_hi", "cws_full"))
        out_hi, back_full, cw_set = sem("out_hi"), sem("back_full"), sem("cw_set")
        LINKS = 12

        pieces = []
        for n, W, first in (("wg", WG, 0), ("wu", WU, 0)):
            v = d[n].rearrange("(k p) n -> p k n", p=P)
            pieces += [(v[:, c, u * 800:(u + 1) * 800], lambda a, W=W, c=c, u=u: W[:, a, c, u * 800:(u + 1) * 800])
                       for c in range(KD) for u in range(4)]
        v = d["wd"].rearrange("(e p) n -> p e n", p=P)
        pieces += [(v[:, u:min(u + 4, NE), :], lambda a, u=u: WD[:, a, u:min(u + 4, NE), :]) for u in range(0, NE, 4)]

        def staging(j):
            src = pieces[j][0]
            n = int(np.prod(src.shape[1:]))
            view = stage[j % 2][:, 0:n]
            return view.rearrange("p (a n) -> p a n", n=DIM) if len(src.shape) == 3 else view

        plan = {r: [] for r in "GUC"}
        for e in [23, 24] + list(range(23)):
            if e == 23:
                plan["G"] += ["x", "logits"]
                plan["U"] += ["x"]
            for r in "GUC":
                plan[r] += [(e + 2) % NE]
            if e == 23:
                plan["G"] += ["cw"]
        where = {}
        for r, names in plan.items():
            for n, name in enumerate(names):
                where[r, name] = (n % 2, sum(1 for m in range(n) if m % 2 == n % 2))
        uses_of = {r: [len(plan[r][b::2]) for b in range(2)] for r in "GUC"}

        def use(r, name, c):
            bank, n = where[r, name]
            return bank, c * uses_of[r][bank] + n

        def done(s):
            return s + 2

        def freed(r, name, c):
            if name == "x":
                return x_lo, 2 * c + {"G": 1, "U": 2}[r]
            if name in ("logits", "cw"):
                return {"logits": prob_full, "cw": cws_full}[name], c + 1
            return {"G": sg_full, "U": hu_full, "C": hw_full}[r], done(c * NE + name)

        def free(pe, r, name, c):
            at = plan[r].index(name)
            if at >= 2:
                pe.wait_ge(*freed(r, plan[r][at - 2], c))
            elif not (isinstance(c, int) and c == 0):
                bank = at % 2
                pe.wait_ge(*freed(r, plan[r][bank::2][-1], c - 1))
            return where[r, name][0]

        def after(c, e):
            return (c + 1, e - NE) if e >= NE else (c, e)

        block = ctx.enter_context(nc.Block())

        @block.sync
        def _(sp):
            kept = [b.rearrange("(c t p) n -> p c t n", p=P, t=CT4) for b in (x2_kept, x_kept, out)]

            def rows(b, c):
                return kept[b][:, bass.ds(c, 1), :, :].rearrange("p c t n -> p (c t) n")

            sp.dma_start(x2[:], rows(0, 0)).then_inc(x2_in, 16)
            sp.dma_start(xk[:], rows(1, 0)).then_inc(xk_in, 16)
            for dst, src in ((ident, d["ident"]), (ln2, d["ln2"].partition_broadcast(P)), (tri, d["tri"].partition_broadcast(P)),
                             (gate_raw, d["wr"].rearrange("(k p) n -> p k n", p=P))):
                sp.dma_start(dst[:], src).then_inc(tab_in, 16)
            for j, (src, _) in enumerate(pieces):
                if j >= 2:
                    sp.wait_ge(w_lo, j - 1)
                sp.dma_start(staging(j), src).then_inc(staged[j % 2], 16)
            with sp.Fori(0, NC - 1) as c:
                sp.wait_ge(xs_full, c + 1)
                sp.dma_start(x2[:], rows(0, c + 1)).then_inc(x2_in, 16)
                sp.dma_start(xk[:], rows(1, c + 1)).then_inc(xk_in, 16)
                sp.wait_ge(res_full, 2 * c + 4)
                sp.dma_start(rows(2, c), xs[:]).then_inc(stored, 16)
            sp.wait_ge(res_full, 2 * NC + 2)
            sp.dma_start(rows(2, NC - 1), xs[:]).then_inc(stored, 16)
            sp.wait_ge(stored, 16 * NC + 16)

        @block.scalar
        def _(act):
            act.sem_inc(sg_full, 1)
            act.sem_inc(hh_hi, 1)

            def squares(c, squared):
                act.wait_ge(x2_in, 16 * c + 16)
                for t in range(CT4):
                    act.activation(squared, x2[:, t, :], ACT.Square, accum_out=msq[:, t:t + 1]).then_inc(msq_full, 1)
                    act.wait_ge(msq_full, 4 * c + (t + 1))

            def x_split(c):
                for j, (r, B) in enumerate((("G", G), ("U", U))):
                    bank, n = use(r, "x", c)
                    act.wait_ge(full[r][bank], n + 1)
                    act.activation(HT[:, HI, j, :], B[bank][:, :], ACT.Copy).then_inc(x_hi, 1)

            def route(c):
                bank, n = use("G", "logits", c)
                act.wait_ge(top_full, c + 1)
                for t in range(CT4):
                    last = act.activation(prob[:, t, :], G[bank][:, t * EXPERTS:(t + 1) * EXPERTS], ACT.Exp, bias=top[:, t:t + 1],
                                          accum_out=total[:, t:t + 1])
                last.then_inc(prob_full, 1)

            def cw_split(c):
                bank, n = use("G", "cw", c)
                act.wait_ge(full["G"][bank], n + 1)
                act.activation(CWS[0:32, :], G[bank][0:32, :], ACT.Copy).then_inc(cws_hi, 1)

            def gate(c, e):
                bank, n = use("G", e, c)
                act.wait_ge(full["G"][bank], n + 1)
                act.wait_ge(hu_full, done(c * NE + (e - 1)))
                act.activation(sg[:], G[bank][:, :], ACT.Silu).then_inc(sg_full, 1)

            def high(c, e):
                act.wait_ge(down_done, done(c * NE + (e - 1 if e == 0 else e - 2)))
                act.wait_ge(hw_full, done(c * NE + e))
                act.activation(HH[e % 2][:, HI], hw[:], ACT.Copy).then_inc(hh_hi, 1)

            def chunk(c, last=False):
                for e in range(NE):
                    if not (last and e == NE - 1):
                        gate(*after(c, e + 1))
                        high(*after(c, e + 1))
                    if e == 23 and not last:
                        x_split(c + 1)
                        route(c + 1)
                        cw_split(c + 1)
                    if e == 10 and not last:
                        act.wait_ge(back_full, c + 1)
                        squares(c + 1, xn[:, 0, :])
                act.wait_ge(down_done, done(c * NE + (NE - 1)))
                for j in range(KD):
                    act.activation(out_t[:, j, :], ACC[j][:, :], ACT.Copy).then_inc(out_hi, 1)

            squares(0, hu[:, 0:DIM])
            for j, (_, dst) in enumerate(pieces):
                act.wait_ge(staged[j % 2], 16 * (j // 2 + 1))
                act.activation(dst(HI), staging(j), ACT.Copy).then_inc(w_hi, 1)
            act.wait_ge(tab_in, 4 * 16)
            act.activation(WR[:, HI], gate_raw[:], ACT.Copy).then_inc(w_hi, 1)
            x_split(0)
            route(0)
            cw_split(0)
            gate(0, 0)
            high(0, 0)
            with act.Fori(0, NC - 1) as c:
                chunk(c)
            chunk(NC - 1, last=True)

        @block.vector
        def _(dve):
            dve.sem_inc(hu_full, 1)
            dve.sem_inc(hw_full, 1)
            dve.sem_inc(res_full, 2)

            def rms_apply(c):
                dve.wait_ge(rr_full, c + 1)
                for t in range(CT4):
                    last = dve.scalar_tensor_tensor(xn[:, t, :], x2[:, t, :], rr[:, t:t + 1], ln2[:], ALU.mult, ALU.mult)
                last.then_inc(xn_full, 1)

            def x_split(c):
                for j, (r, B) in enumerate((("G", G), ("U", U))):
                    dve.wait_ge(x_hi, 2 * c + (j + 1))
                    dve.tensor_tensor(HT[:, LO, j, :], B[where[r, "x"][0]][:, :], HT[:, HI, j, :], ALU.subtract).then_inc(x_lo, 1)

            def top_logit(c):
                bank, n = use("G", "logits", c)
                dve.wait_ge(full["G"][bank], n + 1)
                dve.tensor_reduce(top[:], G[bank][:, 0:CT4 * EXPERTS].rearrange("p (t e) -> p t e", t=CT4), AX.X, ALU.max,
                                  negate=True).then_inc(top_full, 1)

            def route(c):
                link = iter(range(1, LINKS + 1))

                def chain(ins):
                    ins.then_inc(router, 1)
                    dve.wait_ge(router, LINKS * c + next(link))

                four = [P, CT4, EXPERTS, EXPERTS]
                other, own = prob[:, :, None, :].broadcast_to(four), prob[:, :, :, None].broadcast_to(four)
                dve.wait_ge(prob_full, c + 1)
                chain(dve.reciprocal(inv[:], total[:]))
                chain(dve.tensor_tensor(prob[:], prob[:], inv[:, :, None].broadcast_to(four[:3]), ALU.mult))
                chain(dve.tensor_tensor(beats, other, own, ALU.is_gt))
                chain(dve.tensor_reduce(rank[:], beats, AX.X, ALU.add))
                chain(dve.tensor_tensor(beats, other, own, ALU.is_equal))
                chain(dve.tensor_tensor(beats, beats, tri[:, None, :].broadcast_to([P, CT4, EXPERTS * EXPERTS])
                                        .rearrange("p t (e f) -> p t e f", f=EXPERTS), ALU.mult))
                chain(dve.tensor_reduce(ties[:], beats, AX.X, ALU.add))
                chain(dve.tensor_tensor(rank[:], rank[:], ties[:], ALU.add))
                chain(dve.scalar_tensor_tensor(pick[:], rank[:], float(TOPK), prob[:], ALU.is_lt, ALU.mult))
                chain(dve.tensor_reduce(total[:], pick[:], AX.X, ALU.add))
                chain(dve.reciprocal(inv[:], total[:]))
                chain(dve.tensor_tensor(cw[:, :, 0:EXPERTS], pick[:], inv[:, :, None].broadcast_to(four[:3]), ALU.mult))

            def cw_split(c):
                dve.wait_ge(cws_hi, c + 1)
                dve.tensor_tensor(CWS[32:64, :], G[where["G", "cw"][0]][0:32, :], CWS[0:32, :], ALU.subtract).then_inc(cws_full, 1)

            def scale(c, e):
                s = c * NE + e
                (bu, nu), (bc, n_c) = use("U", e, c), use("C", e, c)
                dve.wait_ge(full["U"][bu], nu + 1)
                dve.wait_ge(hw_full, done(c * NE + (e - 1)))
                dve.wait_ge(sg_full, done(s))
                dve.tensor_tensor(hu[:], U[bu][:, :], sg[:], ALU.mult).then_inc(hu_full, 1)
                dve.wait_ge(full["C"][bc], n_c + 1)
                dve.wait_ge(hh_full, done(c * NE + (e - 1)))
                dve.wait_ge(hu_full, done(s))
                dve.tensor_tensor(hw[:], C[bc][:, :], hu[:], ALU.mult).then_inc(hw_full, 1)

            def chunk(c, last=False):
                for e in range(NE):
                    if not (last and e == NE - 1):
                        scale(*after(c, e + 1))
                    if e == 23 and not last:
                        x_split(c + 1)
                        top_logit(c + 1)
                        route(c + 1)
                        cw_split(c + 1)
                    if e == 13 and not last:
                        rms_apply(c + 1)
                dve.wait_ge(back_full, c + 2)
                dve.wait_ge(xs_full, c + 1)
                for u in range(2):
                    rows = xs[:, 2 * u:2 * u + 2, :]
                    dve.tensor_tensor(rows, ACC[u][:, :].rearrange("p (a n) -> p a n", a=2), rows, ALU.add).then_inc(res_full, 1)

            for j, (_, dst) in enumerate(pieces):
                dve.wait_ge(w_hi, j + 1)
                dve.tensor_tensor(dst(LO), staging(j), dst(HI), ALU.subtract).then_inc(w_lo, 1)
            dve.wait_ge(w_hi, len(pieces) + 1)
            dve.tensor_tensor(WR[:, LO], gate_raw[:], WR[:, HI], ALU.subtract).then_inc(w_lo, 1)
            dve.wait_ge(w_lo, len(pieces) + 1)
            dve.wait_ge(cw_set, 2)
            rms_apply(0)
            x_split(0)
            top_logit(0)
            route(0)
            cw_split(0)
            scale(0, 0)
            with dve.Fori(0, NC - 1) as c:
                chunk(c)
            chunk(NC - 1, last=True)

        @block.gpsimd
        def _(pool):
            pool.dma_start(SEL[:], d["sel_e"]).then_inc(sel_in, 16)
            pool.sem_inc(hh_full, 1)
            pool.sem_inc(stored, 16)
            pool.memset(inv_dim[:], 1.0 / DIM)
            pool.memset(eps[:], 1e-6)
            pool.memset(mhalf[:], -0.5)
            pool.memset(cw[:], 0.0).then_inc(cw_set, 1)
            pool.wait_ge(cw_set, 1)
            pool.memset(cw[:, :, EXPERTS:EXPERTS + 1], 1.0).then_inc(cw_set, 1)

            def rms_rstd(c):
                pool.wait_ge(msq_full, 4 * c + 4)
                pool.tensor_tensor(rr[:], msq[:], inv_dim[:], ALU.mult).then_inc(var_full, 1)
                pool.wait_ge(var_full, 2 * c + 1)
                pool.tensor_tensor(rr[:], rr[:], eps[:], ALU.add).then_inc(var_full, 1)
                pool.wait_ge(var_full, 2 * c + 2)
                pool.tensor_tensor(rr[:], rr[:], mhalf[:], ALU.pow).then_inc(rr_full, 1)

            def low(c, e):
                pool.wait_ge(hh_hi, done(c * NE + e))
                pool.tensor_tensor(HH[e % 2][:, LO], hw[:], HH[e % 2][:, HI], ALU.subtract).then_inc(hh_full, 1)

            def chunk(c, last=False):
                for e in range(NE):
                    if not (last and e == NE - 1):
                        low(*after(c, e + 1))
                    if e == 3:
                        pool.wait_ge(x2_in, 16 * c + 16)
                        pool.wait_ge(xk_in, 16 * c + 16)
                        pool.wait_ge(stored, 16 * c + 16)
                        pool.tensor_tensor(xs[:], x2[:], xk[:], ALU.add).then_inc(xs_full, 1)
                    if e == 11 and not last:
                        rms_rstd(c + 1)

            rms_rstd(0)
            low(0, 0)
            with pool.Fori(0, NC - 1) as c:
                chunk(c)
            chunk(NC - 1, last=True)

        @block.tensor
        def _(pe):
            pe.sem_inc(down_done, 1)
            pe.sem_inc(back_full, 1)

            def x_turn(c):
                pe.wait_ge(xn_full, c + 1)
                for j, (r, B) in enumerate((("G", G), ("U", U))):
                    bank = free(pe, r, "x", c)
                    for t in range(CT4):
                        mm = pe.transpose(B[bank][:, t * P:(t + 1) * P], xn[:, t, j * P:(j + 1) * P], ident[:])
                    mm.then_inc(full[r][bank], 1)
                bank = free(pe, "G", "logits", c)
                pe.wait_ge(x_lo, 2 * c + 2)
                for t in range(CT4):
                    for j in range(KD):
                        mm = product(pe, G[bank][:, t * EXPERTS:(t + 1) * EXPERTS], lambda a: HT[:, a, j, t * P:(t + 1) * P],
                                     lambda a: WR[:, a, j, :], j == 0, j == KD - 1)
                mm.then_inc(full["G"][bank], 1)

            def gates(c, e):
                for r, B, W in (("G", G, WG), ("U", U, WU)):
                    bank = free(pe, r, e, c)
                    for j in range(KD):
                        mm = product(pe, B[bank][:, :], lambda a: W[:, a, j, e * P:(e + 1) * P], lambda a: HT[:, a, j, :],
                                     j == 0, j == KD - 1)
                    mm.then_inc(full[r][bank], 1)

            def cw_turn(c):
                bank = free(pe, "G", "cw", c)
                pe.wait_ge(router, LINKS * c + LINKS)
                for t in range(CT4):
                    mm = pe.transpose(G[bank][0:32, t * P:(t + 1) * P], cw[:, t, :], ident[:])
                mm.then_inc(full["G"][bank], 1)

            def spread(c, e):
                if e == 0:
                    pe.wait_ge(cws_full, c + 1)
                bank = free(pe, "C", e, c)
                pe.matmul(C[bank][:, :], SEL[:, e, :], CWS[:, :], start=True, stop=True).then_inc(full["C"][bank], 1)

            def down(c, e):
                s = c * NE + e
                pe.wait_ge(hh_full, done(s))
                if e == 0:
                    pe.wait_ge(res_full, 2 * c + 2)
                for j in range(KD):
                    mm = product(pe, ACC[j][:, :], lambda a: WD[:, a, e, j * P:(j + 1) * P], lambda a: HH[e % 2][:, a, :],
                                 e == 0, e == NE - 1)
                mm.then_inc(down_done, 1)

            def chunk(c, last=False):
                for e in range(NE):
                    more = not (last and e >= 23)
                    if more:
                        if e == 23:
                            x_turn(c + 1)
                        gates(*after(c, e + 2))
                    if e == 23:
                        down(c, e)
                    if more:
                        if e == 23:
                            cw_turn(c + 1)
                        spread(*after(c, e + 2))
                    if e != 23:
                        down(c, e)
                pe.wait_ge(out_hi, 2 * c + 2)
                for t in range(CT4):
                    for j in range(KD):
                        mm = pe.transpose(ACC[t // 2][:, (t % 2) * DIM + j * P:(t % 2) * DIM + (j + 1) * P],
                                          out_t[:, j, t * P:(t + 1) * P], ident[:])
                mm.then_inc(back_full, 1)

            pe.wait_ge(tab_in, 4 * 16)
            pe.wait_ge(sel_in, 16)
            pe.wait_ge(w_lo, len(pieces) + 1)
            x_turn(0)
            gates(0, 0)
            cw_turn(0)
            spread(0, 0)
            gates(0, 1)
            spread(0, 1)
            with pe.Fori(0, NC - 1) as c:
                chunk(c)
            chunk(NC - 1, last=True)


def store_tokens(nc, X, out):
    with ExitStack() as ctx:
        stored = ctx.enter_context(nc.semaphore("stored"))
        block = ctx.enter_context(nc.Block())

        @block.sync
        def _(sp):
            sp.dma_start(out.rearrange("(t p) n -> p t n", p=P), X[:, :, :]).then_inc(stored, 16)
            sp.wait_ge(stored, 16)


def rope_tables():
    inv = (1.0 / np.float32(10000.0) ** (np.arange(0, HD, 2, dtype=np.float32) / np.float32(HD))).astype(np.float32)
    angle = np.outer(np.arange(LEN, dtype=np.float32), inv).astype(np.float32)
    cos, sin = np.cos(angle), np.sin(angle)
    return (np.tile(np.concatenate([cos, cos], 1), (2, 1)).astype(np.float32),
            np.tile(np.concatenate([-sin, sin], 1), (2, 1)).astype(np.float32))


def selectors():
    unit = np.arange(NE * P).reshape(1, NE, P)
    return ((np.arange(64) % 32)[:, None, None] == np.minimum(unit // INNER, EXPERTS)).astype(np.float32)


def constants():
    cos, sin = rope_tables()
    q, key = np.arange(P)[:, None], np.arange(P)[None, :]
    return {
        "ident": np.eye(P, dtype=np.float32), "cos": cos, "sin": sin,
        "sel_bc": np.stack([np.where(np.arange(64)[:, None] % 32 == r, np.float32(1), np.float32(0)).repeat(P, 1)
                            for r in range(2 * DSTATE)], 1),
        "smask": np.where((key > q) | (key // LEN != q // LEN), np.float32(NEG), np.float32(0)),
        "tri": (np.arange(EXPERTS)[None, :] < np.arange(EXPERTS)[:, None]).astype(np.float32).reshape(-1),
        "sel_e": selectors(),
        "xmask": np.where(np.arange(LEN)[None, :] > q % LEN, np.float32(NEG), np.float32(0)),
    }


def layouts(a):
    def kv(wk, wv):
        both = np.stack([wk.reshape(KD, P, NG, HD), wv.reshape(KD, P, NG, HD)], axis=3)
        return both.transpose(1, 0, 2, 3, 4).reshape(P, -1)

    def units(routed, shared):
        return np.concatenate([routed.reshape(ROWS, DIM), shared, np.zeros((NE * P - ROWS - SHARED, DIM), np.float32)])

    return {
        "wg": units(a["L0_ffn_eg_w"], a["L0_ffn_sg_w"]).T, "wu": units(a["L0_ffn_eu_w"], a["L0_ffn_su_w"]).T,
        "wd": units(a["L0_ffn_ed_w"].transpose(0, 2, 1), a["L0_ffn_sd_w"].T), "wr": a["L0_ffn_gate_w"].T,
        "x": a["x"].reshape(BATCH * LEN, DIM),
        "ctxT": a["ctx_2048"].reshape(NT, 2 * CTX, KD, P).transpose(0, 3, 2, 1),
        "wq": a["L0_xattn_wq"], "wo": a["L0_xattn_wo"],
        "wkv": kv(a["L0_xattn_wk"], a["L0_xattn_wv"]), "wkvc": kv(a["L0_xattn_wk_ctx"], a["L0_xattn_wv_ctx"]),
        "xproj": a["L0_attn_x_proj_w"].T, "dtproj": a["L0_attn_dt_proj_w"].T, "dtbias": a["L0_attn_dt_proj_b"].reshape(KD, P).T,
        "alog": a["L0_attn_A_log"], "skip": a["L0_attn_D"].reshape(KD, P).T,
        "ffn_wq": a["L0_ffn_wq"], "ffn_wk": a["L0_ffn_wk"], "ffn_wv": a["L0_ffn_wv"], "ffn_wo": a["L0_ffn_wo"],
        "ln1": a["L0_ffn_ln1_w"], "ln2": a["L0_ffn_ln2_w"],
        "qnorm": a["L0_xattn_q_norm_w"], "knorm": a["L0_xattn_k_norm_w"],
    }


def perceiver_block(nc, d, out):
    x_kept, x2_kept = (nc.dram_tensor(n, (BATCH * LEN, DIM), F32, kind="Internal").ap() for n in ("x_kept", "x2_kept"))
    with ExitStack() as ctx:
        X = ctx.enter_context(nc.sbuf_tensor("X", [P, NT, DIM], F32))
        cross_attention(nc, X, d["x"], d)
        selective_scan(nc, X, d)
        self_attention(nc, X, x_kept, d)
        store_tokens(nc, X, x2_kept)
    mixture_of_experts(nc, x_kept, x2_kept, d, out)


def kernel(**inputs):
    import concourse.bacc as bacc
    from concourse.bass_utils import run_bass_kernel_spmd as run

    nc = bacc.Bacc("TRN2", target_bir_lowering=False, num_devices=1)
    arrays = {n: np.ascontiguousarray(v) for n, v in {**layouts({n: np.asarray(v) for n, v in inputs.items()}), **constants()}.items()}
    d = {n: nc.dram_tensor(f"{n}_dram", v.shape, F32, kind="ExternalInput").ap() for n, v in arrays.items()}
    out = nc.dram_tensor("out_dram", (BATCH * LEN, DIM), F32, kind="ExternalOutput").ap()
    perceiver_block(nc, d, out)
    r = run(nc, [{f"{n}_dram": v for n, v in arrays.items()}], core_ids=[0])
    return r.results[0]["out_dram"].reshape(BATCH, LEN, DIM)
```

```python
from contextlib import ExitStack

import numpy as np

import concourse.bass as bass
from concourse import mybir

F32 = mybir.dt.float32
F32R = mybir.dt.float32r
ALU = mybir.AluOpType
ACT = mybir.ActivationFunctionType
AX = mybir.AxisListType

P = 128
BATCH, LEN, DIM = 32, 64, 256
CTX = 128
NT = BATCH * LEN // P
KD = DIM // P
HD = 128
NEG = -1.0e30

HI, LO = 0, 1
THREE = ((HI, HI), (HI, LO), (LO, HI))


class Kit:

    def __init__(self, nc, ctx, tag):
        self.nc, self.ctx, self.tag = nc, ctx, tag

    def sb(self, name, shape, dt=F32):
        return self.ctx.enter_context(self.nc.sbuf_tensor(f"{self.tag}_{name}", shape, dt))

    def ps(self, name, shape):
        return self.ctx.enter_context(self.nc.psum_tensor(f"{self.tag}_{name}", shape, F32))

    def sem(self, name):
        return self.ctx.enter_context(self.nc.semaphore(f"{self.tag}_{name}"))

    def sems(self, name, n=2):
        return [self.sem(f"{name}{j}") for j in range(n)]


def product(pe, out, lhs, rhs, start, stop, **kw):
    for n, (a, b) in enumerate(THREE):
        last = pe.matmul(out, lhs(a), rhs(b), start=start and n == 0, stop=stop and n == 2, **kw)
    return last


NQ, NG, REP = 16, 4, 4
KEYS = CTX + LEN


def cross_attention(nc, X, xd, d):
    with ExitStack() as ctx:
        k = Kit(nc, ctx, "xa")
        sb, sem, sems = k.sb, k.sem, k.sems
        WQ = sb("WQ", [P, 2, KD, NQ * HD], F32R)
        WKV = sb("WKV", [P, 2, KD, NG, 2 * HD], F32R)
        WKVC = sb("WKVC", [P, 2, KD, NG, 2 * HD], F32R)
        WO = sb("WO", [P, 2, NQ, DIM], F32R)
        stage = [sb(f"stage{j}", [P, 2048]) for j in range(2)]
        ident = sb("ident", [P, P])
        cosw = [sb(f"cosw{j}", [P, HD]) for j in range(2)]
        sinw = [sb(f"sinw{j}", [P, HD]) for j in range(2)]
        normw = [sb(f"normw{j}", [P, HD]) for j in range(2)]
        cos, sin = sb("cos", [P, HD]), sb("sin", [P, HD])
        mask = sb("mask", [P, LEN])
        mhalf, lneps = sb("mhalf", [P, 8]), sb("lneps", [P, 1])
        stats, mv, rstd, xn = sb("stats", [P, 6]), sb("mv", [P, 2]), sb("rstd", [P, 1]), sb("xn", [P, DIM])
        XT = sb("XT", [P, 2, KD, P], F32R)
        ctx_raw = sb("ctx_raw", [P, KD, 2 * CTX])
        CT = sb("CT", [P, 2, KD, 2 * CTX], F32R)
        sq, t1, t2, qn = sb("sq", [P, 7, HD]), sb("t1", [P, 7, HD]), sb("t2", [P, 5, HD]), sb("qn", [P, 7, HD])
        ss, var, rs = sb("ss", [P, 8]), sb("var", [P, 8]), sb("rs", [P, 8])
        QT = [sb(f"QT{j}", [P, 2, 2, REP * LEN], F32R) for j in range(2)]
        KT = [sb(f"KT{j}", [P, 2, 2, KEYS], F32R) for j in range(2)]
        VS = [sb(f"VS{j}", [P, 2, HD], F32R) for j in range(NG)]
        VC = [sb(f"VC{j}", [P, 2, 2, HD], F32R) for j in range(NG)]
        PR = [sb(f"PR{b}", [P, 2, KEYS]) for b in range(2)]
        nmax = [sb(f"nmax{b}", [P, 2]) for b in range(2)]
        rsum = [sb(f"rsum{b}", [P, 2]) for b in range(2)]
        rinv = [sb(f"rinv{b}", [P, 2]) for b in range(2)]
        PT = [sb(f"PT{b}", [P, 2, 2, REP * LEN], F32R) for b in range(2)]
        OT = sb("OT", [P, 2, REP, P], F32R)
        J = [k.ps(f"J{j}", [P, 512]) for j in range(2)]
        T = [k.ps(f"T{j}", [P, 512]) for j in range(2)]
        S = [k.ps(f"S{b}", [P, 2, KEYS]) for b in range(2)]
        PO = k.ps("PO", [P, 2, REP * LEN])
        ACC = k.ps("ACC", [P, DIM])

        x_in, tab_in, staged = sem("x_in"), sem("tab_in"), sems("staged")
        w_hi, w_lo, tabs = sem("w_hi"), sem("w_lo"), sem("tabs")
        ctx_in, ct_hi, ct_full = sem("ctx_in"), sem("ct_hi"), sem("ct_full")
        stat_full, mv_full, rstd_full, xn_full = sem("stat_full"), sem("mv_full"), sem("rstd_full"), sem("xn_full")
        J_full = sems("J_full")
        J_act, J_dve = sems("J_act"), sems("J_dve")
        T_full, T_act, T_dve = sems("T_full"), sems("T_act"), sems("T_dve")
        S_full, S_mask = sems("S_full"), sems("S_mask")
        nmax_full, exp_full, rinv_full, pr_full = sems("nmax_full"), sems("exp_full"), sems("rinv_full"), sems("pr_full")
        ss_full, var_full, rs_full, rope_full, t_sum, qn_full = (
            sem(n) for n in ("ss_full", "var_full", "rs_full", "rope_full", "t_sum", "qn_full"))
        pv_done, ot_hi, ot_full = sems("pv_done"), sem("ot_hi"), sem("ot_full")
        wo_done, acc_read = sem("wo_done"), sem("acc_read")

        pieces = [(d["wq"].rearrange("(k p) n -> p k n", p=P)[:, c, :], lambda a, c=c: WQ[:, a, c, :]) for c in range(KD)]
        pieces += [(src, lambda a, W=W: W[:, a].rearrange("p k g n -> p (k g n)")) for src, W in ((d["wkv"], WKV), (d["wkvc"], WKVC))]
        pieces += [(d["wo"].rearrange("(h p) n -> p h n", p=P)[:, 8 * c:8 * c + 8, :],
                    lambda a, c=c: WO[:, a, 8 * c:8 * c + 8, :]) for c in range(2)]

        def staging(j):
            view = stage[j % 2][:, :]
            return view.rearrange("p (a n) -> p a n", n=DIM) if len(pieces[j][0].shape) == 3 else view

        def use(n, per, i):
            return n % 2, i * (per // 2) + n // 2

        def j_use(i, g, u):
            return use(8 + 3 * g + (2 if g >= 2 else 0) + u, 14, i)

        def j_x(i, c):
            return use(14 + c, 14, i)

        def t_use(i, g, u):
            return use(2 + 4 * g + u, 16, i)

        J_FIRST = [use(n, 14, 0) for n in range(8)]
        T_FIRST = [use(n, 16, 0) for n in range(2)]

        def pr_uses(i, g, last):
            first = 0 if last and g == NG - 1 else 2
            return [t_use(i, g, first + b) for b in range(2)]

        SELF = (slice(0, LEN), slice(CTX, KEYS))
        CKEY = (slice(LEN, KEYS), slice(0, CTX))

        block = ctx.enter_context(nc.Block())

        @block.sync
        def _(sp):
            xt = xd.rearrange("(t p) n -> p t n", p=P)
            sp.dma_start(X[:, 0:2, :], xt[:, 0:2, :]).then_inc(x_in, 16)
            sp.dma_start(ctx_raw[:], d["ctxT"][0]).then_inc(ctx_in, 16)
            for dst, src in ((ident, d["ident"]), (cos, d["cos"]), (sin, d["sin"]), (mask, d["xmask"]),
                             (normw[0], d["qnorm"].partition_broadcast(P)), (normw[1], d["knorm"].partition_broadcast(P))):
                sp.dma_start(dst[:, :], src).then_inc(tab_in, 16)
            for j, (src, _) in enumerate(pieces):
                if j >= 2:
                    sp.wait_ge(w_lo, j - 1)
                sp.dma_start(staging(j), src).then_inc(staged[j % 2], 16)
            sp.wait_ge(x_in, 16)
            sp.dma_start(X[:, 2:, :], xt[:, 2:, :]).then_inc(x_in, 16)
            with sp.Fori(1, NT) as t:
                sp.wait_ge(ct_full, t)
                sp.dma_start(ctx_raw[:].rearrange("p k n -> p (k n)").unsqueeze(1),
                             d["ctxT"].rearrange("t p k n -> p t (k n)")[:, bass.ds(t, 1), :]).then_inc(ctx_in, 16)

        @block.scalar
        def _(act):
            for j, (_, dst) in enumerate(pieces):
                act.wait_ge(staged[j % 2], 16 * (j // 2 + 1))
                act.activation(dst(HI), staging(j), ACT.Copy).then_inc(w_hi, 1)

            def context_split(t):
                act.wait_ge(ctx_in, 16 * t + 16)
                act.activation(CT[:, HI], ctx_raw[:], ACT.Copy).then_inc(ct_hi, 1)

            def x_split(uses):
                for c, (bank, n) in enumerate(uses):
                    act.wait_ge(J_full[bank], n + 1)
                    act.activation(XT[:, HI, c, :], J[bank][:, 0:P], ACT.Copy).then_inc(J_act[bank], 1)

            def square(head, src):
                return act.activation(sq[:, head, :], src, ACT.Square, accum_out=ss[:, head:head + 1])

            def project_q(use):
                bank, n = use
                act.wait_ge(J_full[bank], n + 1)
                for h in range(REP):
                    last = square(h, J[bank][:, h * HD:(h + 1) * HD])
                last.then_inc(J_act[bank], 1)

            def project_context(use, g):
                bank, n = use
                act.wait_ge(J_full[bank], n + 1)
                kv = J[bank][:, :].rearrange("p (b n) -> p b n", b=2)
                for b in range(2):
                    square(5 + b, kv[:, b, 0:HD])
                act.activation(VC[g][:, HI], kv[:, :, HD:], ACT.Copy).then_inc(J_act[bank], 1)

            def project_kv(use, g):
                bank, n = use
                act.wait_ge(J_full[bank], n + 1)
                square(4, J[bank][:, 0:HD]).then_inc(ss_full, 1)
                act.activation(VS[g][:, HI], J[bank][:, HD:2 * HD], ACT.Copy).then_inc(J_act[bank], 1)

            def q_split(use, par):
                bank, n = use
                act.wait_ge(T_full[bank], n + 1)
                act.activation(QT[par][:, HI].rearrange("p b (h l) -> p h b l", h=REP),
                               T[bank][:, :].rearrange("p (h b l) -> p h b l", h=REP, b=2), ACT.Copy).then_inc(T_act[bank], 1)

            def k_split(use, par):
                bank, n = use
                act.wait_ge(T_full[bank], n + 1)
                act.activation(KT[par][:, HI], T[bank][:, 0:2 * KEYS].rearrange("p (b n) -> p b n", b=2),
                               ACT.Copy).then_inc(T_act[bank], 1)

            def exps(s, b):
                act.wait_ge(nmax_full[b], s + 1)
                act.wait_ge(pv_done[b], s + 1)
                for pair in range(2):
                    act.activation(PR[b][:, pair, :], S[b][:, pair, :], ACT.Exp, bias=nmax[b][:, pair:pair + 1],
                                   accum_out=rsum[b][:, pair:pair + 1]).then_inc(exp_full[b], 1)

            def slot(i, g, last=False):
                s = 4 * i + g
                turn, project = not (last and g == NG - 1), not (last and g >= 2)
                exps(s, 0)
                if turn:
                    act.wait_ge(S_full[1], s + 1)
                    q_split(t_use(i, g, 0), (g + 1) % 2)
                exps(s, 1)
                if project:
                    project_q(j_use(i, g, 0))
                if turn:
                    k_split(t_use(i, g, 1), (g + 1) % 2)
                if project:
                    project_context(j_use(i, g, 1), (g + 2) % NG)
                for b, (bank, n) in enumerate(pr_uses(i, g, last)):
                    act.wait_ge(T_full[bank], n + 1)
                    act.activation(PT[b][:, HI], T[bank][:, :].rearrange("p (a n) -> p a n", a=2),
                                   ACT.Copy).then_inc(T_act[bank], 1)
                if project:
                    project_kv(j_use(i, g, 2), (g + 2) % NG)
                if g == 1 and not last:
                    context_split(i + 1)
                act.wait_ge(pv_done[1], s + 2)
                act.wait_ge(wo_done, s + 1)
                act.activation(OT[:, HI].rearrange("p h (b l) -> p b h l", b=2),
                               PO[:, :, :].rearrange("p b (h l) -> p b h l", h=REP), ACT.Copy).then_inc(ot_hi, 1)
                if g == 1 and not last:
                    x_split([j_x(i, c) for c in range(KD)])

            context_split(0)
            x_split(J_FIRST[0:2])
            for g in range(2):
                if g:
                    act.wait_ge(qn_full, 2)
                project_q(J_FIRST[2 + 3 * g])
                project_context(J_FIRST[3 + 3 * g], g)
                project_kv(J_FIRST[4 + 3 * g], g)
            q_split(T_FIRST[0], 0)
            k_split(T_FIRST[1], 0)
            with act.Fori(0, NT - 1) as i:
                for g in range(NG):
                    slot(i, g)
            for g in range(NG):
                slot(NT - 1, g, last=True)

        @block.vector
        def _(dve):
            for unused in (ot_full, acc_read):
                dve.sem_inc(unused, 1)
            dve.wait_ge(tab_in, 6 * 16)
            half = HD // 2
            for j, scale in enumerate((HD ** -0.5, 1.0)):
                dve.scalar_tensor_tensor(cosw[j][:], cos[:], scale, normw[j][:], ALU.mult, ALU.mult)
                dve.scalar_tensor_tensor(sinw[j][:, :half], sin[:, :half], scale, normw[j][:, half:], ALU.mult, ALU.mult)
                dve.scalar_tensor_tensor(sinw[j][:, half:], sin[:, half:], scale, normw[j][:, :half], ALU.mult, ALU.mult).then_inc(tabs, 1)

            def norm_stats(x):
                dve.bn_stats(stats[:], x).then_inc(stat_full, 1)

            def norm_var():
                dve.bn_aggr(mv[:], stats[:]).then_inc(mv_full, 1)

            def norm_apply(x, t):
                dve.wait_ge(rstd_full, t + 1)
                dve.tensor_scalar(xn[:], x, mv[:, 0:1], rstd[:, 0:1], ALU.subtract, ALU.mult).then_inc(xn_full, 1)

            dve.wait_ge(x_in, 16)
            norm_stats(X[:, 0, :])
            dve.wait_ge(stat_full, 1)
            norm_var()
            for j, (_, dst) in enumerate(pieces):
                dve.wait_ge(w_hi, j + 1)
                dve.tensor_tensor(dst(LO), staging(j), dst(HI), ALU.subtract).then_inc(w_lo, 1)
            norm_apply(X[:, 0, :], 0)

            def context_split(t):
                dve.wait_ge(ct_hi, t + 1)
                dve.tensor_tensor(CT[:, LO], ctx_raw[:], CT[:, HI], ALU.subtract).then_inc(ct_full, 1)

            def x_split(uses):
                for c, (bank, n) in enumerate(uses):
                    dve.wait_ge(J_act[bank], n + 1)
                    dve.tensor_tensor(XT[:, LO, c, :], J[bank][:, 0:P], XT[:, HI, c, :], ALU.subtract).then_inc(J_dve[bank], 1)

            def rope(src, first, heads, j):
                v = src.rearrange("p (h e) -> p h e", h=heads)
                half = HD // 2
                dve.tensor_tensor(t1[:, first:first + heads, :], v, cosw[j][:, None, :].broadcast_to([P, heads, HD]), ALU.mult)
                dve.tensor_tensor(t2[:, first:first + heads, :half], v[:, :, half:],
                                  sinw[j][:, None, :half].broadcast_to([P, heads, half]), ALU.mult)
                return dve.tensor_tensor(t2[:, first:first + heads, half:], v[:, :, :half],
                                         sinw[j][:, None, half:].broadcast_to([P, heads, half]), ALU.mult)

            def project_q(use):
                bank, n = use
                dve.wait_ge(J_act[bank], n + 1)
                rope(J[bank][:, :], 0, REP, 0).then_inc(J_dve[bank], 1)

            def project_context(use, g):
                bank, n = use
                kv = J[bank][:, :].rearrange("p (b n) -> p b n", b=2)
                dve.wait_ge(J_act[bank], n + 1)
                dve.tensor_tensor(t1[:, 5:7, :], kv[:, :, 0:HD], normw[1][:, None, :].broadcast_to([P, 2, HD]), ALU.mult)
                dve.tensor_tensor(VC[g][:, LO], kv[:, :, HD:], VC[g][:, HI], ALU.subtract).then_inc(J_dve[bank], 1)

            def project_kv(use, g):
                bank, n = use
                dve.wait_ge(J_act[bank], n + 1)
                rope(J[bank][:, 0:HD], 4, 1, 1).then_inc(rope_full, 1)
                dve.tensor_tensor(VS[g][:, LO], J[bank][:, HD:2 * HD], VS[g][:, HI], ALU.subtract).then_inc(J_dve[bank], 1)

            def q_split(use, par):
                bank, n = use
                dve.wait_ge(T_act[bank], n + 1)
                dve.tensor_tensor(QT[par][:, LO].rearrange("p b (h l) -> p h b l", h=REP),
                                  T[bank][:, :].rearrange("p (h b l) -> p h b l", h=REP, b=2),
                                  QT[par][:, HI].rearrange("p b (h l) -> p h b l", h=REP), ALU.subtract).then_inc(T_dve[bank], 1)

            def k_split(use, par):
                bank, n = use
                dve.wait_ge(T_act[bank], n + 1)
                dve.tensor_tensor(KT[par][:, LO], T[bank][:, 0:2 * KEYS].rearrange("p (b n) -> p b n", b=2),
                                  KT[par][:, HI], ALU.subtract).then_inc(T_dve[bank], 1)

            def normalise(s, b):
                dve.wait_ge(exp_full[b], 2 * s + 2)
                dve.reciprocal(rinv[b][:], rsum[b][:]).then_inc(rinv_full[b], 1)
                dve.wait_ge(rinv_full[b], s + 1)
                for pair in range(2):
                    done = dve.tensor_scalar(PR[b][:, pair, :], PR[b][:, pair, :], rinv[b][:, pair:pair + 1], None, ALU.mult)
                done.then_inc(pr_full[b], 1)

            def maxima(s):
                for b in range(2):
                    dve.wait_ge(S_full[b], s + 2)
                    own = S[b][:, :, SELF[b]]
                    dve.tensor_tensor(own, own, mask[:, None, :].broadcast_to([P, 2, LEN]), ALU.add).then_inc(S_mask[b], 1)
                    dve.wait_ge(S_mask[b], s + 1)
                    dve.tensor_reduce(nmax[b][:], S[b][:, :, :], AX.X, ALU.max, negate=True).then_inc(nmax_full[b], 1)

            def slot(i, g, last=False):
                s = 4 * i + g
                turn, project = not (last and g == NG - 1), not (last and g >= 2)
                if g == 0 and not last:
                    norm_stats(X[:, bass.ds(i + 1, 1), :].rearrange("p a n -> p (a n)"))
                normalise(s, 0)
                if turn:
                    q_split(t_use(i, g, 0), (g + 1) % 2)
                if g == 0 and not last:
                    dve.wait_ge(stat_full, i + 2)
                normalise(s, 1)
                if g == 0 and not last:
                    norm_var()
                if project:
                    project_q(j_use(i, g, 0))
                if turn:
                    k_split(t_use(i, g, 1), (g + 1) % 2)
                if project:
                    project_context(j_use(i, g, 1), (g + 2) % NG)
                for b, (bank, n) in enumerate(pr_uses(i, g, last)):
                    dve.wait_ge(T_act[bank], n + 1)
                    dve.tensor_tensor(PT[b][:, LO], T[bank][:, :].rearrange("p (a n) -> p a n", a=2),
                                      PT[b][:, HI], ALU.subtract).then_inc(T_dve[bank], 1)
                if project:
                    project_kv(j_use(i, g, 2), (g + 2) % NG)
                if g == 0 and not last:
                    norm_apply(X[:, bass.ds(i + 1, 1), :].rearrange("p a n -> p (a n)"), i + 1)
                if g == 1 and not last:
                    context_split(i + 1)
                dve.wait_ge(ot_hi, s + 1)
                dve.tensor_tensor(OT[:, LO].rearrange("p h (b l) -> p b h l", b=2),
                                  PO[:, :, :].rearrange("p b (h l) -> p b h l", h=REP),
                                  OT[:, HI].rearrange("p h (b l) -> p b h l", b=2), ALU.subtract).then_inc(ot_full, 1)
                if turn:
                    maxima(s + 1)
                if g == 1 and not last:
                    x_split([j_x(i, c) for c in range(KD)])
                if g == NG - 1:
                    dve.wait_ge(wo_done, s + 2)
                    x = X[:, bass.ds(i, 1), :].rearrange("p a n -> p (a n)") if not last else X[:, i, :]
                    dve.tensor_tensor(x, ACC[:, :], x, ALU.add).then_inc(acc_read, 1)

            dve.wait_ge(tabs, 2)
            context_split(0)
            x_split(J_FIRST[0:2])
            for g in range(2):
                if g:
                    dve.wait_ge(qn_full, 2)
                project_q(J_FIRST[2 + 3 * g])
                project_context(J_FIRST[3 + 3 * g], g)
                project_kv(J_FIRST[4 + 3 * g], g)
            q_split(T_FIRST[0], 0)
            k_split(T_FIRST[1], 0)
            maxima(0)
            dve.wait_ge(x_in, 32)
            with dve.Fori(0, NT - 1) as i:
                for g in range(NG):
                    slot(i, g)
            for g in range(NG):
                slot(NT - 1, g, last=True)

        @block.gpsimd
        def _(pool):
            pool.memset(lneps[:], 1e-5)
            pool.memset(mhalf[:], -0.5).then_inc(var_full, 1)
            pool.wait_ge(var_full, 1)

            def ln_rstd(t, n):
                pool.wait_ge(mv_full, t + 1)
                pool.tensor_tensor(rstd[:], mv[:, 1:2], lneps[:], ALU.add).then_inc(var_full, 1)
                pool.wait_ge(var_full, n + 1)
                pool.tensor_tensor(rstd[:], rstd[:], mhalf[:, 0:1], ALU.pow).then_inc(rstd_full, 1)

            def norms(s, n, q_use, k_turn=None):
                def scaled(heads):
                    return pool.tensor_tensor(qn[:, heads, :], t1[:, heads, :],
                                              rs[:, heads, None].broadcast_to([P, heads.stop - heads.start, HD]), ALU.mult)

                pool.wait_ge(J_dve[q_use[0]], q_use[1] + 1)
                pool.tensor_tensor(t1[:, 0:4, :], t1[:, 0:4, :], t2[:, 0:4, :], ALU.add).then_inc(t_sum, 1)
                pool.wait_ge(ss_full, s + 1)
                pool.tensor_tensor(var[:, 7:8], mhalf[:, 7:8], mhalf[:, 7:8], ALU.mult)
                pool.tensor_scalar(var[:, 0:7], ss[:, 0:7], 1.0 / HD, 1e-6, ALU.mult, ALU.add).then_inc(var_full, 1)
                pool.wait_ge(var_full, n + 1)
                pool.tensor_tensor(rs[:, 0:7], var[:, 0:7], mhalf[:, 0:7], ALU.pow).then_inc(rs_full, 1)
                pool.wait_ge(rope_full, s + 1)
                pool.tensor_tensor(t1[:, 4, :], t1[:, 4, :], t2[:, 4, :], ALU.add).then_inc(t_sum, 1)
                pool.wait_ge(rs_full, s + 1)
                pool.wait_ge(t_sum, 2 * s + 2)
                if k_turn:
                    pool.wait_ge(T_full[k_turn[0]], k_turn[1] + 1)
                scaled(slice(0, 4)).then_inc(qn_full, 1)
                scaled(slice(4, 7)).then_inc(qn_full, 1)

            ln_rstd(0, 1)
            norms(0, 2, J_FIRST[2])
            norms(1, 3, J_FIRST[5], T_FIRST[1])
            with pool.Fori(0, NT - 1) as i:
                for g in range(NG):
                    if g == 0:
                        ln_rstd(i + 1, 5 * i + 4)
                    norms(4 * i + g + 2, 5 * i + 5 + g, j_use(i, g, 0), t_use(i, g, 1))
            for g in range(2):
                norms(4 * (NT - 1) + g + 2, 5 * (NT - 1) + 4 + g, j_use(NT - 1, g, 0), t_use(NT - 1, g, 1))

        @block.tensor
        def _(pe):
            def fill_j(bank, n):
                if not (isinstance(n, int) and n == 0):
                    pe.wait_ge(J_dve[bank], n)

            def x_turn(uses, t):
                pe.wait_ge(xn_full, t + 1)
                for c, (bank, n) in enumerate(uses):
                    fill_j(bank, n)
                    pe.transpose(J[bank][:, 0:P], xn[:, c * P:(c + 1) * P], ident[:]).then_inc(J_full[bank], 1)

            def project_q(uses, g):
                (bq, nq), (bc, n_c), _ = uses
                fill_j(bq, nq)
                if g == 0:
                    fill_j(bc, n_c)
                for c in range(KD):
                    mm = product(pe, J[bq][:, :], lambda a: XT[:, a, c, :], lambda a: WQ[:, a, c, g * 512:(g + 1) * 512],
                                 c == 0, c == KD - 1)
                mm.then_inc(J_full[bq], 1)

            def project_context(uses, g, t):
                bc, n_c = uses[1]
                fill_j(bc, n_c)
                if g == 0:
                    pe.wait_ge(ct_full, t + 1)
                for b in range(2):
                    for c in range(KD):
                        mm = product(pe, J[bc][:, b * 256:(b + 1) * 256], lambda a: CT[:, a, c, b * CTX:(b + 1) * CTX],
                                     lambda a: WKVC[:, a, c, g, :], c == 0, c == KD - 1)
                mm.then_inc(J_full[bc], 1)

            def project_kv(uses, g):
                bs, n_s = uses[2]
                fill_j(bs, n_s)
                for c in range(KD):
                    mm = product(pe, J[bs][:, 0:256], lambda a: XT[:, a, c, :], lambda a: WKV[:, a, c, g, :], c == 0, c == KD - 1)
                mm.then_inc(J_full[bs], 1)

            def q_turn(use, s):
                bank, n = use
                pe.wait_ge(qn_full, 2 * s + 1)
                if not (isinstance(n, int) and n == 0):
                    pe.wait_ge(T_dve[bank], n)
                for h in range(REP):
                    mm = pe.transpose(T[bank][:, h * P:(h + 1) * P], qn[:, h, :], ident[:])
                mm.then_inc(T_full[bank], 1)

            def k_turn(use, s):
                bank, n = use
                pe.wait_ge(qn_full, 2 * s + 2)
                if not (isinstance(n, int) and n == 0):
                    pe.wait_ge(T_dve[bank], n)
                for b in range(2):
                    pe.transpose(T[bank][:, b * KEYS + CKEY[b].start:b * KEYS + CKEY[b].stop], qn[:, 5 + b, :], ident[:])
                own = T[bank][:, 0:2 * KEYS].rearrange("p (r l) -> p r l", l=LEN)[:, ::5, :]
                pe.transpose(own, qn[:, 4, :], ident[:]).then_inc(T_full[bank], 1)

            def scores(uses, s, par):
                (bq, nq), (bk, nk) = uses
                pe.wait_ge(T_dve[bq], nq + 1)
                pe.wait_ge(T_dve[bk], nk + 1)
                for b in range(2):
                    if not (isinstance(s, int) and s == 0):
                        pe.wait_ge(exp_full[b], 2 * s)
                    for pair in range(2):
                        mm = product(pe, S[b][:, pair, :], lambda a: QT[par][:, a, b, pair * P:(pair + 1) * P],
                                     lambda a: KT[par][:, a, b, :], True, True)
                    mm.then_inc(S_full[b], 1)

            def slot(i, g, last=False):
                s = 4 * i + g
                uses = [j_use(i, g, u) for u in range(3)]
                next_qk = [t_use(i, g, u) for u in (0, 1)]
                turn, project = not (last and g == NG - 1), not (last and g >= 2)
                if turn:
                    q_turn(next_qk[0], s + 1)
                if project:
                    project_q(uses, (g + 2) % NG)
                if turn:
                    k_turn(next_qk[1], s + 1)
                if project:
                    project_context(uses, (g + 2) % NG, i + 1)
                for b, (bank, n) in enumerate(pr_uses(i, g, last)):
                    pe.wait_ge(pr_full[b], s + 1)
                    pe.wait_ge(T_dve[bank], n)
                    at_own = (0, LEN)[b]
                    for part, col in ((0, CKEY[b].start), (1, at_own)):
                        for pair in range(2):
                            mm = pe.transpose(T[bank][:, part * 256 + pair * P:part * 256 + (pair + 1) * P],
                                              PR[b][:, pair, col:col + P], ident[:])
                    mm.then_inc(T_full[bank], 1)
                if project:
                    project_kv(uses, (g + 2) % NG)
                for b, (bank, n) in enumerate(pr_uses(i, g, last)):
                    pe.wait_ge(T_dve[bank], n + 1)
                    if b == 0:
                        pe.wait_ge(ot_full, s + 1)
                    product(pe, PO[:, b, :], lambda a: VC[g][:, a, b, :], lambda a: PT[b][:, a, 0, :], True, False)
                    own = slice(b * LEN, (b + 1) * LEN)
                    if b == 1:
                        pe.wait_ge(pv_done[0], s + 2)
                    product(pe, PO[:, b, :], lambda a: VS[g][own, a, :], lambda a: PT[b][own, a, 1, :], False, True)\
                        .then_inc(pv_done[b], 1)
                if turn:
                    scores(next_qk, s + 1, (g + 1) % 2)
                if g == 1 and not last:
                    x_turn([j_x(i, c) for c in range(KD)], i + 1)
                pe.wait_ge(ot_full, s + 2)
                if g == 0:
                    pe.wait_ge(acc_read, i + 1)
                for h in range(REP):
                    mm = product(pe, ACC[:, :], lambda a: OT[:, a, h, :], lambda a: WO[:, a, REP * g + h, :],
                                 g == 0 and h == 0, g == NG - 1 and h == REP - 1)
                mm.then_inc(wo_done, 1)

            for unused in (*pv_done, *S_full, wo_done):
                pe.sem_inc(unused, 1)
            pe.wait_ge(tab_in, 6 * 16)
            x_turn(J_FIRST[0:2], 0)
            pe.wait_ge(w_lo, len(pieces))
            for g in range(2):
                project_q(J_FIRST[2 + 3 * g:5 + 3 * g], g)
                project_context(J_FIRST[2 + 3 * g:5 + 3 * g], g, 0)
                project_kv(J_FIRST[2 + 3 * g:5 + 3 * g], g)
            q_turn(T_FIRST[0], 0)
            k_turn(T_FIRST[1], 0)
            scores(T_FIRST, 0, 0)
            with pe.Fori(0, NT - 1) as i:
                for g in range(NG):
                    slot(i, g)
            for g in range(NG):
                slot(NT - 1, g, last=True)


DSTATE, DTRANK = 16, 128
CT4 = 4
NC = NT // CT4
CHUNK = CT4 * P


def tokens(X, c, first=0, n=CT4):
    return X[:, bass.ds(c * CT4 + first, n), :]


def tile_of(X, c, t):
    return tokens(X, c, t, 1).rearrange("p a n -> p (a n)")


def selective_scan(nc, X, d):
    with ExitStack() as ctx:
        k = Kit(nc, ctx, "ss")
        sb, sem, sems = k.sb, k.sem, k.sems
        ident, scrap, lneps, mhalf = sb("ident", [P, P]), sb("scrap", [P, 1]), sb("lneps", [P, CT4]), sb("mhalf", [P, CT4])
        w_raw = sb("w_raw", [P, KD, DTRANK + 2 * DSTATE])
        W = sb("W", [P, 2, KD, DTRANK + 2 * DSTATE], F32R)
        dt_raw, DTW = sb("dt_raw", [P, DIM]), sb("DTW", [P, 2, DIM], F32R)
        sel_raw = sb("sel_raw", [64, 2 * DSTATE, P])
        SEL = sb("SEL", [64, 2 * DSTATE, P], F32R)
        bias, alog, A, skip = sb("bias", [P, KD]), sb("alog", [P, KD, DSTATE]), sb("A", [P, KD, DSTATE]), sb("skip", [P, KD])
        stats, mv, rstd = sb("stats", [P, CT4, 6]), sb("mv", [P, CT4, 2]), sb("rstd", [P, CT4])
        xn = sb("xn", [P, CT4, DIM])
        XT, XF = sb("XT", [P, 2, KD, CHUNK], F32R), sb("XF", [P, KD, CHUNK])
        DL, BC = sb("DL", [P, 2, CHUNK], F32R), sb("BC", [64, CHUNK], F32R)
        az, rz, ez, lz = (sb(n, [P, KD, CHUNK]) for n in ("az", "rz", "ez", "lz"))
        dt, u, y = (sb(n, [P, KD, CHUNK]) for n in ("dt", "u", "y"))
        decay = [sb(f"decay{j}", [P, CHUNK // LEN, LEN]) for j in range(2)]
        bx, state = sb("bx", [P, CHUNK]), sb("state", [P, CHUNK])
        cy = [sb(f"cy{j}", [P, CHUNK]) for j in range(2)]
        M = [k.ps(f"M{j}", [P, CHUNK]) for j in range(2)]
        BB = [k.ps(f"BB{j}", [P, CHUNK]) for j in range(2)]
        CB = [k.ps(f"CB{j}", [P, CHUNK]) for j in range(2)]
        YT = [k.ps(f"YT{j}", [P, 2, DIM]) for j in range(2)]

        w_in, w_hi, w_full, decay_zero = sem("w_in"), sem("w_hi"), sem("w_full"), sem("decay_zero")
        stat_full, mv_full, var_full, rstd_full, xn_full = (sem(n) for n in ("stat_full", "mv_full", "var_full", "rstd_full", "xn_full"))
        M_full, M_act, M_dve = sems("M_full"), sems("M_act"), sems("M_dve")
        ez_full, lz_full, dt_full, du_full = (sem(n) for n in ("ez_full", "lz_full", "dt_full", "du_full"))
        decay_full, bb_full, cb_full = sem("decay_full"), sem("bb_full"), sem("cb_full")
        bx_full, state_full, cy_full, y_sum = sem("bx_full"), sem("state_full"), sem("cy_full"), sem("y_sum")
        yt_full, x_sum = sem("yt_full"), sem("x_sum")
        Q = KD * DSTATE

        def step(c, q):
            return c * Q + (q + 3)

        block = ctx.enter_context(nc.Block())

        @block.sync
        def _(sp):
            for dst, src in ((ident, d["ident"]), (w_raw, d["xproj"].rearrange("(k p) n -> p k n", p=P)), (dt_raw, d["dtproj"]),
                             (sel_raw, d["sel_bc"]), (bias, d["dtbias"]),
                             (alog, d["alog"].rearrange("(k p) n -> p k n", p=P)), (skip, d["skip"])):
                sp.dma_start(dst[:], src).then_inc(w_in, 16)

        @block.scalar
        def _(act):
            act.wait_ge(w_in, 7 * 16)
            act.activation(W[:, HI], w_raw[:], ACT.Copy)
            act.activation(DTW[:, HI], dt_raw[:], ACT.Copy)
            act.activation(SEL[:], sel_raw[:], ACT.Copy)
            act.activation(A[:], alog[:], ACT.Exp).then_inc(w_hi, 1)
            act.wait_ge(decay_zero, 1)

            def chunk(c):
                for j in range(KD):
                    act.wait_ge(M_full[j], 3 * c + 1)
                    act.activation(XT[:, HI, j, :], M[j][:, :], ACT.Copy)
                    act.activation(XF[:, j, :], M[j][:, :], ACT.Copy).then_inc(M_act[j], 1)
                act.wait_ge(M_full[0], 3 * c + 2)
                act.activation(DL[:, HI], M[0][:, :], ACT.Copy).then_inc(M_act[0], 1)
                act.wait_ge(M_full[1], 3 * c + 2)
                act.activation(BC[0:32, :], M[1][0:32, :], ACT.Copy).then_inc(M_act[1], 1)
                for j in range(KD):
                    act.wait_ge(M_full[j], 3 * c + 3)
                    act.activation(az[:, j, :], M[j][:, :], ACT.Abs, bias=bias[:, j:j + 1]).then_inc(M_act[j], 1)
                for j in range(KD):
                    act.wait_ge(M_act[j], 3 * c + 3)
                    act.activation(ez[:, j, :], az[:, j, :], ACT.Exp, scale=-1.0).then_inc(ez_full, 1)
                act.wait_ge(ez_full, 2 * c + 2)
                for j in range(KD):
                    act.activation(lz[:, j, :], ez[:, j, :], ACT.Ln, bias=1.0).then_inc(lz_full, 1)
                for q in range(Q):
                    half, n = divmod(q, DSTATE)
                    if n == 0:
                        act.wait_ge(du_full, 2 * c + half + 1)
                    act.wait_ge(state_full, step(c, q - 2))
                    act.activation(decay[q % 2][:, :, 1:], dt[:, half, :].rearrange("p (b l) -> p b l", l=LEN)[:, :, 1:],
                                   ACT.Exp, scale=A[:, half, n:n + 1]).then_inc(decay_full, 1)

            with act.Fori(0, NC) as c:
                chunk(c)

        @block.vector
        def _(dve):
            for used in (bx_full, state_full, cy_full):
                dve.sem_inc(used, 2)
            dve.memset(decay[0][:], 0.0)
            dve.memset(decay[1][:], 0.0).then_inc(decay_zero, 1)
            dve.wait_ge(w_hi, 1)
            dve.tensor_tensor(W[:, LO], w_raw[:], W[:, HI], ALU.subtract)
            dve.tensor_tensor(DTW[:, LO], dt_raw[:], DTW[:, HI], ALU.subtract)
            dve.tensor_scalar(A[:], A[:], -1.0, None, ALU.mult).then_inc(w_full, 1)

            def chunk(c):
                for t in range(CT4):
                    done = dve.bn_stats(stats[:, t, :], tile_of(X, c, t))
                done.then_inc(stat_full, 1)
                dve.wait_ge(stat_full, c + 1)
                dve.memset(scrap[:], 0.0)
                for t in range(CT4):
                    done = dve.bn_aggr(mv[:, t, :], stats[:, t, :])
                done.then_inc(mv_full, 1)
                dve.wait_ge(rstd_full, c + 1)
                dve.memset(scrap[:], 0.0)
                for t in range(CT4):
                    done = dve.tensor_scalar(xn[:, t, :], tile_of(X, c, t), mv[:, t, 0:1], rstd[:, t:t + 1], ALU.subtract, ALU.mult)
                done.then_inc(xn_full, 1)
                for j in range(KD):
                    dve.wait_ge(M_act[j], 3 * c + 1)
                    dve.tensor_tensor(XT[:, LO, j, :], M[j][:, :], XT[:, HI, j, :], ALU.subtract).then_inc(M_dve[j], 1)
                dve.wait_ge(M_act[0], 3 * c + 2)
                dve.tensor_tensor(DL[:, LO], M[0][:, :], DL[:, HI], ALU.subtract).then_inc(M_dve[0], 1)
                dve.wait_ge(M_act[1], 3 * c + 2)
                dve.tensor_tensor(BC[32:64, :], M[1][0:32, :], BC[0:32, :], ALU.subtract).then_inc(M_dve[1], 1)
                for j in range(KD):
                    dve.wait_ge(M_act[j], 3 * c + 3)
                    dve.tensor_scalar(rz[:, j, :], M[j][:, :], bias[:, j:j + 1], 0.0, ALU.add, ALU.max).then_inc(M_dve[j], 1)
                for j in range(KD):
                    dve.tensor_scalar(y[:, j, :], XF[:, j, :], skip[:, j:j + 1], None, ALU.mult)
                for j in range(KD):
                    dve.wait_ge(M_dve[j], 3 * c + 3)
                    dve.wait_ge(lz_full, 2 * c + j + 1)
                    dve.tensor_tensor(dt[:, j, :], rz[:, j, :], lz[:, j, :], ALU.add).then_inc(dt_full, 1)
                    dve.wait_ge(dt_full, 2 * c + j + 1)
                    dve.tensor_tensor(u[:, j, :], dt[:, j, :], XF[:, j, :], ALU.mult).then_inc(du_full, 1)
                for q in range(Q):
                    half, n = divmod(q, DSTATE)
                    if n == 0:
                        dve.wait_ge(du_full, 2 * c + half + 1)
                    dve.wait_ge(bb_full, c * Q + q + 1)
                    dve.wait_ge(state_full, step(c, q - 1))
                    dve.tensor_tensor(bx[:], BB[q % 2][:, :], u[:, half, :], ALU.mult).then_inc(bx_full, 1)
                    dve.wait_ge(decay_full, c * Q + q + 1)
                    dve.wait_ge(bx_full, step(c, q))
                    dve.wait_ge(cy_full, step(c, q - 1))
                    dve.tensor_tensor_scan(state[:], decay[q % 2][:].rearrange("p b l -> p (b l)"), bx[:], 0.0,
                                           ALU.mult, ALU.add).then_inc(state_full, 1)
                    dve.wait_ge(cb_full, c * Q + q + 1)
                    dve.wait_ge(state_full, step(c, q))
                    dve.wait_ge(y_sum, step(c, q - 2))
                    dve.tensor_tensor(cy[q % 2][:], CB[q % 2][:, :], state[:], ALU.mult).then_inc(cy_full, 1)
                dve.wait_ge(yt_full, c + 1)
                for t in range(0, CT4, 2):
                    done = dve.tensor_tensor(tokens(X, c, t, 2), YT[t // 2][:, :, :], tokens(X, c, t, 2), ALU.add)
                done.then_inc(x_sum, 1)

            dve.wait_ge(w_full, 1)
            with dve.Fori(0, NC) as c:
                chunk(c)

        @block.gpsimd
        def _(pool):
            pool.sem_inc(y_sum, 2)
            pool.memset(lneps[:], 1e-5)
            pool.memset(mhalf[:], -0.5).then_inc(var_full, 1)
            pool.wait_ge(var_full, 1)

            def chunk(c):
                pool.wait_ge(mv_full, c + 1)
                pool.tensor_tensor(rstd[:], mv[:, :, 1], lneps[:], ALU.add).then_inc(var_full, 1)
                pool.wait_ge(var_full, c + 2)
                pool.tensor_tensor(rstd[:], rstd[:], mhalf[:], ALU.pow).then_inc(rstd_full, 1)
                for q in range(Q):
                    half = q // DSTATE
                    pool.wait_ge(cy_full, step(c, q))
                    pool.wait_ge(y_sum, step(c, q - 1))
                    pool.tensor_tensor(y[:, half, :], y[:, half, :], cy[q % 2][:], ALU.add).then_inc(y_sum, 1)

            with pool.Fori(0, NC) as c:
                chunk(c)

        @block.tensor
        def _(pe):
            pe.wait_ge(w_full, 1)

            def spread(dst, c, q, row, free, full):
                pe.wait_ge(free, step(c, q - 2))
                pe.matmul(dst[:, :], SEL[:, row, :], BC[:, :], start=True, stop=True).then_inc(full, 1)

            def chunk(c):
                pe.wait_ge(xn_full, c + 1)
                for j in range(KD):
                    for t in range(CT4):
                        mm = pe.transpose(M[j][:, t * P:(t + 1) * P], xn[:, t, j * P:(j + 1) * P], ident[:])
                    mm.then_inc(M_full[j], 1)
                pe.wait_ge(M_dve[0], 3 * c + 1)
                pe.wait_ge(M_dve[1], 3 * c + 1)
                for m, rows in ((0, slice(0, DTRANK)), (1, slice(DTRANK, DTRANK + 2 * DSTATE))):
                    for j in range(KD):
                        mm = product(pe, M[m][0:rows.stop - rows.start, :], lambda a: W[:, a, j, rows], lambda a: XT[:, a, j, :],
                                     j == 0, j == KD - 1)
                    mm.then_inc(M_full[m], 1)
                pe.wait_ge(M_dve[0], 3 * c + 2)
                pe.wait_ge(M_dve[1], 3 * c + 2)
                for j in range(KD):
                    product(pe, M[j][:, :], lambda a: DTW[:, a, j * P:(j + 1) * P], lambda a: DL[:, a, :], True, True)\
                        .then_inc(M_full[j], 1)
                for q in range(Q):
                    n = q % DSTATE
                    spread(BB[q % 2], c, q, n, bx_full, bb_full)
                    spread(CB[q % 2], c, q, DSTATE + n, cy_full, cb_full)
                pe.wait_ge(y_sum, step(c, Q - 1))
                for t in range(CT4):
                    for j in range(KD):
                        mm = pe.transpose(YT[t // 2][:, t % 2, j * P:(j + 1) * P], y[:, j, t * P:(t + 1) * P], ident[:])
                mm.then_inc(yt_full, 1)

            with pe.Fori(0, NC) as c:
                chunk(c)


def self_attention(nc, X, x_kept, d):
    H = 16
    with ExitStack() as ctx:
        k = Kit(nc, ctx, "sa")
        sb, sem, sems = k.sb, k.sem, k.sems
        W = {n: sb(n, [P, 2, KD, H * HD], F32R) for n in ("WQ", "WK", "WV")}
        WO = sb("WO", [P, 2, H, DIM], F32R)
        ident, mask, ln1 = sb("ident", [P, P]), sb("mask", [P, P]), sb("ln1", [P, DIM])
        scrap, eps, mhalf, inv_dim = sb("scrap", [P, 1]), sb("eps", [P, 2, CT4]), sb("mhalf", [P, CT4]), sb("inv_dim", [P, CT4])
        stats, mv, rstd = sb("stats", [P, CT4, 6]), sb("mv", [P, CT4, 2]), sb("rstd", [P, CT4])
        sqs, msq, rr = sb("sqs", [P, DIM]), sb("msq", [P, CT4]), sb("rr", [P, CT4])
        xn = sb("xn", [P, CT4, DIM])
        HT = sb("HT", [P, 2, KD, CHUNK], F32R)
        QT, KT = ([sb(f"{n}{j}", [P, 2, CHUNK], F32R) for j in range(2)] for n in ("QT", "KT"))
        V = [sb(f"V{j}", [P, 2, CT4, 2 * HD], F32R) for j in range(2)]
        PRs = sb("PR", [P, 2, CT4, P])
        PR = [PRs[:, j] for j in range(2)]
        stage = [xn[:].rearrange("p a n -> p (a n)"), PRs[:].rearrange("p j a n -> p (j a n)")]
        nmax, rsum, rinv = sb("nmax", [P, CT4]), sb("rsum", [P, CT4]), sb("rinv", [P, CT4])
        PT, OT = sb("PT", [P, 2, CHUNK], F32R), sb("OT", [P, 2, CHUNK], F32R)
        out_t = xn[:].rearrange("p (k a) n -> p k (a n)", k=KD)
        J = [k.ps(f"J{j}", [P, CHUNK]) for j in range(2)]
        S = [k.ps(f"S{j}", [P, CT4, P]) for j in range(2)]
        T, PO = k.ps("T", [P, CHUNK]), k.ps("PO", [P, CHUNK])
        ACC = [k.ps(f"ACC{j}", [P, CHUNK]) for j in range(KD)]

        x_saved, tab_in, staged, w_hi, w_lo = sem("x_saved"), sem("tab_in"), sems("staged"), sem("w_hi"), sem("w_lo")
        stat_full, mv_full, var_full, rstd_full, h_full, msq_full, rr_full, xn_full = (
            sem(n) for n in ("stat_full", "mv_full", "var_full", "rstd_full", "h_full", "msq_full", "rr_full", "xn_full"))
        J_full, J_act, J_dve = sems("J_full"), sems("J_act"), sems("J_dve")
        T_full, T_act, T_dve = sem("T_full"), sem("T_act"), sem("T_dve")
        S_full, S_mask, nmax_full, exp_full, rinv_full, pr_full = (
            sem(n) for n in ("S_full", "S_mask", "nmax_full", "exp_full", "rinv_full", "pr_full"))
        pv_done, ot_hi, ot_full, wo_done = sem("pv_done"), sem("ot_hi"), sem("ot_full"), sem("wo_done")
        out_hi, x_sum = sem("out_hi"), sem("x_sum")

        pieces = []
        for n, w in (("WQ", "ffn_wq"), ("WK", "ffn_wk"), ("WV", "ffn_wv")):
            v = d[w].rearrange("(k p) n -> p k n", p=P)
            pieces += [(v[:, c, u * 1024:(u + 1) * 1024], lambda a, n=n, c=c, u=u: W[n][:, a, c, u * 1024:(u + 1) * 1024])
                       for c in range(KD) for u in range(2)]
        v = d["ffn_wo"].rearrange("(h p) n -> p h n", p=P)
        pieces += [(v[:, u * 4:(u + 1) * 4, :], lambda a, u=u: WO[:, a, u * 4:(u + 1) * 4, :]) for u in range(4)]

        def staging(j):
            view = stage[j % 2]
            return view.rearrange("p (a n) -> p a n", n=DIM) if len(pieces[j][0].shape) == 3 else view

        PER = 3 * H + KD

        def j_use(c, n):
            return n % 2, c * (PER // 2) + n // 2

        def slot_uses(c, h):
            n = 8 + 3 * h + (2 if h >= 14 else 0)
            return [j_use(c, n + u) for u in range(3)]

        def x_uses(c):
            return [j_use(c, 8 + 3 * 14 + u) for u in range(KD)]

        def qk_uses(c, h):
            return slot_uses(c, h)[0:2]

        def v_use(c, h):
            return slot_uses(c, h)[2], (h // 2 + 1) % (H // 2), 2 * (h % 2)

        def done(s):
            return s + 2

        STEP_SIGNALS = {"pe": (S_full, pv_done, wo_done), "dve": (S_mask, nmax_full, rinv_full, ot_full),
                        "act": (exp_full, ot_hi), "pool": (pr_full,)}

        def start(engine, name):
            for signal in STEP_SIGNALS[name]:
                engine.sem_inc(signal, 1)

        block = ctx.enter_context(nc.Block())

        @block.sync
        def _(sp):
            sp.dma_start(x_kept.rearrange("(t p) n -> p t n", p=P), X[:, :, :]).then_inc(x_saved, 16)
            for dst, src in ((ident, d["ident"]), (mask, d["smask"]), (ln1, d["ln1"].partition_broadcast(P))):
                sp.dma_start(dst[:], src).then_inc(tab_in, 16)
            for j, (src, _) in enumerate(pieces):
                if j >= 2:
                    sp.wait_ge(w_lo, j - 1)
                sp.dma_start(staging(j), src).then_inc(staged[j % 2], 16)

        @block.scalar
        def _(act):
            start(act, "act")

            def squares(c):
                act.wait_ge(h_full, c + 1)
                for t in range(CT4):
                    x = X[:, t, :] if isinstance(c, int) else tile_of(X, c, t)
                    act.activation(sqs[:], x, ACT.Square, accum_out=msq[:, t:t + 1]).then_inc(msq_full, 1)
                    if t < CT4 - 1:
                        act.wait_ge(msq_full, 4 * c + (t + 1))

            def x_split(uses):
                for j, (bank, n) in enumerate(uses):
                    act.wait_ge(J_full[bank], n + 1)
                    act.activation(HT[:, HI, j, :], J[bank][:, :], ACT.Copy).then_inc(J_act[bank], 1)

            def qk_split(use, u, par):
                bank, n = use
                act.wait_ge(J_full[bank], n + 1)
                act.activation((QT, KT)[u][par][:, HI], J[bank][:, :], ACT.Copy, scale=(HD ** -0.5, 1.0)[u]).then_inc(J_act[bank], 1)

            def v_split(v_use):
                (bank, n), pair, t = v_use
                act.wait_ge(J_full[bank], n + 1)
                act.activation(V[pair % 2][:, HI, t:t + 2, :], J[bank][:, :].rearrange("p (a n) -> p a n", a=2),
                               ACT.Copy).then_inc(J_act[bank], 1)

            def exps(s, par):
                act.wait_ge(nmax_full, done(s))
                for t in range(CT4):
                    last = act.activation(PR[par][:, t, :], S[par][:, t, :], ACT.Exp, bias=nmax[:, t:t + 1], accum_out=rsum[:, t:t + 1])
                last.then_inc(exp_full, 1)

            def slot(c, h, last):
                s, more = c * H + h, not (last and h >= 14)
                if h == 14 and more:
                    x_split(x_uses(c))
                act.wait_ge(T_full, c * (H + 1) + (h + 1))
                act.activation(PT[:, HI], T[:, :], ACT.Copy).then_inc(T_act, 1)
                if not (last and h == 15):
                    act.wait_ge(pv_done, s + 1)
                    exps(s + 1, (h + 1) % 2)
                if more:
                    act.wait_ge(S_full, done(s))
                    for u in range(2):
                        qk_split(qk_uses(c, h)[u], u, h % 2)
                act.wait_ge(pv_done, done(s))
                act.wait_ge(wo_done, s + 1)
                act.activation(OT[:, HI], PO[:, :], ACT.Copy).then_inc(ot_hi, 1)
                if more:
                    v_split(v_use(c, h))
                if h == 11 and not last:
                    squares(c + 1)

            def chunk(c, last=False):
                for h in range(H):
                    slot(c, h, last)
                act.wait_ge(wo_done, done(c * H + (H - 1)))
                for j in range(KD):
                    act.activation(out_t[:, j, :], ACC[j][:, :], ACT.Copy).then_inc(out_hi, 1)

            squares(0)
            for j, (_, dst) in enumerate(pieces):
                act.wait_ge(staged[j % 2], 16 * (j // 2 + 1))
                act.activation(dst(HI), staging(j), ACT.Copy).then_inc(w_hi, 1)
            x_split(x_uses(-1))
            for h in (14, 15):
                for u in range(2):
                    qk_split(qk_uses(-1, h)[u], u, h % 2)
                v_split(v_use(-1, h))
            exps(0, 0)
            with act.Fori(0, NC - 1) as c:
                chunk(c)
            chunk(NC - 1, last=True)

        @block.vector
        def _(dve):
            start(dve, "dve")

            def tile(buf, c, t):
                return buf[:, c * CT4 + t, :] if isinstance(c, int) else tile_of(buf, c, t)

            def norm_stats(c):
                for t in range(CT4):
                    last = dve.bn_stats(stats[:, t, :], tile(X, c, t))
                last.then_inc(stat_full, 1)

            def norm_var(c):
                dve.wait_ge(stat_full, c + 1)
                dve.memset(scrap[:], 0.0)
                for t in range(CT4):
                    last = dve.bn_aggr(mv[:, t, :], stats[:, t, :])
                last.then_inc(mv_full, 1)

            def norm_apply(c):
                dve.wait_ge(rstd_full, c + 1)
                dve.memset(scrap[:], 0.0)
                for t in range(CT4):
                    last = dve.tensor_scalar(tile(X, c, t), tile(X, c, t), mv[:, t, 0:1], rstd[:, t:t + 1], ALU.subtract, ALU.mult)
                last.then_inc(h_full, 1)

            def rms_apply(c):
                dve.wait_ge(rr_full, c + 1)
                dve.memset(scrap[:], 0.0)
                for t in range(CT4):
                    last = dve.scalar_tensor_tensor(xn[:, t, :], tile(X, c, t), rr[:, t:t + 1], ln1[:], ALU.mult, ALU.mult)
                last.then_inc(xn_full, 1)

            def x_split(uses):
                for j, (bank, n) in enumerate(uses):
                    dve.wait_ge(J_act[bank], n + 1)
                    dve.tensor_tensor(HT[:, LO, j, :], J[bank][:, :], HT[:, HI, j, :], ALU.subtract).then_inc(J_dve[bank], 1)

            def qk_split(uses, par, first=0):
                for u, (bank, n) in enumerate(uses, first):
                    buf = (QT, KT)[u][par]
                    dve.wait_ge(J_act[bank], n + 1)
                    dve.scalar_tensor_tensor(buf[:, LO], J[bank][:, :], (HD ** -0.5, 1.0)[u], buf[:, HI],
                                             ALU.mult, ALU.subtract).then_inc(J_dve[bank], 1)

            def v_split(v_use):
                (bank, n), pair, t = v_use
                dve.wait_ge(J_act[bank], n + 1)
                dve.tensor_tensor(V[pair % 2][:, LO, t:t + 2, :], J[bank][:, :].rearrange("p (a n) -> p a n", a=2),
                                  V[pair % 2][:, HI, t:t + 2, :], ALU.subtract).then_inc(J_dve[bank], 1)

            def maxima(s, par):
                dve.wait_ge(S_full, done(s))
                dve.tensor_tensor(S[par][:, :, :], S[par][:, :, :], mask[:, None, :].broadcast_to([P, CT4, P]),
                                  ALU.add).then_inc(S_mask, 1)
                dve.wait_ge(S_mask, done(s))
                dve.tensor_reduce(nmax[:], S[par][:, :, :], AX.X, ALU.max, negate=True).then_inc(nmax_full, 1)

            def inverse(s):
                dve.wait_ge(exp_full, done(s))
                dve.wait_ge(pr_full, s + 1)
                dve.reciprocal(rinv[:], rsum[:]).then_inc(rinv_full, 1)

            def slot(c, h, last):
                s, more = c * H + h, not (last and h >= 14)
                if not (last and h == 15):
                    maxima(s + 1, (h + 1) % 2)
                if h == 14 and more:
                    x_split(x_uses(c))
                dve.wait_ge(T_act, s + 1)
                dve.tensor_tensor(PT[:, LO], T[:, :], PT[:, HI], ALU.subtract).then_inc(T_dve, 1)
                if more:
                    qk_split(qk_uses(c, h)[0:1], h % 2)
                if not (last and h == 15):
                    inverse(s + 1)
                if more:
                    qk_split(qk_uses(c, h)[1:2], h % 2, 1)
                dve.wait_ge(ot_hi, done(s))
                dve.tensor_tensor(OT[:, LO], PO[:, :], OT[:, HI], ALU.subtract).then_inc(ot_full, 1)
                if more:
                    v_split(v_use(c, h))
                if not last:
                    for at, stage_of in ((8, norm_stats), (9, norm_var), (10, norm_apply), (12, rms_apply)):
                        if h == at:
                            stage_of(c + 1)

            def chunk(c, last=False):
                for h in range(H):
                    slot(c, h, last)
                dve.wait_ge(T_full, (c + 1) * (H + 1))
                for u, bank in ((0, T), (1, PO)):
                    x = X[:, c * CT4 + 2 * u:c * CT4 + 2 * u + 2, :] if last else tokens(X, c, 2 * u, 2)
                    dve.tensor_tensor(x, bank[:, :].rearrange("p (a n) -> p a n", a=2), x, ALU.add).then_inc(x_sum, 1)

            norm_stats(0)
            norm_var(0)
            dve.wait_ge(x_saved, 16)
            norm_apply(0)
            for j, (_, dst) in enumerate(pieces):
                dve.wait_ge(w_hi, j + 1)
                dve.tensor_tensor(dst(LO), staging(j), dst(HI), ALU.subtract).then_inc(w_lo, 1)
            dve.wait_ge(tab_in, 3 * 16)
            dve.wait_ge(w_lo, len(pieces))
            rms_apply(0)
            x_split(x_uses(-1))
            for h in (14, 15):
                qk_split(qk_uses(-1, h), h % 2)
                v_split(v_use(-1, h))
            maxima(0, 0)
            dve.wait_ge(exp_full, done(0))
            dve.reciprocal(rinv[:], rsum[:]).then_inc(rinv_full, 1)
            with dve.Fori(0, NC - 1) as c:
                chunk(c)
            chunk(NC - 1, last=True)

        @block.gpsimd
        def _(pool):
            start(pool, "pool")
            pool.memset(inv_dim[:], 1.0 / DIM)
            pool.memset(eps[:, 0, :], 1e-5)
            pool.memset(eps[:, 1, :], 1e-6)
            pool.memset(mhalf[:], -0.5).then_inc(var_full, 1)
            pool.wait_ge(var_full, 1)

            def ln_rstd(c):
                pool.wait_ge(mv_full, c + 1)
                pool.tensor_tensor(rstd[:], mv[:, :, 1], eps[:, 0, :], ALU.add).then_inc(var_full, 1)
                pool.wait_ge(var_full, 3 * c + 2)
                pool.tensor_tensor(rstd[:], rstd[:], mhalf[:], ALU.pow).then_inc(rstd_full, 1)

            def rms_rstd(c):
                pool.wait_ge(msq_full, 4 * c + 4)
                pool.tensor_tensor(rr[:], msq[:], inv_dim[:], ALU.mult).then_inc(var_full, 1)
                pool.wait_ge(var_full, 3 * c + 3)
                pool.tensor_tensor(rr[:], rr[:], eps[:, 1, :], ALU.add).then_inc(var_full, 1)
                pool.wait_ge(var_full, 3 * c + 4)
                pool.tensor_tensor(rr[:], rr[:], mhalf[:], ALU.pow).then_inc(rr_full, 1)

            def normalise(s, par):
                pool.wait_ge(rinv_full, done(s))
                pool.tensor_tensor(PR[par][:], PR[par][:], rinv[:, :, None].broadcast_to([P, CT4, P]), ALU.mult).then_inc(pr_full, 1)

            def chunk(c, last=False):
                for h in range(H):
                    if not (last and h == 15):
                        normalise(c * H + (h + 1), (h + 1) % 2)
                    if h == 9 and not last:
                        ln_rstd(c + 1)
                    if h == 11 and not last:
                        rms_rstd(c + 1)

            ln_rstd(0)
            rms_rstd(0)
            normalise(0, 0)
            with pool.Fori(0, NC - 1) as c:
                chunk(c)
            chunk(NC - 1, last=True)

        @block.tensor
        def _(pe):
            start(pe, "pe")

            def x_turn(uses, c):
                pe.wait_ge(xn_full, c + 1)
                for j, (bank, n) in enumerate(uses):
                    pe.wait_ge(J_dve[bank], n)
                    for t in range(CT4):
                        mm = pe.transpose(J[bank][:, t * P:(t + 1) * P], xn[:, t, j * P:(j + 1) * P], ident[:])
                    mm.then_inc(J_full[bank], 1)

            def qk_project(uses, h):
                for u, (bank, n) in enumerate(uses):
                    pe.wait_ge(J_dve[bank], n)
                    w = W[("WQ", "WK")[u]]
                    for j in range(KD):
                        mm = product(pe, J[bank][:, :], lambda a: w[:, a, j, h * HD:(h + 1) * HD], lambda a: HT[:, a, j, :],
                                     j == 0, j == KD - 1)
                    mm.then_inc(J_full[bank], 1)

            def v_project(v_use):
                (bank, n), pair, t = v_use
                pe.wait_ge(J_dve[bank], n)
                for u in range(2):
                    at = slice((t + u) * P, (t + u + 1) * P)
                    for j in range(KD):
                        mm = product(pe, J[bank][:, u * 2 * HD:(u + 1) * 2 * HD], lambda a: HT[:, a, j, at],
                                     lambda a: W["WV"][:, a, j, pair * 2 * HD:(pair + 1) * 2 * HD], j == 0, j == KD - 1)
                mm.then_inc(J_full[bank], 1)

            def scores(uses, s, par):
                for bank, n in uses:
                    pe.wait_ge(J_dve[bank], n + 1)
                for t in range(CT4):
                    mm = product(pe, S[par][:, t, :], lambda a: QT[par][:, a, t * P:(t + 1) * P],
                                 lambda a: KT[par][:, a, t * P:(t + 1) * P], True, True)
                mm.then_inc(S_full, 1)

            def slot(c, h, last):
                s, par, more = c * H + h, h % 2, not (last and h >= 14)
                if not (last and h == 15):
                    scores(qk_uses(c, h - 1), s + 1, 1 - par)
                if h == 14 and more:
                    x_turn(x_uses(c), c + 1)
                pe.wait_ge(pr_full, done(s))
                for t in range(CT4):
                    mm = pe.transpose(T[:, t * P:(t + 1) * P], PR[par][:, t, :], ident[:])
                mm.then_inc(T_full, 1)
                if h == 14 and more:
                    for bank, n in x_uses(c):
                        pe.wait_ge(J_dve[bank], n + 1)
                if more:
                    qk_project(qk_uses(c, h), (h + 2) % H)
                pe.wait_ge(T_dve, s + 1)
                pe.wait_ge(ot_full, s + 1)
                for t in range(CT4):
                    mm = product(pe, PO[:, t * P:(t + 1) * P], lambda a: V[h // 2 % 2][:, a, t, h % 2 * HD:(h % 2 + 1) * HD],
                                 lambda a: PT[:, a, t * P:(t + 1) * P], True, True)
                mm.then_inc(pv_done, 1)
                if more:
                    v_project(v_use(c, h))
                pe.wait_ge(ot_full, done(s))
                for j in range(KD):
                    mm = product(pe, ACC[j][:, :], lambda a: WO[:, a, h, j * P:(j + 1) * P], lambda a: OT[:, a, :], h == 0, h == H - 1)
                mm.then_inc(wo_done, 1)

            def chunk(c, last=False):
                for h in range(H):
                    slot(c, h, last)
                pe.wait_ge(out_hi, 2 * c + 2)
                for t in range(CT4):
                    for j in range(KD):
                        mm = pe.transpose((T, PO)[t // 2][:, (t % 2) * DIM + j * P:(t % 2) * DIM + (j + 1) * P],
                                          out_t[:, j, t * P:(t + 1) * P], ident[:])
                mm.then_inc(T_full, 1)
                pe.wait_ge(x_sum, 2 * c + 2)

            pe.wait_ge(tab_in, 3 * 16)
            x_turn(x_uses(-1), 0)
            pe.wait_ge(w_lo, len(pieces))
            for bank, n in x_uses(-1):
                pe.wait_ge(J_dve[bank], n + 1)
            for h in (14, 15):
                qk_project(qk_uses(-1, h), h - 14)
                v_project(v_use(-1, h))
            scores(qk_uses(-1, 14), 0, 0)
            with pe.Fori(0, NC - 1) as c:
                chunk(c)
            chunk(NC - 1, last=True)


EXPERTS, TOPK, INNER, SHARED = 16, 6, 176, 352
ROWS = EXPERTS * INNER
NE = (ROWS + SHARED + P - 1) // P


def mixture_of_experts(nc, x_kept, x2_kept, d, out):
    with ExitStack() as ctx:
        k = Kit(nc, ctx, "me")
        sb, sem, sems = k.sb, k.sem, k.sems
        WG, WU = (sb(n, [P, 2, KD, NE * P], F32R) for n in ("WG", "WU"))
        WD = sb("WD", [P, 2, NE, DIM], F32R)
        gate_raw, WR = sb("gate_raw", [P, KD, EXPERTS]), sb("WR", [P, 2, KD, EXPERTS], F32R)
        SEL = sb("SEL", [64, NE, P], F32R)
        ident, ln2, tri = sb("ident", [P, P]), sb("ln2", [P, DIM]), sb("tri", [P, EXPERTS * EXPERTS])
        eps, mhalf, inv_dim = (sb(n, [P, CT4]) for n in ("eps", "mhalf", "inv_dim"))
        x2, xk, xs, xn = (sb(n, [P, CT4, DIM]) for n in ("x2", "xk", "xs", "xn"))
        msq, rr = sb("msq", [P, CT4]), sb("rr", [P, CT4])
        HT = sb("HT", [P, 2, KD, CHUNK], F32R)
        top, total, inv = sb("top", [P, CT4]), sb("total", [P, CT4]), sb("inv", [P, CT4])
        prob, pick, rank, ties = (sb(n, [P, CT4, EXPERTS]) for n in ("prob", "pick", "rank", "ties"))
        cw = sb("cw", [P, CT4, 32])
        CWS = sb("CWS", [64, CHUNK], F32R)
        sg, hu, hw = (sb(n, [P, CHUNK]) for n in ("sg", "hu", "hw"))
        HH = [sb(f"HH{j}", [P, 2, CHUNK], F32R) for j in range(2)]
        stage = [b[:].rearrange("p a n -> p (a n)") for b in (xn, xs)]
        beats = xn[:].rearrange("p a (e f) -> p a e f", f=EXPERTS)
        out_t = xn[:].rearrange("p (k a) n -> p k (a n)", k=KD)
        G, U, C = ([k.ps(f"{n}{j}", [P, CHUNK]) for j in range(2)] for n in "GUC")
        ACC = [k.ps(f"ACC{j}", [P, CHUNK]) for j in range(KD)]

        tab_in, sel_in, staged, w_hi, w_lo = sem("tab_in"), sem("sel_in"), sems("staged"), sem("w_hi"), sem("w_lo")
        x2_in, xk_in, xs_full, res_full, stored = (sem(n) for n in ("x2_in", "xk_in", "xs_full", "res_full", "stored"))
        var_full, msq_full, rr_full, xn_full = (sem(n) for n in ("var_full", "msq_full", "rr_full", "xn_full"))
        full = {r: sems(f"{r}_full") for r in "GUC"}
        x_hi, x_lo = sem("x_hi"), sem("x_lo")
        sg_full, hu_full, hw_full, hh_hi, hh_full, down_done = (
            sem(n) for n in ("sg_full", "hu_full", "hw_full", "hh_hi", "hh_full", "down_done"))
        top_full, prob_full, router, cws_hi, cws_full = (
            sem(n) for n in ("top_full", "prob_full", "router", "cws_hi", "cws_full"))
        out_hi, back_full, cw_set = sem("out_hi"), sem("back_full"), sem("cw_set")
        LINKS = 12

        pieces = []
        for n, W, first in (("wg", WG, 0), ("wu", WU, 0)):
            v = d[n].rearrange("(k p) n -> p k n", p=P)
            pieces += [(v[:, c, u * 800:(u + 1) * 800], lambda a, W=W, c=c, u=u: W[:, a, c, u * 800:(u + 1) * 800])
                       for c in range(KD) for u in range(4)]
        v = d["wd"].rearrange("(e p) n -> p e n", p=P)
        pieces += [(v[:, u:min(u + 4, NE), :], lambda a, u=u: WD[:, a, u:min(u + 4, NE), :]) for u in range(0, NE, 4)]

        def staging(j):
            src = pieces[j][0]
            n = int(np.prod(src.shape[1:]))
            view = stage[j % 2][:, 0:n]
            return view.rearrange("p (a n) -> p a n", n=DIM) if len(src.shape) == 3 else view

        plan = {r: [] for r in "GUC"}
        for e in [23, 24] + list(range(23)):
            if e == 23:
                plan["G"] += ["x", "logits"]
                plan["U"] += ["x"]
            for r in "GUC":
                plan[r] += [(e + 2) % NE]
            if e == 23:
                plan["G"] += ["cw"]
        where = {}
        for r, names in plan.items():
            for n, name in enumerate(names):
                where[r, name] = (n % 2, sum(1 for m in range(n) if m % 2 == n % 2))
        uses_of = {r: [len(plan[r][b::2]) for b in range(2)] for r in "GUC"}

        def use(r, name, c):
            bank, n = where[r, name]
            return bank, c * uses_of[r][bank] + n

        def done(s):
            return s + 2

        def freed(r, name, c):
            if name == "x":
                return x_lo, 2 * c + {"G": 1, "U": 2}[r]
            if name in ("logits", "cw"):
                return {"logits": prob_full, "cw": cws_full}[name], c + 1
            return {"G": sg_full, "U": hu_full, "C": hw_full}[r], done(c * NE + name)

        def free(pe, r, name, c):
            at = plan[r].index(name)
            if at >= 2:
                pe.wait_ge(*freed(r, plan[r][at - 2], c))
            elif not (isinstance(c, int) and c == 0):
                bank = at % 2
                pe.wait_ge(*freed(r, plan[r][bank::2][-1], c - 1))
            return where[r, name][0]

        def after(c, e):
            return (c + 1, e - NE) if e >= NE else (c, e)

        block = ctx.enter_context(nc.Block())

        @block.sync
        def _(sp):
            kept = [b.rearrange("(c t p) n -> p c t n", p=P, t=CT4) for b in (x2_kept, x_kept, out)]

            def rows(b, c):
                return kept[b][:, bass.ds(c, 1), :, :].rearrange("p c t n -> p (c t) n")

            sp.dma_start(x2[:], rows(0, 0)).then_inc(x2_in, 16)
            sp.dma_start(xk[:], rows(1, 0)).then_inc(xk_in, 16)
            for dst, src in ((ident, d["ident"]), (ln2, d["ln2"].partition_broadcast(P)), (tri, d["tri"].partition_broadcast(P)),
                             (gate_raw, d["wr"].rearrange("(k p) n -> p k n", p=P))):
                sp.dma_start(dst[:], src).then_inc(tab_in, 16)
            for j, (src, _) in enumerate(pieces):
                if j >= 2:
                    sp.wait_ge(w_lo, j - 1)
                sp.dma_start(staging(j), src).then_inc(staged[j % 2], 16)
            with sp.Fori(0, NC - 1) as c:
                sp.wait_ge(xs_full, c + 1)
                sp.dma_start(x2[:], rows(0, c + 1)).then_inc(x2_in, 16)
                sp.dma_start(xk[:], rows(1, c + 1)).then_inc(xk_in, 16)
                sp.wait_ge(res_full, 2 * c + 4)
                sp.dma_start(rows(2, c), xs[:]).then_inc(stored, 16)
            sp.wait_ge(res_full, 2 * NC + 2)
            sp.dma_start(rows(2, NC - 1), xs[:]).then_inc(stored, 16)
            sp.wait_ge(stored, 16 * NC + 16)

        @block.scalar
        def _(act):
            act.sem_inc(sg_full, 1)
            act.sem_inc(hh_hi, 1)

            def squares(c, squared):
                act.wait_ge(x2_in, 16 * c + 16)
                for t in range(CT4):
                    act.activation(squared, x2[:, t, :], ACT.Square, accum_out=msq[:, t:t + 1]).then_inc(msq_full, 1)
                    act.wait_ge(msq_full, 4 * c + (t + 1))

            def x_split(c):
                for j, (r, B) in enumerate((("G", G), ("U", U))):
                    bank, n = use(r, "x", c)
                    act.wait_ge(full[r][bank], n + 1)
                    act.activation(HT[:, HI, j, :], B[bank][:, :], ACT.Copy).then_inc(x_hi, 1)

            def route(c):
                bank, n = use("G", "logits", c)
                act.wait_ge(top_full, c + 1)
                for t in range(CT4):
                    last = act.activation(prob[:, t, :], G[bank][:, t * EXPERTS:(t + 1) * EXPERTS], ACT.Exp, bias=top[:, t:t + 1],
                                          accum_out=total[:, t:t + 1])
                last.then_inc(prob_full, 1)

            def cw_split(c):
                bank, n = use("G", "cw", c)
                act.wait_ge(full["G"][bank], n + 1)
                act.activation(CWS[0:32, :], G[bank][0:32, :], ACT.Copy).then_inc(cws_hi, 1)

            def gate(c, e):
                bank, n = use("G", e, c)
                act.wait_ge(full["G"][bank], n + 1)
                act.wait_ge(hu_full, done(c * NE + (e - 1)))
                act.activation(sg[:], G[bank][:, :], ACT.Silu).then_inc(sg_full, 1)

            def high(c, e):
                act.wait_ge(down_done, done(c * NE + (e - 1 if e == 0 else e - 2)))
                act.wait_ge(hw_full, done(c * NE + e))
                act.activation(HH[e % 2][:, HI], hw[:], ACT.Copy).then_inc(hh_hi, 1)

            def chunk(c, last=False):
                for e in range(NE):
                    if not (last and e == NE - 1):
                        gate(*after(c, e + 1))
                        high(*after(c, e + 1))
                    if e == 23 and not last:
                        x_split(c + 1)
                        route(c + 1)
                        cw_split(c + 1)
                    if e == 10 and not last:
                        act.wait_ge(back_full, c + 1)
                        squares(c + 1, xn[:, 0, :])
                act.wait_ge(down_done, done(c * NE + (NE - 1)))
                for j in range(KD):
                    act.activation(out_t[:, j, :], ACC[j][:, :], ACT.Copy).then_inc(out_hi, 1)

            squares(0, hu[:, 0:DIM])
            for j, (_, dst) in enumerate(pieces):
                act.wait_ge(staged[j % 2], 16 * (j // 2 + 1))
                act.activation(dst(HI), staging(j), ACT.Copy).then_inc(w_hi, 1)
            act.wait_ge(tab_in, 4 * 16)
            act.activation(WR[:, HI], gate_raw[:], ACT.Copy).then_inc(w_hi, 1)
            x_split(0)
            route(0)
            cw_split(0)
            gate(0, 0)
            high(0, 0)
            with act.Fori(0, NC - 1) as c:
                chunk(c)
            chunk(NC - 1, last=True)

        @block.vector
        def _(dve):
            dve.sem_inc(hu_full, 1)
            dve.sem_inc(hw_full, 1)
            dve.sem_inc(res_full, 2)

            def rms_apply(c):
                dve.wait_ge(rr_full, c + 1)
                for t in range(CT4):
                    last = dve.scalar_tensor_tensor(xn[:, t, :], x2[:, t, :], rr[:, t:t + 1], ln2[:], ALU.mult, ALU.mult)
                last.then_inc(xn_full, 1)

            def x_split(c):
                for j, (r, B) in enumerate((("G", G), ("U", U))):
                    dve.wait_ge(x_hi, 2 * c + (j + 1))
                    dve.tensor_tensor(HT[:, LO, j, :], B[where[r, "x"][0]][:, :], HT[:, HI, j, :], ALU.subtract).then_inc(x_lo, 1)

            def top_logit(c):
                bank, n = use("G", "logits", c)
                dve.wait_ge(full["G"][bank], n + 1)
                dve.tensor_reduce(top[:], G[bank][:, 0:CT4 * EXPERTS].rearrange("p (t e) -> p t e", t=CT4), AX.X, ALU.max,
                                  negate=True).then_inc(top_full, 1)

            def route(c):
                link = iter(range(1, LINKS + 1))

                def chain(ins):
                    ins.then_inc(router, 1)
                    dve.wait_ge(router, LINKS * c + next(link))

                four = [P, CT4, EXPERTS, EXPERTS]
                other, own = prob[:, :, None, :].broadcast_to(four), prob[:, :, :, None].broadcast_to(four)
                dve.wait_ge(prob_full, c + 1)
                chain(dve.reciprocal(inv[:], total[:]))
                chain(dve.tensor_tensor(prob[:], prob[:], inv[:, :, None].broadcast_to(four[:3]), ALU.mult))
                chain(dve.tensor_tensor(beats, other, own, ALU.is_gt))
                chain(dve.tensor_reduce(rank[:], beats, AX.X, ALU.add))
                chain(dve.tensor_tensor(beats, other, own, ALU.is_equal))
                chain(dve.tensor_tensor(beats, beats, tri[:, None, :].broadcast_to([P, CT4, EXPERTS * EXPERTS])
                                        .rearrange("p t (e f) -> p t e f", f=EXPERTS), ALU.mult))
                chain(dve.tensor_reduce(ties[:], beats, AX.X, ALU.add))
                chain(dve.tensor_tensor(rank[:], rank[:], ties[:], ALU.add))
                chain(dve.scalar_tensor_tensor(pick[:], rank[:], float(TOPK), prob[:], ALU.is_lt, ALU.mult))
                chain(dve.tensor_reduce(total[:], pick[:], AX.X, ALU.add))
                chain(dve.reciprocal(inv[:], total[:]))
                chain(dve.tensor_tensor(cw[:, :, 0:EXPERTS], pick[:], inv[:, :, None].broadcast_to(four[:3]), ALU.mult))

            def cw_split(c):
                dve.wait_ge(cws_hi, c + 1)
                dve.tensor_tensor(CWS[32:64, :], G[where["G", "cw"][0]][0:32, :], CWS[0:32, :], ALU.subtract).then_inc(cws_full, 1)

            def scale(c, e):
                s = c * NE + e
                (bu, nu), (bc, n_c) = use("U", e, c), use("C", e, c)
                dve.wait_ge(full["U"][bu], nu + 1)
                dve.wait_ge(hw_full, done(c * NE + (e - 1)))
                dve.wait_ge(sg_full, done(s))
                dve.tensor_tensor(hu[:], U[bu][:, :], sg[:], ALU.mult).then_inc(hu_full, 1)
                dve.wait_ge(full["C"][bc], n_c + 1)
                dve.wait_ge(hh_full, done(c * NE + (e - 1)))
                dve.wait_ge(hu_full, done(s))
                dve.tensor_tensor(hw[:], C[bc][:, :], hu[:], ALU.mult).then_inc(hw_full, 1)

            def chunk(c, last=False):
                for e in range(NE):
                    if not (last and e == NE - 1):
                        scale(*after(c, e + 1))
                    if e == 23 and not last:
                        x_split(c + 1)
                        top_logit(c + 1)
                        route(c + 1)
                        cw_split(c + 1)
                    if e == 13 and not last:
                        rms_apply(c + 1)
                dve.wait_ge(back_full, c + 2)
                dve.wait_ge(xs_full, c + 1)
                for u in range(2):
                    rows = xs[:, 2 * u:2 * u + 2, :]
                    dve.tensor_tensor(rows, ACC[u][:, :].rearrange("p (a n) -> p a n", a=2), rows, ALU.add).then_inc(res_full, 1)

            for j, (_, dst) in enumerate(pieces):
                dve.wait_ge(w_hi, j + 1)
                dve.tensor_tensor(dst(LO), staging(j), dst(HI), ALU.subtract).then_inc(w_lo, 1)
            dve.wait_ge(w_hi, len(pieces) + 1)
            dve.tensor_tensor(WR[:, LO], gate_raw[:], WR[:, HI], ALU.subtract).then_inc(w_lo, 1)
            dve.wait_ge(w_lo, len(pieces) + 1)
            dve.wait_ge(cw_set, 2)
            rms_apply(0)
            x_split(0)
            top_logit(0)
            route(0)
            cw_split(0)
            scale(0, 0)
            with dve.Fori(0, NC - 1) as c:
                chunk(c)
            chunk(NC - 1, last=True)

        @block.gpsimd
        def _(pool):
            pool.dma_start(SEL[:], d["sel_e"]).then_inc(sel_in, 16)
            pool.sem_inc(hh_full, 1)
            pool.sem_inc(stored, 16)
            pool.memset(inv_dim[:], 1.0 / DIM)
            pool.memset(eps[:], 1e-6)
            pool.memset(mhalf[:], -0.5)
            pool.memset(cw[:], 0.0).then_inc(cw_set, 1)
            pool.wait_ge(cw_set, 1)
            pool.memset(cw[:, :, EXPERTS:EXPERTS + 1], 1.0).then_inc(cw_set, 1)

            def rms_rstd(c):
                pool.wait_ge(msq_full, 4 * c + 4)
                pool.tensor_tensor(rr[:], msq[:], inv_dim[:], ALU.mult).then_inc(var_full, 1)
                pool.wait_ge(var_full, 2 * c + 1)
                pool.tensor_tensor(rr[:], rr[:], eps[:], ALU.add).then_inc(var_full, 1)
                pool.wait_ge(var_full, 2 * c + 2)
                pool.tensor_tensor(rr[:], rr[:], mhalf[:], ALU.pow).then_inc(rr_full, 1)

            def low(c, e):
                pool.wait_ge(hh_hi, done(c * NE + e))
                pool.tensor_tensor(HH[e % 2][:, LO], hw[:], HH[e % 2][:, HI], ALU.subtract).then_inc(hh_full, 1)

            def chunk(c, last=False):
                for e in range(NE):
                    if not (last and e == NE - 1):
                        low(*after(c, e + 1))
                    if e == 3:
                        pool.wait_ge(x2_in, 16 * c + 16)
                        pool.wait_ge(xk_in, 16 * c + 16)
                        pool.wait_ge(stored, 16 * c + 16)
                        pool.tensor_tensor(xs[:], x2[:], xk[:], ALU.add).then_inc(xs_full, 1)
                    if e == 11 and not last:
                        rms_rstd(c + 1)

            rms_rstd(0)
            low(0, 0)
            with pool.Fori(0, NC - 1) as c:
                chunk(c)
            chunk(NC - 1, last=True)

        @block.tensor
        def _(pe):
            pe.sem_inc(down_done, 1)
            pe.sem_inc(back_full, 1)

            def x_turn(c):
                pe.wait_ge(xn_full, c + 1)
                for j, (r, B) in enumerate((("G", G), ("U", U))):
                    bank = free(pe, r, "x", c)
                    for t in range(CT4):
                        mm = pe.transpose(B[bank][:, t * P:(t + 1) * P], xn[:, t, j * P:(j + 1) * P], ident[:])
                    mm.then_inc(full[r][bank], 1)
                bank = free(pe, "G", "logits", c)
                pe.wait_ge(x_lo, 2 * c + 2)
                for t in range(CT4):
                    for j in range(KD):
                        mm = product(pe, G[bank][:, t * EXPERTS:(t + 1) * EXPERTS], lambda a: HT[:, a, j, t * P:(t + 1) * P],
                                     lambda a: WR[:, a, j, :], j == 0, j == KD - 1)
                mm.then_inc(full["G"][bank], 1)

            def gates(c, e):
                for r, B, W in (("G", G, WG), ("U", U, WU)):
                    bank = free(pe, r, e, c)
                    for j in range(KD):
                        mm = product(pe, B[bank][:, :], lambda a: W[:, a, j, e * P:(e + 1) * P], lambda a: HT[:, a, j, :],
                                     j == 0, j == KD - 1)
                    mm.then_inc(full[r][bank], 1)

            def cw_turn(c):
                bank = free(pe, "G", "cw", c)
                pe.wait_ge(router, LINKS * c + LINKS)
                for t in range(CT4):
                    mm = pe.transpose(G[bank][0:32, t * P:(t + 1) * P], cw[:, t, :], ident[:])
                mm.then_inc(full["G"][bank], 1)

            def spread(c, e):
                if e == 0:
                    pe.wait_ge(cws_full, c + 1)
                bank = free(pe, "C", e, c)
                pe.matmul(C[bank][:, :], SEL[:, e, :], CWS[:, :], start=True, stop=True).then_inc(full["C"][bank], 1)

            def down(c, e):
                s = c * NE + e
                pe.wait_ge(hh_full, done(s))
                if e == 0:
                    pe.wait_ge(res_full, 2 * c + 2)
                for j in range(KD):
                    mm = product(pe, ACC[j][:, :], lambda a: WD[:, a, e, j * P:(j + 1) * P], lambda a: HH[e % 2][:, a, :],
                                 e == 0, e == NE - 1)
                mm.then_inc(down_done, 1)

            def chunk(c, last=False):
                for e in range(NE):
                    more = not (last and e >= 23)
                    if more:
                        if e == 23:
                            x_turn(c + 1)
                        gates(*after(c, e + 2))
                    if e == 23:
                        down(c, e)
                    if more:
                        if e == 23:
                            cw_turn(c + 1)
                        spread(*after(c, e + 2))
                    if e != 23:
                        down(c, e)
                pe.wait_ge(out_hi, 2 * c + 2)
                for t in range(CT4):
                    for j in range(KD):
                        mm = pe.transpose(ACC[t // 2][:, (t % 2) * DIM + j * P:(t % 2) * DIM + (j + 1) * P],
                                          out_t[:, j, t * P:(t + 1) * P], ident[:])
                mm.then_inc(back_full, 1)

            pe.wait_ge(tab_in, 4 * 16)
            pe.wait_ge(sel_in, 16)
            pe.wait_ge(w_lo, len(pieces) + 1)
            x_turn(0)
            gates(0, 0)
            cw_turn(0)
            spread(0, 0)
            gates(0, 1)
            spread(0, 1)
            with pe.Fori(0, NC - 1) as c:
                chunk(c)
            chunk(NC - 1, last=True)


def store_tokens(nc, X, out):
    with ExitStack() as ctx:
        stored = ctx.enter_context(nc.semaphore("stored"))
        block = ctx.enter_context(nc.Block())

        @block.sync
        def _(sp):
            sp.dma_start(out.rearrange("(t p) n -> p t n", p=P), X[:, :, :]).then_inc(stored, 16)
            sp.wait_ge(stored, 16)


def rope_tables():
    inv = (1.0 / np.float32(10000.0) ** (np.arange(0, HD, 2, dtype=np.float32) / np.float32(HD))).astype(np.float32)
    angle = np.outer(np.arange(LEN, dtype=np.float32), inv).astype(np.float32)
    cos, sin = np.cos(angle), np.sin(angle)
    return (np.tile(np.concatenate([cos, cos], 1), (2, 1)).astype(np.float32),
            np.tile(np.concatenate([-sin, sin], 1), (2, 1)).astype(np.float32))


def selectors():
    unit = np.arange(NE * P).reshape(1, NE, P)
    return ((np.arange(64) % 32)[:, None, None] == np.minimum(unit // INNER, EXPERTS)).astype(np.float32)


def constants():
    cos, sin = rope_tables()
    q, key = np.arange(P)[:, None], np.arange(P)[None, :]
    return {
        "ident": np.eye(P, dtype=np.float32), "cos": cos, "sin": sin,
        "sel_bc": np.stack([np.where(np.arange(64)[:, None] % 32 == r, np.float32(1), np.float32(0)).repeat(P, 1)
                            for r in range(2 * DSTATE)], 1),
        "smask": np.where((key > q) | (key // LEN != q // LEN), np.float32(NEG), np.float32(0)),
        "tri": (np.arange(EXPERTS)[None, :] < np.arange(EXPERTS)[:, None]).astype(np.float32).reshape(-1),
        "sel_e": selectors(),
        "xmask": np.where(np.arange(LEN)[None, :] > q % LEN, np.float32(NEG), np.float32(0)),
    }


def layouts(a):
    def kv(wk, wv):
        both = np.stack([wk.reshape(KD, P, NG, HD), wv.reshape(KD, P, NG, HD)], axis=3)
        return both.transpose(1, 0, 2, 3, 4).reshape(P, -1)

    def units(routed, shared):
        return np.concatenate([routed.reshape(ROWS, DIM), shared, np.zeros((NE * P - ROWS - SHARED, DIM), np.float32)])

    return {
        "wg": units(a["L0_ffn_eg_w"], a["L0_ffn_sg_w"]).T, "wu": units(a["L0_ffn_eu_w"], a["L0_ffn_su_w"]).T,
        "wd": units(a["L0_ffn_ed_w"].transpose(0, 2, 1), a["L0_ffn_sd_w"].T), "wr": a["L0_ffn_gate_w"].T,
        "x": a["x"].reshape(BATCH * LEN, DIM),
        "ctxT": a["ctx_2048"].reshape(NT, 2 * CTX, KD, P).transpose(0, 3, 2, 1),
        "wq": a["L0_xattn_wq"], "wo": a["L0_xattn_wo"],
        "wkv": kv(a["L0_xattn_wk"], a["L0_xattn_wv"]), "wkvc": kv(a["L0_xattn_wk_ctx"], a["L0_xattn_wv_ctx"]),
        "xproj": a["L0_attn_x_proj_w"].T, "dtproj": a["L0_attn_dt_proj_w"].T, "dtbias": a["L0_attn_dt_proj_b"].reshape(KD, P).T,
        "alog": a["L0_attn_A_log"], "skip": a["L0_attn_D"].reshape(KD, P).T,
        "ffn_wq": a["L0_ffn_wq"], "ffn_wk": a["L0_ffn_wk"], "ffn_wv": a["L0_ffn_wv"], "ffn_wo": a["L0_ffn_wo"],
        "ln1": a["L0_ffn_ln1_w"], "ln2": a["L0_ffn_ln2_w"],
        "qnorm": a["L0_xattn_q_norm_w"], "knorm": a["L0_xattn_k_norm_w"],
    }


def perceiver_block(nc, d, out):
    x_kept, x2_kept = (nc.dram_tensor(n, (BATCH * LEN, DIM), F32, kind="Internal").ap() for n in ("x_kept", "x2_kept"))
    with ExitStack() as ctx:
        X = ctx.enter_context(nc.sbuf_tensor("X", [P, NT, DIM], F32))
        cross_attention(nc, X, d["x"], d)
        selective_scan(nc, X, d)
        self_attention(nc, X, x_kept, d)
        store_tokens(nc, X, x2_kept)
    mixture_of_experts(nc, x_kept, x2_kept, d, out)


def kernel(**inputs):
    import concourse.bacc as bacc
    from concourse.bass_utils import run_bass_kernel_spmd as run

    nc = bacc.Bacc("TRN2", target_bir_lowering=False, num_devices=1)
    arrays = {n: np.ascontiguousarray(v) for n, v in {**layouts({n: np.asarray(v) for n, v in inputs.items()}), **constants()}.items()}
    d = {n: nc.dram_tensor(f"{n}_dram", v.shape, F32, kind="ExternalInput").ap() for n, v in arrays.items()}
    out = nc.dram_tensor("out_dram", (BATCH * LEN, DIM), F32, kind="ExternalOutput").ap()
    perceiver_block(nc, d, out)
    r = run(nc, [{f"{n}_dram": v for n, v in arrays.items()}], core_ids=[0])
    return r.results[0]["out_dram"].reshape(BATCH, LEN, DIM)
```

```python
from contextlib import ExitStack

import numpy as np

import concourse.bass as bass
from concourse import mybir

F32 = mybir.dt.float32
F32R = mybir.dt.float32r
ALU = mybir.AluOpType
ACT = mybir.ActivationFunctionType
AX = mybir.AxisListType

P = 128
BATCH, LEN, DIM = 32, 64, 256
CTX = 128
NT = BATCH * LEN // P
KD = DIM // P
HD = 128
NEG = -1.0e30

HI, LO = 0, 1
THREE = ((HI, HI), (HI, LO), (LO, HI))


class Kit:

    def __init__(self, nc, ctx, tag):
        self.nc, self.ctx, self.tag = nc, ctx, tag

    def sb(self, name, shape, dt=F32):
        return self.ctx.enter_context(self.nc.sbuf_tensor(f"{self.tag}_{name}", shape, dt))

    def ps(self, name, shape):
        return self.ctx.enter_context(self.nc.psum_tensor(f"{self.tag}_{name}", shape, F32))

    def sem(self, name):
        return self.ctx.enter_context(self.nc.semaphore(f"{self.tag}_{name}"))

    def sems(self, name, n=2):
        return [self.sem(f"{name}{j}") for j in range(n)]


class Staged:

    def __init__(self, nc, ctx, n):
        self.sems, self.before = [ctx.enter_context(nc.semaphore(f"staged{j}")) for j in range(n)], [0] * n

    def counts(self, pieces, stages):
        out = []
        for j in range(pieces):
            self.before[j % stages] += 16
            out.append((self.sems[j % stages], self.before[j % stages]))
        return out


def stages(nc, tag, n, columns):
    with ExitStack() as ctx:
        return [ctx.enter_context(nc.sbuf_tensor(f"{tag}_stage{j}", [P, columns], F32))[:] for j in range(n)]


def product(pe, out, lhs, rhs, start, stop, **kw):
    for n, (a, b) in enumerate(THREE):
        last = pe.matmul(out, lhs(a), rhs(b), start=start and n == 0, stop=stop and n == 2, **kw)
    return last


NQ, NG, REP = 16, 4, 4
KEYS = CTX + LEN


def cross_attention(nc, X, xd, d, loads):
    with ExitStack() as ctx:
        k = Kit(nc, ctx, "xa")
        sb, sem, sems = k.sb, k.sem, k.sems
        WQ = sb("WQ", [P, 2, KD, NQ * HD], F32R)
        WKV = sb("WKV", [P, 2, KD, NG, 2 * HD], F32R)
        WKVC = sb("WKVC", [P, 2, KD, NG, 2 * HD], F32R)
        WO = sb("WO", [P, 2, NQ, DIM], F32R)
        ident = sb("ident", [P, P])
        cosw = [sb(f"cosw{j}", [P, HD]) for j in range(2)]
        sinw = [sb(f"sinw{j}", [P, HD]) for j in range(2)]
        normw = [sb(f"normw{j}", [P, HD]) for j in range(2)]
        cos, sin = sb("cos", [P, HD]), sb("sin", [P, HD])
        mask = sb("mask", [P, LEN])
        mhalf, lneps = sb("mhalf", [P, 8]), sb("lneps", [P, 1])
        stats, mv, rstd, xn = sb("stats", [P, 6]), sb("mv", [P, 2]), sb("rstd", [P, 1]), sb("xn", [P, DIM])
        XT = sb("XT", [P, 2, KD, P], F32R)
        ctx_raw = sb("ctx_raw", [P, KD, 2 * CTX])
        CT = sb("CT", [P, 2, KD, 2 * CTX], F32R)
        NS = 6
        stage = stages(nc, "xa", NS, 2048)
        sq, t1, t2, qn = sb("sq", [P, 7, HD]), sb("t1", [P, 7, HD]), sb("t2", [P, 5, HD]), sb("qn", [P, 7, HD])
        ss, var, rs = sb("ss", [P, 8]), sb("var", [P, 8]), sb("rs", [P, 8])
        QT = [sb(f"QT{j}", [P, 2, 2, REP * LEN], F32R) for j in range(2)]
        KT = [sb(f"KT{j}", [P, 2, 2, KEYS], F32R) for j in range(2)]
        VS = [sb(f"VS{j}", [P, 2, HD], F32R) for j in range(NG)]
        VC = [sb(f"VC{j}", [P, 2, 2, HD], F32R) for j in range(NG)]
        PR = [sb(f"PR{b}", [P, 2, KEYS]) for b in range(2)]
        nmax = [sb(f"nmax{b}", [P, 2]) for b in range(2)]
        rsum = [sb(f"rsum{b}", [P, 2]) for b in range(2)]
        rinv = [sb(f"rinv{b}", [P, 2]) for b in range(2)]
        PT = [sb(f"PT{b}", [P, 2, 2, REP * LEN], F32R) for b in range(2)]
        OT = sb("OT", [P, 2, REP, P], F32R)
        J = [k.ps(f"J{j}", [P, 512]) for j in range(2)]
        T = [k.ps(f"T{j}", [P, 512]) for j in range(2)]
        S = [k.ps(f"S{b}", [P, 2, KEYS]) for b in range(2)]
        PO = k.ps("PO", [P, 2, REP * LEN])
        ACC = k.ps("ACC", [P, DIM])

        x_in, tab_in = sem("x_in"), sem("tab_in")
        w_hi, w_lo, tabs = sem("w_hi"), sem("w_lo"), sem("tabs")
        ctx_in, ct_hi, ct_full = sem("ctx_in"), sem("ct_hi"), sem("ct_full")
        stat_full, mv_full, rstd_full, xn_full = sem("stat_full"), sem("mv_full"), sem("rstd_full"), sem("xn_full")
        J_full = sems("J_full")
        J_act, J_dve = sems("J_act"), sems("J_dve")
        T_full, T_act, T_dve = sems("T_full"), sems("T_act"), sems("T_dve")
        S_full, S_mask = sems("S_full"), sems("S_mask")
        nmax_full, exp_full, rinv_full, pr_full = sems("nmax_full"), sems("exp_full"), sems("rinv_full"), sems("pr_full")
        ss_full, var_full, rs_full, rope_full, t_sum, qn_full = (
            sem(n) for n in ("ss_full", "var_full", "rs_full", "rope_full", "t_sum", "qn_full"))
        pv_done, ot_hi, ot_full = sems("pv_done"), sem("ot_hi"), sem("ot_full")
        wo_done, acc_read = sem("wo_done"), sem("acc_read")

        pieces = [(d["wq"].rearrange("(k p) n -> p k n", p=P)[:, c, :], lambda a, c=c: WQ[:, a, c, :]) for c in range(KD)]
        pieces += [(src, lambda a, W=W: W[:, a].rearrange("p k g n -> p (k g n)")) for src, W in ((d["wkv"], WKV), (d["wkvc"], WKVC))]
        pieces += [(d["wo"].rearrange("(h p) n -> p h n", p=P)[:, 8 * c:8 * c + 8, :],
                    lambda a, c=c: WO[:, a, 8 * c:8 * c + 8, :]) for c in range(2)]

        staged = loads.counts(len(pieces), NS)

        def staging(j):
            view = stage[j % NS]
            return view.rearrange("p (a n) -> p a n", n=DIM) if len(pieces[j][0].shape) == 3 else view

        def use(n, per, i):
            return n % 2, i * (per // 2) + n // 2

        def j_use(i, g, u):
            return use(8 + 3 * g + (2 if g >= 2 else 0) + u, 14, i)

        def j_x(i, c):
            return use(14 + c, 14, i)

        def t_use(i, g, u):
            return use(2 + 4 * g + u, 16, i)

        J_FIRST = [use(n, 14, 0) for n in range(8)]
        T_FIRST = [use(n, 16, 0) for n in range(2)]

        def pr_uses(i, g, last):
            first = 0 if last and g == NG - 1 else 2
            return [t_use(i, g, first + b) for b in range(2)]

        SELF = (slice(0, LEN), slice(CTX, KEYS))
        CKEY = (slice(LEN, KEYS), slice(0, CTX))

        block = ctx.enter_context(nc.Block())

        @block.sync
        def _(sp):
            xt = xd.rearrange("(t p) n -> p t n", p=P)
            sp.dma_start(X[:, 0:2, :], xt[:, 0:2, :]).then_inc(x_in, 16)
            sp.dma_start(ctx_raw[:], d["ctxT"][0]).then_inc(ctx_in, 16)
            for dst, src in ((ident, d["ident"]), (cos, d["cos"]), (sin, d["sin"]), (mask, d["xmask"]),
                             (normw[0], d["qnorm"].partition_broadcast(P)), (normw[1], d["knorm"].partition_broadcast(P))):
                sp.dma_start(dst[:, :], src).then_inc(tab_in, 16)
            for j, (src, _) in enumerate(pieces):
                if j >= NS:
                    sp.wait_ge(w_lo, j - NS + 1)
                sp.dma_start(staging(j), src).then_inc(staged[j][0], 16)
            sp.wait_ge(x_in, 16)
            sp.dma_start(X[:, 2:, :], xt[:, 2:, :]).then_inc(x_in, 16)
            with sp.Fori(1, NT) as t:
                sp.wait_ge(ct_full, t)
                sp.dma_start(ctx_raw[:].rearrange("p k n -> p (k n)").unsqueeze(1),
                             d["ctxT"].rearrange("t p k n -> p t (k n)")[:, bass.ds(t, 1), :]).then_inc(ctx_in, 16)

        @block.scalar
        def _(act):
            for j, (_, dst) in enumerate(pieces):
                act.wait_ge(*staged[j])
                act.activation(dst(HI), staging(j), ACT.Copy).then_inc(w_hi, 1)

            def context_split(t):
                act.wait_ge(ctx_in, 16 * t + 16)
                act.activation(CT[:, HI], ctx_raw[:], ACT.Copy).then_inc(ct_hi, 1)

            def x_split(uses):
                for c, (bank, n) in enumerate(uses):
                    act.wait_ge(J_full[bank], n + 1)
                    act.activation(XT[:, HI, c, :], J[bank][:, 0:P], ACT.Copy).then_inc(J_act[bank], 1)

            def square(head, src):
                return act.activation(sq[:, head, :], src, ACT.Square, accum_out=ss[:, head:head + 1])

            def project_q(use):
                bank, n = use
                act.wait_ge(J_dve[bank], n + 1)
                for h in range(REP):
                    last = square(h, J[bank][:, h * HD:(h + 1) * HD])
                last.then_inc(J_act[bank], 1)

            def project_context(use, g):
                bank, n = use
                act.wait_ge(J_full[bank], n + 1)
                kv = J[bank][:, :].rearrange("p (b n) -> p b n", b=2)
                for b in range(2):
                    square(5 + b, kv[:, b, 0:HD])
                act.activation(VC[g][:, HI], kv[:, :, HD:], ACT.Copy).then_inc(J_act[bank], 1)

            def project_kv(use, g):
                bank, n = use
                act.wait_ge(J_full[bank], n + 1)
                square(4, J[bank][:, 0:HD]).then_inc(ss_full, 1)
                act.activation(VS[g][:, HI], J[bank][:, HD:2 * HD], ACT.Copy).then_inc(J_act[bank], 1)

            def q_split(use, par):
                bank, n = use
                act.wait_ge(T_full[bank], n + 1)
                act.activation(QT[par][:, HI].rearrange("p b (h l) -> p h b l", h=REP),
                               T[bank][:, :].rearrange("p (h b l) -> p h b l", h=REP, b=2), ACT.Copy).then_inc(T_act[bank], 1)

            def k_split(use, par):
                bank, n = use
                act.wait_ge(T_full[bank], n + 1)
                act.activation(KT[par][:, HI], T[bank][:, 0:2 * KEYS].rearrange("p (b n) -> p b n", b=2),
                               ACT.Copy).then_inc(T_act[bank], 1)

            def exps(s, b):
                act.wait_ge(nmax_full[b], s + 1)
                act.wait_ge(pv_done[b], s + 1)
                for pair in range(2):
                    act.activation(PR[b][:, pair, :], S[b][:, pair, :], ACT.Exp, bias=nmax[b][:, pair:pair + 1],
                                   accum_out=rsum[b][:, pair:pair + 1]).then_inc(exp_full[b], 1)

            def slot(i, g, last=False):
                s = 4 * i + g
                turn, project = not (last and g == NG - 1), not (last and g >= 2)
                exps(s, 0)
                if turn:
                    act.wait_ge(S_full[1], s + 1)
                    q_split(t_use(i, g, 0), (g + 1) % 2)
                exps(s, 1)
                if turn:
                    k_split(t_use(i, g, 1), (g + 1) % 2)
                if project:
                    project_q(j_use(i, g, 0))
                for b, (bank, n) in enumerate(pr_uses(i, g, last)):
                    act.wait_ge(T_full[bank], n + 1)
                    act.activation(PT[b][:, HI], T[bank][:, :].rearrange("p (a n) -> p a n", a=2),
                                   ACT.Copy).then_inc(T_act[bank], 1)
                if project:
                    project_context(j_use(i, g, 1), (g + 2) % NG)
                    project_kv(j_use(i, g, 2), (g + 2) % NG)
                if g == 1 and not last:
                    context_split(i + 1)
                act.wait_ge(pv_done[1], s + 2)
                act.wait_ge(wo_done, s + 1)
                act.activation(OT[:, HI].rearrange("p h (b l) -> p b h l", b=2),
                               PO[:, :, :].rearrange("p b (h l) -> p b h l", h=REP), ACT.Copy).then_inc(ot_hi, 1)
                if g == 1 and not last:
                    x_split([j_x(i, c) for c in range(KD)])

            context_split(0)
            x_split(J_FIRST[0:2])
            for g in range(2):
                if g:
                    act.wait_ge(qn_full, 2)
                project_q(J_FIRST[2 + 3 * g])
                project_context(J_FIRST[3 + 3 * g], g)
                project_kv(J_FIRST[4 + 3 * g], g)
            q_split(T_FIRST[0], 0)
            k_split(T_FIRST[1], 0)
            with act.Fori(0, NT - 1) as i:
                for g in range(NG):
                    slot(i, g)
            for g in range(NG):
                slot(NT - 1, g, last=True)

        @block.vector
        def _(dve):
            for unused in (ot_full, acc_read):
                dve.sem_inc(unused, 1)
            dve.wait_ge(tab_in, 6 * 16)
            half = HD // 2
            for j, scale in enumerate((HD ** -0.5, 1.0)):
                dve.scalar_tensor_tensor(cosw[j][:], cos[:], scale, normw[j][:], ALU.mult, ALU.mult)
                dve.scalar_tensor_tensor(sinw[j][:, :half], sin[:, :half], scale, normw[j][:, half:], ALU.mult, ALU.mult)
                dve.scalar_tensor_tensor(sinw[j][:, half:], sin[:, half:], scale, normw[j][:, :half], ALU.mult, ALU.mult).then_inc(tabs, 1)

            def norm_stats(x):
                dve.bn_stats(stats[:], x).then_inc(stat_full, 1)

            def norm_var():
                dve.bn_aggr(mv[:], stats[:]).then_inc(mv_full, 1)

            def norm_apply(x, t):
                dve.wait_ge(rstd_full, t + 1)
                dve.tensor_scalar(xn[:], x, mv[:, 0:1], rstd[:, 0:1], ALU.subtract, ALU.mult).then_inc(xn_full, 1)

            dve.wait_ge(x_in, 16)
            norm_stats(X[:, 0, :])
            dve.wait_ge(stat_full, 1)
            norm_var()
            for j, (_, dst) in enumerate(pieces):
                dve.wait_ge(w_hi, j + 1)
                dve.tensor_tensor(dst(LO), staging(j), dst(HI), ALU.subtract).then_inc(w_lo, 1)
            norm_apply(X[:, 0, :], 0)

            def context_split(t):
                dve.wait_ge(ct_hi, t + 1)
                dve.tensor_tensor(CT[:, LO], ctx_raw[:], CT[:, HI], ALU.subtract).then_inc(ct_full, 1)

            def x_split(uses):
                for c, (bank, n) in enumerate(uses):
                    dve.wait_ge(J_act[bank], n + 1)
                    dve.tensor_tensor(XT[:, LO, c, :], J[bank][:, 0:P], XT[:, HI, c, :], ALU.subtract).then_inc(J_dve[bank], 1)

            def rope(src, first, heads, j):
                v = src.rearrange("p (h e) -> p h e", h=heads)
                half = HD // 2
                dve.tensor_tensor(t1[:, first:first + heads, :], v, cosw[j][:, None, :].broadcast_to([P, heads, HD]), ALU.mult)
                dve.tensor_tensor(t2[:, first:first + heads, :half], v[:, :, half:],
                                  sinw[j][:, None, :half].broadcast_to([P, heads, half]), ALU.mult)
                return dve.tensor_tensor(t2[:, first:first + heads, half:], v[:, :, :half],
                                         sinw[j][:, None, half:].broadcast_to([P, heads, half]), ALU.mult)

            def project_q(use):
                bank, n = use
                dve.wait_ge(J_full[bank], n + 1)
                rope(J[bank][:, :], 0, REP, 0).then_inc(J_dve[bank], 1)

            def project_context(use, g):
                bank, n = use
                kv = J[bank][:, :].rearrange("p (b n) -> p b n", b=2)
                dve.wait_ge(J_act[bank], n + 1)
                dve.tensor_tensor(t1[:, 5:7, :], kv[:, :, 0:HD], normw[1][:, None, :].broadcast_to([P, 2, HD]), ALU.mult)
                dve.tensor_tensor(VC[g][:, LO], kv[:, :, HD:], VC[g][:, HI], ALU.subtract).then_inc(J_dve[bank], 1)

            def project_kv(use, g):
                bank, n = use
                dve.wait_ge(J_act[bank], n + 1)
                rope(J[bank][:, 0:HD], 4, 1, 1).then_inc(rope_full, 1)
                dve.tensor_tensor(VS[g][:, LO], J[bank][:, HD:2 * HD], VS[g][:, HI], ALU.subtract).then_inc(J_dve[bank], 1)

            def q_split(use, par):
                bank, n = use
                dve.wait_ge(T_act[bank], n + 1)
                dve.tensor_tensor(QT[par][:, LO].rearrange("p b (h l) -> p h b l", h=REP),
                                  T[bank][:, :].rearrange("p (h b l) -> p h b l", h=REP, b=2),
                                  QT[par][:, HI].rearrange("p b (h l) -> p h b l", h=REP), ALU.subtract).then_inc(T_dve[bank], 1)

            def k_split(use, par):
                bank, n = use
                dve.wait_ge(T_act[bank], n + 1)
                dve.tensor_tensor(KT[par][:, LO], T[bank][:, 0:2 * KEYS].rearrange("p (b n) -> p b n", b=2),
                                  KT[par][:, HI], ALU.subtract).then_inc(T_dve[bank], 1)

            def normalise(s, b):
                dve.wait_ge(exp_full[b], 2 * s + 2)
                dve.reciprocal(rinv[b][:], rsum[b][:]).then_inc(rinv_full[b], 1)
                dve.wait_ge(rinv_full[b], s + 1)
                for pair in range(2):
                    done = dve.tensor_scalar(PR[b][:, pair, :], PR[b][:, pair, :], rinv[b][:, pair:pair + 1], None, ALU.mult)
                done.then_inc(pr_full[b], 1)

            def maxima(s):
                for b in range(2):
                    dve.wait_ge(S_full[b], s + 2)
                    own = S[b][:, :, SELF[b]]
                    dve.tensor_tensor(own, own, mask[:, None, :].broadcast_to([P, 2, LEN]), ALU.add).then_inc(S_mask[b], 1)
                    dve.wait_ge(S_mask[b], s + 1)
                    dve.tensor_reduce(nmax[b][:], S[b][:, :, :], AX.X, ALU.max, negate=True).then_inc(nmax_full[b], 1)

            def slot(i, g, last=False):
                s = 4 * i + g
                turn, project = not (last and g == NG - 1), not (last and g >= 2)
                if g == 0 and not last:
                    norm_stats(X[:, bass.ds(i + 1, 1), :].rearrange("p a n -> p (a n)"))
                normalise(s, 0)
                if turn:
                    q_split(t_use(i, g, 0), (g + 1) % 2)
                if project:
                    project_q(j_use(i, g, 0))
                if g == 0 and not last:
                    dve.wait_ge(stat_full, i + 2)
                normalise(s, 1)
                if g == 0 and not last:
                    norm_var()
                if turn:
                    k_split(t_use(i, g, 1), (g + 1) % 2)
                for b, (bank, n) in enumerate(pr_uses(i, g, last)):
                    dve.wait_ge(T_act[bank], n + 1)
                    dve.tensor_tensor(PT[b][:, LO], T[bank][:, :].rearrange("p (a n) -> p a n", a=2),
                                      PT[b][:, HI], ALU.subtract).then_inc(T_dve[bank], 1)
                if project:
                    project_context(j_use(i, g, 1), (g + 2) % NG)
                    project_kv(j_use(i, g, 2), (g + 2) % NG)
                if g == 0 and not last:
                    norm_apply(X[:, bass.ds(i + 1, 1), :].rearrange("p a n -> p (a n)"), i + 1)
                if g == 1 and not last:
                    context_split(i + 1)
                dve.wait_ge(ot_hi, s + 1)
                dve.tensor_tensor(OT[:, LO].rearrange("p h (b l) -> p b h l", b=2),
                                  PO[:, :, :].rearrange("p b (h l) -> p b h l", h=REP),
                                  OT[:, HI].rearrange("p h (b l) -> p b h l", b=2), ALU.subtract).then_inc(ot_full, 1)
                if turn:
                    maxima(s + 1)
                if g == 1 and not last:
                    x_split([j_x(i, c) for c in range(KD)])
                if g == NG - 1:
                    dve.wait_ge(wo_done, s + 2)
                    x = X[:, bass.ds(i, 1), :].rearrange("p a n -> p (a n)") if not last else X[:, i, :]
                    dve.tensor_tensor(x, ACC[:, :], x, ALU.add).then_inc(acc_read, 1)

            dve.wait_ge(tabs, 2)
            context_split(0)
            x_split(J_FIRST[0:2])
            for g in range(2):
                if g:
                    dve.wait_ge(qn_full, 2)
                project_q(J_FIRST[2 + 3 * g])
                project_context(J_FIRST[3 + 3 * g], g)
                project_kv(J_FIRST[4 + 3 * g], g)
            q_split(T_FIRST[0], 0)
            k_split(T_FIRST[1], 0)
            maxima(0)
            dve.wait_ge(x_in, 32)
            with dve.Fori(0, NT - 1) as i:
                for g in range(NG):
                    slot(i, g)
            for g in range(NG):
                slot(NT - 1, g, last=True)

        @block.gpsimd
        def _(pool):
            pool.memset(lneps[:], 1e-5)
            pool.memset(mhalf[:], -0.5).then_inc(var_full, 1)
            pool.wait_ge(var_full, 1)

            def ln_rstd(t, n):
                pool.wait_ge(mv_full, t + 1)
                pool.tensor_tensor(rstd[:], mv[:, 1:2], lneps[:], ALU.add).then_inc(var_full, 1)
                pool.wait_ge(var_full, n + 1)
                pool.tensor_tensor(rstd[:], rstd[:], mhalf[:, 0:1], ALU.pow).then_inc(rstd_full, 1)

            def norms(s, n, q_use, k_turn=None):
                def scaled(heads):
                    return pool.tensor_tensor(qn[:, heads, :], t1[:, heads, :],
                                              rs[:, heads, None].broadcast_to([P, heads.stop - heads.start, HD]), ALU.mult)

                pool.wait_ge(J_dve[q_use[0]], q_use[1] + 1)
                pool.tensor_tensor(t1[:, 0:4, :], t1[:, 0:4, :], t2[:, 0:4, :], ALU.add).then_inc(t_sum, 1)
                pool.wait_ge(ss_full, s + 1)
                pool.tensor_tensor(var[:, 7:8], mhalf[:, 7:8], mhalf[:, 7:8], ALU.mult)
                pool.tensor_scalar(var[:, 0:7], ss[:, 0:7], 1.0 / HD, 1e-6, ALU.mult, ALU.add).then_inc(var_full, 1)
                pool.wait_ge(var_full, n + 1)
                pool.tensor_tensor(rs[:, 0:7], var[:, 0:7], mhalf[:, 0:7], ALU.pow).then_inc(rs_full, 1)
                pool.wait_ge(rope_full, s + 1)
                pool.tensor_tensor(t1[:, 4, :], t1[:, 4, :], t2[:, 4, :], ALU.add).then_inc(t_sum, 1)
                pool.wait_ge(rs_full, s + 1)
                pool.wait_ge(t_sum, 2 * s + 2)
                if k_turn:
                    pool.wait_ge(T_full[k_turn[0]], k_turn[1] + 1)
                scaled(slice(0, 4)).then_inc(qn_full, 1)
                scaled(slice(4, 7)).then_inc(qn_full, 1)

            ln_rstd(0, 1)
            norms(0, 2, J_FIRST[2])
            norms(1, 3, J_FIRST[5], T_FIRST[1])
            with pool.Fori(0, NT - 1) as i:
                for g in range(NG):
                    if g == 0:
                        ln_rstd(i + 1, 5 * i + 4)
                    norms(4 * i + g + 2, 5 * i + 5 + g, j_use(i, g, 0), t_use(i, g, 1))
            for g in range(2):
                norms(4 * (NT - 1) + g + 2, 5 * (NT - 1) + 4 + g, j_use(NT - 1, g, 0), t_use(NT - 1, g, 1))

        @block.tensor
        def _(pe):
            def fill_j(bank, n):
                if not (isinstance(n, int) and n == 0):
                    pe.wait_ge(J_dve[bank], n)

            def x_turn(uses, t):
                pe.wait_ge(xn_full, t + 1)
                for c, (bank, n) in enumerate(uses):
                    fill_j(bank, n)
                    pe.transpose(J[bank][:, 0:P], xn[:, c * P:(c + 1) * P], ident[:]).then_inc(J_full[bank], 1)

            def project_q(uses, g):
                (bq, nq), (bc, n_c), _ = uses
                fill_j(bq, nq)
                if g == 0:
                    fill_j(bc, n_c)
                for c in range(KD):
                    mm = product(pe, J[bq][:, :], lambda a: XT[:, a, c, :], lambda a: WQ[:, a, c, g * 512:(g + 1) * 512],
                                 c == 0, c == KD - 1)
                mm.then_inc(J_full[bq], 1)

            def project_context(uses, g, t):
                bc, n_c = uses[1]
                fill_j(bc, n_c)
                if g == 0:
                    pe.wait_ge(ct_full, t + 1)
                for b in range(2):
                    for c in range(KD):
                        mm = product(pe, J[bc][:, b * 256:(b + 1) * 256], lambda a: CT[:, a, c, b * CTX:(b + 1) * CTX],
                                     lambda a: WKVC[:, a, c, g, :], c == 0, c == KD - 1)
                mm.then_inc(J_full[bc], 1)

            def project_kv(uses, g):
                bs, n_s = uses[2]
                pe.wait_ge(J_act[bs], n_s)
                for c in range(KD):
                    mm = product(pe, J[bs][:, 0:256], lambda a: XT[:, a, c, :], lambda a: WKV[:, a, c, g, :], c == 0, c == KD - 1)
                mm.then_inc(J_full[bs], 1)

            def q_turn(use, s):
                bank, n = use
                pe.wait_ge(qn_full, 2 * s + 1)
                if not (isinstance(n, int) and n == 0):
                    pe.wait_ge(T_dve[bank], n)
                for h in range(REP):
                    mm = pe.transpose(T[bank][:, h * P:(h + 1) * P], qn[:, h, :], ident[:])
                mm.then_inc(T_full[bank], 1)

            def k_turn(use, s):
                bank, n = use
                pe.wait_ge(qn_full, 2 * s + 2)
                if not (isinstance(n, int) and n == 0):
                    pe.wait_ge(T_dve[bank], n)
                for b in range(2):
                    pe.transpose(T[bank][:, b * KEYS + CKEY[b].start:b * KEYS + CKEY[b].stop], qn[:, 5 + b, :], ident[:])
                own = T[bank][:, 0:2 * KEYS].rearrange("p (r l) -> p r l", l=LEN)[:, ::5, :]
                pe.transpose(own, qn[:, 4, :], ident[:]).then_inc(T_full[bank], 1)

            def scores(uses, s, par):
                (bq, nq), (bk, nk) = uses
                pe.wait_ge(T_dve[bq], nq + 1)
                pe.wait_ge(T_dve[bk], nk + 1)
                for b in range(2):
                    if not (isinstance(s, int) and s == 0):
                        pe.wait_ge(exp_full[b], 2 * s)
                    for pair in range(2):
                        mm = product(pe, S[b][:, pair, :], lambda a: QT[par][:, a, b, pair * P:(pair + 1) * P],
                                     lambda a: KT[par][:, a, b, :], True, True)
                    mm.then_inc(S_full[b], 1)

            def slot(i, g, last=False):
                s = 4 * i + g
                uses = [j_use(i, g, u) for u in range(3)]
                next_qk = [t_use(i, g, u) for u in (0, 1)]
                turn, project = not (last and g == NG - 1), not (last and g >= 2)
                if turn:
                    q_turn(next_qk[0], s + 1)
                if project:
                    project_q(uses, (g + 2) % NG)
                if turn:
                    k_turn(next_qk[1], s + 1)
                if project:
                    project_context(uses, (g + 2) % NG, i + 1)
                for b, (bank, n) in enumerate(pr_uses(i, g, last)):
                    pe.wait_ge(pr_full[b], s + 1)
                    pe.wait_ge(T_dve[bank], n)
                    at_own = (0, LEN)[b]
                    for part, col in ((0, CKEY[b].start), (1, at_own)):
                        for pair in range(2):
                            mm = pe.transpose(T[bank][:, part * 256 + pair * P:part * 256 + (pair + 1) * P],
                                              PR[b][:, pair, col:col + P], ident[:])
                    mm.then_inc(T_full[bank], 1)
                if project:
                    project_kv(uses, (g + 2) % NG)
                for b, (bank, n) in enumerate(pr_uses(i, g, last)):
                    pe.wait_ge(T_dve[bank], n + 1)
                    if b == 0:
                        pe.wait_ge(ot_full, s + 1)
                    product(pe, PO[:, b, :], lambda a: VC[g][:, a, b, :], lambda a: PT[b][:, a, 0, :], True, False)
                    own = slice(b * LEN, (b + 1) * LEN)
                    if b == 1:
                        pe.wait_ge(pv_done[0], s + 2)
                    product(pe, PO[:, b, :], lambda a: VS[g][own, a, :], lambda a: PT[b][own, a, 1, :], False, True)\
                        .then_inc(pv_done[b], 1)
                if turn:
                    scores(next_qk, s + 1, (g + 1) % 2)
                if g == 1 and not last:
                    x_turn([j_x(i, c) for c in range(KD)], i + 1)
                pe.wait_ge(ot_full, s + 2)
                if g == 0:
                    pe.wait_ge(acc_read, i + 1)
                for h in range(REP):
                    mm = product(pe, ACC[:, :], lambda a: OT[:, a, h, :], lambda a: WO[:, a, REP * g + h, :],
                                 g == 0 and h == 0, g == NG - 1 and h == REP - 1)
                mm.then_inc(wo_done, 1)

            for unused in (*pv_done, *S_full, wo_done):
                pe.sem_inc(unused, 1)
            pe.wait_ge(tab_in, 6 * 16)
            x_turn(J_FIRST[0:2], 0)
            pe.wait_ge(w_lo, len(pieces))
            for g in range(2):
                project_q(J_FIRST[2 + 3 * g:5 + 3 * g], g)
                project_context(J_FIRST[2 + 3 * g:5 + 3 * g], g, 0)
                project_kv(J_FIRST[2 + 3 * g:5 + 3 * g], g)
            q_turn(T_FIRST[0], 0)
            k_turn(T_FIRST[1], 0)
            scores(T_FIRST, 0, 0)
            with pe.Fori(0, NT - 1) as i:
                for g in range(NG):
                    slot(i, g)
            for g in range(NG):
                slot(NT - 1, g, last=True)


DSTATE, DTRANK = 16, 128
CT4 = 4
NC = NT // CT4
CHUNK = CT4 * P


def tokens(X, c, first=0, n=CT4):
    return X[:, bass.ds(c * CT4 + first, n), :]


def tile_of(X, c, t):
    return tokens(X, c, t, 1).rearrange("p a n -> p (a n)")


def selective_scan(nc, X, d):
    Q = KD * DSTATE
    RING, AHEAD = 4, 4
    POOL_STEPS = [q for q in range(Q) if q % 8 in (3, 7)]
    DVE_STEPS = [q for q in range(Q) if q not in POOL_STEPS]
    with ExitStack() as ctx:
        k = Kit(nc, ctx, "ss")
        sb, sem, sems = k.sb, k.sem, k.sems
        ident, scrap, lneps, mhalf = sb("ident", [P, P]), sb("scrap", [P, 1]), sb("lneps", [P, CT4]), sb("mhalf", [P, CT4])
        w_raw = sb("w_raw", [P, KD, DTRANK + 2 * DSTATE])
        W = sb("W", [P, 2, KD, DTRANK + 2 * DSTATE], F32R)
        dt_raw, DTW = sb("dt_raw", [P, DIM]), sb("DTW", [P, 2, DIM], F32R)
        SEL = sb("SEL", [64, 2 * DSTATE, P], F32R)
        bias, alog, A, skip = sb("bias", [P, KD]), sb("alog", [P, KD, DSTATE]), sb("A", [P, KD, DSTATE]), sb("skip", [P, KD])
        stats, mv, rstd = sb("stats", [P, CT4, 6]), sb("mv", [P, CT4, 2]), sb("rstd", [P, CT4])
        xn = sb("xn", [P, CT4, DIM])
        XT, XF = sb("XT", [P, 2, KD, CHUNK], F32R), sb("XF", [P, KD, CHUNK])
        DL, bc_raw, BC = sb("DL", [P, 2, CHUNK], F32R), sb("bc_raw", [32, CHUNK]), sb("BC", [64, CHUNK], F32R)
        az, rz, ez, lz = (sb(n, [P, KD, CHUNK]) for n in ("az", "rz", "ez", "lz"))
        dt, u, y = (sb(n, [P, KD, CHUNK]) for n in ("dt", "u", "y"))
        decay = [sb(f"decay{j}", [P, CHUNK // LEN, LEN]) for j in range(RING)]
        bx, state, cy = ([sb(f"{n}{j}", [P, CHUNK]) for j in range(RING)] for n in ("bx", "state", "cy"))
        b_all = [sb(f"b_all{j}", [P, CHUNK]) for j in range(2)]
        M = [k.ps(f"M{j}", [P, CHUNK]) for j in range(2)]
        BB = [k.ps(f"BB{j}", [P, CHUNK]) for j in range(RING)]
        CB = [k.ps(f"CB{j}", [P, CHUNK]) for j in range(2)]

        w_in, sel_in, w_hi, w_full = sem("w_in"), sem("sel_in"), sem("w_hi"), sem("w_full")
        stat_full, mv_full, var_full, rstd_full, xn_full = (sem(n) for n in ("stat_full", "mv_full", "var_full", "rstd_full", "xn_full"))
        M_full, M_act, M_dve = sems("M_full"), sems("M_act"), sems("M_dve")
        ez_full, lz_full, dt_full, du_full = (sem(n) for n in ("ez_full", "lz_full", "dt_full", "du_full"))
        bc_hi, bc_full, skip_full = sem("bc_hi"), sem("bc_full"), sem("skip_full")
        bb_full, cb_full, b_full, decay_full, bx_dve, bx_pool, state_full, cy_full, added = (
            sem(n) for n in ("bb_full", "cb_full", "b_full", "decay_full", "bx_dve", "bx_pool", "state_full", "cy_full", "added"))
        yt_full = sem("yt_full")

        START = {"pe": (bb_full, cb_full), "act": (b_full, decay_full), "dve": (bx_dve, state_full, cy_full), "pool": (bx_pool, added)}

        def start(engine, name):
            for signal in START[name]:
                engine.sem_inc(signal, 4)

        def step(c, q):
            return c * Q + (q + 5)

        def some(steps, c, q):
            before = len(steps) if q < 0 else 0
            return c * len(steps) + (4 + sum(m <= q % Q for m in steps) - before)

        def bx_of(c, q):
            return (bx_pool, some(POOL_STEPS, c, q)) if q % Q in POOL_STEPS else (bx_dve, some(DVE_STEPS, c, q))

        def steps(c, last=False):
            return [(c, q) for q in range(AHEAD, Q)] + ([] if last else [(c + 1, q) for q in range(AHEAD)])

        block = ctx.enter_context(nc.Block())

        @block.sync
        def _(sp):
            for dst, src in ((ident, d["ident"]), (w_raw, d["xproj"].rearrange("(k p) n -> p k n", p=P)), (dt_raw, d["dtproj"]),
                             (bias, d["dtbias"]),
                             (alog, d["alog"].rearrange("(k p) n -> p k n", p=P)), (skip, d["skip"])):
                sp.dma_start(dst[:], src).then_inc(w_in, 16)

        @block.scalar
        def _(act):
            start(act, "act")
            act.wait_ge(w_in, 6 * 16)
            act.activation(W[:, HI], w_raw[:], ACT.Copy)
            act.activation(DTW[:, HI], dt_raw[:], ACT.Copy)
            act.activation(A[:], alog[:], ACT.Exp).then_inc(w_hi, 1)
            act.wait_ge(w_full, 2)

            def x_split(c):
                for j in range(KD):
                    act.wait_ge(M_full[j], 3 * c + 1)
                    act.activation(XT[:, HI, j, :], M[j][:, :], ACT.Copy)
                    act.activation(XF[:, j, :], M[j][:, :], ACT.Copy).then_inc(M_act[j], 1)

            def low_split(c):
                act.wait_ge(M_full[0], 3 * c + 2)
                act.activation(DL[:, HI], M[0][:, :], ACT.Copy).then_inc(M_act[0], 1)
                act.wait_ge(M_full[1], 3 * c + 2)
                act.activation(bc_raw[:], M[1][0:32, :], ACT.Copy).then_inc(M_act[1], 1)

            def soft_abs(c):
                for j in range(KD):
                    act.wait_ge(M_full[j], 3 * c + 3)
                    act.activation(az[:, j, :], M[j][:, :], ACT.Abs, bias=bias[:, j:j + 1]).then_inc(M_act[j], 1)

            def soft_exp(c):
                for j in range(KD):
                    act.wait_ge(M_act[j], 3 * c + 3)
                act.activation(ez[:], az[:], ACT.Exp, scale=-1.0).then_inc(ez_full, 1)

            def soft_ln(c):
                act.wait_ge(ez_full, c + 1)
                act.activation(lz[:], ez[:], ACT.Ln, bias=1.0).then_inc(lz_full, 1)

            def bc_split():
                act.activation(BC[0:32, :], bc_raw[:], ACT.Copy).then_inc(bc_hi, 1)

            def run(c, q):
                half, n = divmod(q, DSTATE)
                if q in POOL_STEPS:
                    act.wait_ge(bb_full, step(c, q))
                    k = POOL_STEPS.index(q)
                    before = POOL_STEPS[k - 2] if k >= 2 else POOL_STEPS[k - 2] - Q
                    act.wait_ge(bx_pool, some(POOL_STEPS, c, before))
                    act.activation(b_all[k % 2][:], BB[q % RING][:, :], ACT.Copy).then_inc(b_full, 1)
                if n == 0:
                    act.wait_ge(du_full, 2 * c + half + 1)
                act.wait_ge(state_full, step(c, q - RING))
                act.activation(decay[q % RING][:, :, 1:], dt[:, half, :].rearrange("p (b l) -> p b l", l=LEN)[:, :, 1:],
                               ACT.Exp, scale=A[:, half, n:n + 1]).then_inc(decay_full, 1)
                if q == AHEAD - 1:
                    act.wait_ge(yt_full, c + 1)
                    for j in range(KD):
                        skipped = act.activation(y[:, j, :], XF[:, j, :], ACT.Copy, scale=skip[:, j:j + 1])
                    skipped.then_inc(skip_full, 1)

            def chunk(c, last=False):
                for cc, q in steps(c, last):
                    run(cc, q)
                    if not last and q >= AHEAD:
                        for at, stage_of in ((12, x_split), (18, low_split), (23, soft_abs), (24, soft_exp), (25, soft_ln)):
                            if q == at:
                                stage_of(c + 1)
                        if q == Q - 1:
                            act.wait_ge(cb_full, step(c, Q - 1))
                            bc_split()

            for stage_of in (x_split, low_split, soft_abs, soft_exp, soft_ln):
                stage_of(0)
            act.wait_ge(M_act[1], 2)
            bc_split()
            for q in range(AHEAD):
                run(0, q)
            with act.Fori(0, NC - 1) as c:
                chunk(c)
            chunk(NC - 1, last=True)

        @block.vector
        def _(dve):
            start(dve, "dve")
            for buf in decay:
                zeroed = dve.memset(buf[:], 0.0)
            zeroed.then_inc(w_full, 1)

            def split_weights():
                dve.wait_ge(w_hi, 1)
                dve.tensor_tensor(W[:, LO], w_raw[:], W[:, HI], ALU.subtract)
                dve.tensor_tensor(DTW[:, LO], dt_raw[:], DTW[:, HI], ALU.subtract)
                dve.tensor_scalar(A[:], A[:], -1.0, None, ALU.mult).then_inc(w_full, 1)

            def tile(c, t):
                return X[:, c * CT4 + t, :] if isinstance(c, int) else tile_of(X, c, t)

            def norm_stats(c):
                for t in range(CT4):
                    last = dve.bn_stats(stats[:, t, :], tile(c, t))
                last.then_inc(stat_full, 1)

            def norm_var(c):
                dve.wait_ge(stat_full, c + 1)
                dve.memset(scrap[:], 0.0)
                for t in range(CT4):
                    last = dve.bn_aggr(mv[:, t, :], stats[:, t, :])
                last.then_inc(mv_full, 1)

            def norm_apply(c):
                dve.wait_ge(rstd_full, c + 1)
                dve.memset(scrap[:], 0.0)
                for t in range(CT4):
                    last = dve.tensor_scalar(xn[:, t, :], tile(c, t), mv[:, t, 0:1], rstd[:, t:t + 1], ALU.subtract, ALU.mult)
                last.then_inc(xn_full, 1)

            def x_split(c):
                for j in range(KD):
                    dve.wait_ge(M_act[j], 3 * c + 1)
                    dve.tensor_tensor(XT[:, LO, j, :], M[j][:, :], XT[:, HI, j, :], ALU.subtract).then_inc(M_dve[j], 1)

            def low_split(c):
                dve.wait_ge(M_act[0], 3 * c + 2)
                dve.tensor_tensor(DL[:, LO], M[0][:, :], DL[:, HI], ALU.subtract).then_inc(M_dve[0], 1)

            def soft_max0(c):
                for j in range(KD):
                    dve.wait_ge(M_act[j], 3 * c + 3)
                    dve.tensor_scalar(rz[:, j, :], M[j][:, :], bias[:, j:j + 1], 0.0, ALU.add, ALU.max).then_inc(M_dve[j], 1)

            def bc_split(c):
                dve.wait_ge(bc_hi, c + 1)
                dve.tensor_tensor(BC[32:64, :], bc_raw[:], BC[0:32, :], ALU.subtract).then_inc(bc_full, 1)

            def input_of(c, q):
                half, n = divmod(q, DSTATE)
                if n == 0:
                    dve.wait_ge(du_full, 2 * c + half + 1)
                dve.wait_ge(bb_full, step(c, q))
                dve.wait_ge(state_full, step(c, q - RING))
                dve.tensor_tensor(bx[q % RING][:], BB[q % RING][:, :], u[:, half, :], ALU.mult).then_inc(bx_dve, 1)

            def read_out(c, q):
                dve.wait_ge(cb_full, step(c, q))
                dve.wait_ge(state_full, step(c, q))
                dve.wait_ge(added, step(c, q - RING))
                dve.tensor_tensor(cy[q % RING][:], CB[q % 2][:, :], state[q % RING][:], ALU.mult).then_inc(cy_full, 1)

            def run(c, q):
                if q + 1 in DVE_STEPS:
                    input_of(c, q + 1)
                dve.wait_ge(decay_full, step(c, q))
                dve.wait_ge(*bx_of(c, q))
                dve.wait_ge(cy_full, step(c, q - RING))
                dve.tensor_tensor_scan(state[q % RING][:], decay[q % RING][:].rearrange("p b l -> p (b l)"), bx[q % RING][:], 0.0,
                                       ALU.mult, ALU.add).then_inc(state_full, 1)
                if q:
                    read_out(c, q - 1)

            def chunk(c, last=False):
                for cc, q in steps(c, last):
                    if q == 0:
                        read_out(c, Q - 1)
                        bc_split(c + 1)
                        input_of(c + 1, 0)
                    run(cc, q)
                    if not last and q >= AHEAD:
                        for at, stage_of in ((4, norm_stats), (5, norm_var), (7, norm_apply), (12, x_split), (18, low_split), (23, soft_max0)):
                            if q == at:
                                stage_of(c + 1)
                if last:
                    read_out(c, Q - 1)
                dve.wait_ge(yt_full, c + 2)
                for t in range(0, CT4, 2):
                    x = X[:, c * CT4 + t:c * CT4 + t + 2, :] if last else tokens(X, c, t, 2)
                    dve.tensor_tensor(x, M[t // 2][:, :].rearrange("p (a n) -> p a n", a=2), x, ALU.add)

            for stage_of in (norm_stats, norm_var, norm_apply):
                stage_of(0)
            split_weights()
            dve.wait_ge(w_full, 2)
            for stage_of in (x_split, low_split, soft_max0, bc_split):
                stage_of(0)
            input_of(0, 0)
            for q in range(AHEAD):
                run(0, q)
            with dve.Fori(0, NC - 1) as c:
                chunk(c)
            chunk(NC - 1, last=True)

        @block.gpsimd
        def _(pool):
            start(pool, "pool")
            pool.dma_start(SEL[:], d["sel_bc"]).then_inc(sel_in, 16)
            pool.memset(lneps[:], 1e-5)
            pool.memset(mhalf[:], -0.5).then_inc(var_full, 1)
            pool.wait_ge(var_full, 1)

            def norm_rstd(c):
                pool.wait_ge(mv_full, c + 1)
                pool.tensor_tensor(rstd[:], mv[:, :, 1], lneps[:], ALU.add).then_inc(var_full, 1)
                pool.wait_ge(var_full, c + 2)
                pool.tensor_tensor(rstd[:], rstd[:], mhalf[:], ALU.pow).then_inc(rstd_full, 1)

            def dt_u(c, half):
                pool.wait_ge(lz_full, c + 1)
                pool.wait_ge(M_dve[half], (3 - half) * (c + 1))
                pool.tensor_tensor(dt[:, half, :], rz[:, half, :], lz[:, half, :], ALU.add).then_inc(dt_full, 1)
                pool.wait_ge(dt_full, 2 * c + half + 1)
                pool.tensor_tensor(u[:, half, :], dt[:, half, :], XF[:, half, :], ALU.mult).then_inc(du_full, 1)

            def input_of(c, q):
                half, k = q // DSTATE, POOL_STEPS.index(q)
                if POOL_STEPS[k - 1] // DSTATE != half:
                    pool.wait_ge(du_full, 2 * c + half + 1)
                pool.wait_ge(b_full, some(POOL_STEPS, c, q))
                pool.wait_ge(state_full, step(c, q - RING))
                pool.tensor_tensor(bx[q % RING][:], b_all[k % 2][:], u[:, half, :], ALU.mult).then_inc(bx_pool, 1)

            def run(c, q):
                if q + 3 in POOL_STEPS:
                    input_of(c, q + 3)
                if q == 0:
                    pool.wait_ge(skip_full, c + 1)
                half = q // DSTATE
                pool.wait_ge(cy_full, step(c, q))
                pool.wait_ge(added, step(c, q - 1))
                pool.tensor_tensor(y[:, half, :], y[:, half, :], cy[q % RING][:], ALU.add).then_inc(added, 1)
                if q == 2:
                    dt_u(c, 1)

            def chunk(c, last=False):
                for cc, q in steps(c, last):
                    run(cc, q)
                    if q == 5 and not last:
                        norm_rstd(c + 1)
                    if q == 25 and not last:
                        dt_u(c + 1, 0)

            norm_rstd(0)
            dt_u(0, 0)
            for q in range(AHEAD):
                run(0, q)
            with pool.Fori(0, NC - 1) as c:
                chunk(c)
            chunk(NC - 1, last=True)

        @block.tensor
        def _(pe):
            start(pe, "pe")
            pe.sem_inc(yt_full, 1)
            pe.wait_ge(w_in, 6 * 16)

            def x_turn(c, j):
                pe.wait_ge(xn_full, c + 1)
                for t in range(CT4):
                    mm = pe.transpose(M[j][:, t * P:(t + 1) * P], xn[:, t, j * P:(j + 1) * P], ident[:])
                mm.then_inc(M_full[j], 1)

            def low_project(c, part):
                m, j = divmod(part, KD)
                rows = (slice(0, DTRANK), slice(DTRANK, DTRANK + 2 * DSTATE))[m]
                if part == 0:
                    for b in range(KD):
                        pe.wait_ge(M_dve[b], (3 - b) * c + 1)
                mm = product(pe, M[m][0:rows.stop - rows.start, :], lambda a: W[:, a, j, rows], lambda a: XT[:, a, j, :],
                             j == 0, j == KD - 1)
                if j == KD - 1:
                    mm.then_inc(M_full[m], 1)

            def dt_project(c, j):
                pe.wait_ge(M_dve[0], 3 * c + 2)
                pe.wait_ge(M_act[1], 3 * c + 2)
                product(pe, M[j][:, :], lambda a: DTW[:, a, j * P:(j + 1) * P], lambda a: DL[:, a, :], True, True)\
                    .then_inc(M_full[j], 1)

            def spread_b(c, q):
                prev = q - RING
                pe.wait_ge(*((b_full, some(POOL_STEPS, c, prev)) if prev % Q in POOL_STEPS else bx_of(c, prev)))
                pe.matmul(BB[q % RING][:, :], SEL[:, q % DSTATE, :], BC[:, :], start=True, stop=True).then_inc(bb_full, 1)

            def spread_c(c, q):
                pe.wait_ge(cy_full, step(c, q - 2))
                pe.matmul(CB[q % 2][:, :], SEL[:, DSTATE + q % DSTATE, :], BC[:, :], start=True, stop=True).then_inc(cb_full, 1)

            def run(c, q):
                if q == 0:
                    pe.wait_ge(bc_full, c + 1)
                    spread_b(c, 0)
                    spread_b(c, 1)
                spread_c(c, q)
                if q + 2 < Q:
                    spread_b(c, q + 2)

            def output(c, last):
                pe.wait_ge(added, step(c, Q - 1))
                if not last:
                    for j in range(KD):
                        pe.wait_ge(M_dve[j], (3 - j) * (c + 2))
                for t in range(CT4):
                    for j in range(KD):
                        at = (t % 2) * DIM + j * P
                        mm = pe.transpose(M[t // 2][:, at:at + P], y[:, j, t * P:(t + 1) * P], ident[:])
                mm.then_inc(yt_full, 1)

            def chunk(c, last=False):
                for cc, q in steps(c, last):
                    run(cc, q)
                    if not last:
                        if q == 1:
                            output(c, last)
                        for first, parts, stage_of in PARTS:
                            if first <= q < first + parts:
                                stage_of(c + 1, q - first)
                if last:
                    output(c, last)

            PARTS = ((9, KD, x_turn), (13, 2 * KD, low_project), (20, KD, dt_project))
            for _, parts, stage_of in PARTS:
                for part in range(parts):
                    stage_of(0, part)
                pe.wait_ge(w_full, 2)
            pe.wait_ge(sel_in, 16)
            for q in range(AHEAD):
                run(0, q)
            with pe.Fori(0, NC - 1) as c:
                chunk(c)
            chunk(NC - 1, last=True)


def self_attention(nc, X, x_kept, x2_kept, d, loads):
    H = 16
    with ExitStack() as ctx:
        k = Kit(nc, ctx, "sa")
        sb, sem, sems = k.sb, k.sem, k.sems
        W = {n: sb(n, [P, 2, KD, H * HD], F32R) for n in ("WQ", "WK", "WV")}
        WO = sb("WO", [P, 2, H, DIM], F32R)
        ident, mask, ln1 = sb("ident", [P, P]), sb("mask", [P, P]), sb("ln1", [P, DIM])
        scrap, eps, mhalf, inv_dim = sb("scrap", [P, 1]), sb("eps", [P, 2, CT4]), sb("mhalf", [P, CT4]), sb("inv_dim", [P, CT4])
        stats, mv, rstd = sb("stats", [P, CT4, 6]), sb("mv", [P, CT4, 2]), sb("rstd", [P, CT4])
        sqs, msq, rr = sb("sqs", [P, DIM]), sb("msq", [P, CT4]), sb("rr", [P, CT4])
        NS = 8
        stage = stages(nc, "sa", NS, 1024)
        xn = sb("xn", [P, CT4, DIM])
        HT = sb("HT", [P, 2, KD, CHUNK], F32R)
        QT, KT = ([sb(f"{n}{j}", [P, 2, CHUNK], F32R) for j in range(2)] for n in ("QT", "KT"))
        V = [sb(f"V{j}", [P, 2, CT4, 2 * HD], F32R) for j in range(2)]
        PRs = sb("PR", [P, 2, CT4, P])
        PR = [PRs[:, j] for j in range(2)]
        nmax, rsum, rinv = sb("nmax", [P, CT4]), sb("rsum", [P, CT4]), sb("rinv", [P, CT4])
        PT, OT = sb("PT", [P, 2, CHUNK], F32R), sb("OT", [P, 2, CHUNK], F32R)
        out_t = xn[:].rearrange("p (k a) n -> p k (a n)", k=KD)
        J = [k.ps(f"J{j}", [P, CHUNK]) for j in range(2)]
        S = [k.ps(f"S{j}", [P, CT4, P]) for j in range(2)]
        T, PO = k.ps("T", [P, CHUNK]), k.ps("PO", [P, CHUNK])
        ACC = [k.ps(f"ACC{j}", [P, CHUNK]) for j in range(KD)]

        x_saved, x2_saved, tab_in, w_hi, w_lo = sem("x_saved"), sem("x2_saved"), sem("tab_in"), sem("w_hi"), sem("w_lo")
        stat_full, mv_full, var_full, rstd_full, h_full, msq_full, rr_full, xn_full = (
            sem(n) for n in ("stat_full", "mv_full", "var_full", "rstd_full", "h_full", "msq_full", "rr_full", "xn_full"))
        J_full, J_act, J_dve = sems("J_full"), sems("J_act"), sems("J_dve")
        T_full, T_act, T_dve = sem("T_full"), sem("T_act"), sem("T_dve")
        S_full, S_mask, nmax_full, exp_full, rinv_full, pr_full = (
            sem(n) for n in ("S_full", "S_mask", "nmax_full", "exp_full", "rinv_full", "pr_full"))
        pv_done, ot_hi, ot_full, wo_done = sem("pv_done"), sem("ot_hi"), sem("ot_full"), sem("wo_done")
        out_hi, x_sum = sem("out_hi"), sem("x_sum")

        pieces = []
        for n, w in (("WQ", "ffn_wq"), ("WK", "ffn_wk"), ("WV", "ffn_wv")):
            v = d[w].rearrange("(k p) n -> p k n", p=P)
            pieces += [(v[:, c, u * 1024:(u + 1) * 1024], lambda a, n=n, c=c, u=u: W[n][:, a, c, u * 1024:(u + 1) * 1024])
                       for c in range(KD) for u in range(2)]
        v = d["ffn_wo"].rearrange("(h p) n -> p h n", p=P)
        pieces += [(v[:, u * 4:(u + 1) * 4, :], lambda a, u=u: WO[:, a, u * 4:(u + 1) * 4, :]) for u in range(4)]

        staged = loads.counts(len(pieces), NS)

        def staging(j):
            view = stage[j % NS]
            return view.rearrange("p (a n) -> p a n", n=DIM) if len(pieces[j][0].shape) == 3 else view

        PER = 3 * H + KD

        def j_use(c, n):
            return n % 2, c * (PER // 2) + n // 2

        def slot_uses(c, h):
            n = 8 + 3 * h + (2 if h >= 14 else 0)
            return [j_use(c, n + u) for u in range(3)]

        def x_uses(c):
            return [j_use(c, 8 + 3 * 14 + u) for u in range(KD)]

        def qk_uses(c, h):
            return slot_uses(c, h)[0:2]

        def v_use(c, h):
            return slot_uses(c, h)[2], (h // 2 + 1) % (H // 2), 2 * (h % 2)

        def done(s):
            return s + 2

        STEP_SIGNALS = {"pe": (S_full, pv_done, wo_done), "dve": (S_mask, nmax_full, rinv_full, ot_full),
                        "act": (exp_full, ot_hi), "pool": (pr_full,)}

        def start(engine, name):
            for signal in STEP_SIGNALS[name]:
                engine.sem_inc(signal, 1)

        block = ctx.enter_context(nc.Block())

        @block.sync
        def _(sp):
            kept = x_kept.rearrange("(t p) n -> p t n", p=P)
            sp.dma_start(kept[:, 0:CT4, :], X[:, 0:CT4, :]).then_inc(x_saved, 16)
            for dst, src in ((ident, d["ident"]), (mask, d["smask"]), (ln1, d["ln1"].partition_broadcast(P))):
                sp.dma_start(dst[:], src).then_inc(tab_in, 16)
            for j, (src, _) in enumerate(pieces):
                if j >= NS:
                    sp.wait_ge(w_lo, j - NS + 1)
                sp.dma_start(staging(j), src).then_inc(staged[j][0], 16)
            sp.dma_start(kept[:, CT4:, :], X[:, CT4:, :]).then_inc(x_saved, 16)
            with sp.Fori(0, NC) as c:
                sp.wait_ge(x_sum, 2 * c + 2)
                sp.dma_start(x2_kept.rearrange("(t p) n -> p t n", p=P)[:, bass.ds(c * CT4, CT4), :], tokens(X, c)).then_inc(x2_saved, 16)
            sp.wait_ge(x2_saved, 16 * NC)

        @block.scalar
        def _(act):
            start(act, "act")

            def squares(c):
                act.wait_ge(h_full, c + 1)
                for t in range(CT4):
                    x = X[:, t, :] if isinstance(c, int) else tile_of(X, c, t)
                    act.activation(sqs[:], x, ACT.Square, accum_out=msq[:, t:t + 1]).then_inc(msq_full, 1)
                    if t < CT4 - 1:
                        act.wait_ge(msq_full, 4 * c + (t + 1))

            def x_split(uses):
                for j, (bank, n) in enumerate(uses):
                    act.wait_ge(J_full[bank], n + 1)
                    act.activation(HT[:, HI, j, :], J[bank][:, :], ACT.Copy).then_inc(J_act[bank], 1)

            def qk_split(use, u, par):
                bank, n = use
                act.wait_ge(J_full[bank], n + 1)
                act.activation((QT, KT)[u][par][:, HI], J[bank][:, :], ACT.Copy, scale=(HD ** -0.5, 1.0)[u]).then_inc(J_act[bank], 1)

            def v_split(v_use):
                (bank, n), pair, t = v_use
                act.wait_ge(J_full[bank], n + 1)
                act.activation(V[pair % 2][:, HI, t:t + 2, :], J[bank][:, :].rearrange("p (a n) -> p a n", a=2),
                               ACT.Copy).then_inc(J_act[bank], 1)

            def exps(s, par):
                act.wait_ge(nmax_full, done(s))
                for t in range(CT4):
                    last = act.activation(PR[par][:, t, :], S[par][:, t, :], ACT.Exp, bias=nmax[:, t:t + 1], accum_out=rsum[:, t:t + 1])
                last.then_inc(exp_full, 1)

            def slot(c, h, last):
                s, more = c * H + h, not (last and h >= 14)
                if h == 14 and more:
                    x_split(x_uses(c))
                act.wait_ge(T_full, c * (H + 1) + (h + 1))
                act.activation(PT[:, HI], T[:, :], ACT.Copy).then_inc(T_act, 1)
                if not (last and h == 15):
                    act.wait_ge(pv_done, s + 1)
                    exps(s + 1, (h + 1) % 2)
                if more:
                    act.wait_ge(S_full, done(s))
                    for u in range(2):
                        qk_split(qk_uses(c, h)[u], u, h % 2)
                act.wait_ge(pv_done, done(s))
                act.wait_ge(wo_done, s + 1)
                act.activation(OT[:, HI], PO[:, :], ACT.Copy).then_inc(ot_hi, 1)
                if more:
                    v_split(v_use(c, h))
                if h == 11 and not last:
                    squares(c + 1)

            def chunk(c, last=False):
                for h in range(H):
                    slot(c, h, last)
                act.wait_ge(wo_done, done(c * H + (H - 1)))
                for j in range(KD):
                    act.activation(out_t[:, j, :], ACC[j][:, :], ACT.Copy).then_inc(out_hi, 1)

            squares(0)
            for j, (_, dst) in enumerate(pieces):
                act.wait_ge(*staged[j])
                act.activation(dst(HI), staging(j), ACT.Copy).then_inc(w_hi, 1)
            x_split(x_uses(-1))
            for h in (14, 15):
                for u in range(2):
                    qk_split(qk_uses(-1, h)[u], u, h % 2)
                v_split(v_use(-1, h))
            exps(0, 0)
            with act.Fori(0, NC - 1) as c:
                chunk(c)
            chunk(NC - 1, last=True)

        @block.vector
        def _(dve):
            start(dve, "dve")

            def tile(buf, c, t):
                return buf[:, c * CT4 + t, :] if isinstance(c, int) else tile_of(buf, c, t)

            def norm_stats(c):
                for t in range(CT4):
                    last = dve.bn_stats(stats[:, t, :], tile(X, c, t))
                last.then_inc(stat_full, 1)

            def norm_var(c):
                dve.wait_ge(stat_full, c + 1)
                dve.memset(scrap[:], 0.0)
                for t in range(CT4):
                    last = dve.bn_aggr(mv[:, t, :], stats[:, t, :])
                last.then_inc(mv_full, 1)

            def norm_apply(c):
                dve.wait_ge(rstd_full, c + 1)
                dve.memset(scrap[:], 0.0)
                for t in range(CT4):
                    last = dve.tensor_scalar(tile(X, c, t), tile(X, c, t), mv[:, t, 0:1], rstd[:, t:t + 1], ALU.subtract, ALU.mult)
                last.then_inc(h_full, 1)

            def rms_apply(c):
                dve.wait_ge(rr_full, c + 1)
                dve.memset(scrap[:], 0.0)
                for t in range(CT4):
                    last = dve.scalar_tensor_tensor(xn[:, t, :], tile(X, c, t), rr[:, t:t + 1], ln1[:], ALU.mult, ALU.mult)
                last.then_inc(xn_full, 1)

            def x_split(uses):
                for j, (bank, n) in enumerate(uses):
                    dve.wait_ge(J_act[bank], n + 1)
                    dve.tensor_tensor(HT[:, LO, j, :], J[bank][:, :], HT[:, HI, j, :], ALU.subtract).then_inc(J_dve[bank], 1)

            def qk_split(uses, par, first=0):
                for u, (bank, n) in enumerate(uses, first):
                    buf = (QT, KT)[u][par]
                    dve.wait_ge(J_act[bank], n + 1)
                    dve.scalar_tensor_tensor(buf[:, LO], J[bank][:, :], (HD ** -0.5, 1.0)[u], buf[:, HI],
                                             ALU.mult, ALU.subtract).then_inc(J_dve[bank], 1)

            def v_split(v_use):
                (bank, n), pair, t = v_use
                dve.wait_ge(J_act[bank], n + 1)
                dve.tensor_tensor(V[pair % 2][:, LO, t:t + 2, :], J[bank][:, :].rearrange("p (a n) -> p a n", a=2),
                                  V[pair % 2][:, HI, t:t + 2, :], ALU.subtract).then_inc(J_dve[bank], 1)

            def maxima(s, par):
                dve.wait_ge(S_full, done(s))
                dve.tensor_tensor(S[par][:, :, :], S[par][:, :, :], mask[:, None, :].broadcast_to([P, CT4, P]),
                                  ALU.add).then_inc(S_mask, 1)
                dve.wait_ge(S_mask, done(s))
                dve.tensor_reduce(nmax[:], S[par][:, :, :], AX.X, ALU.max, negate=True).then_inc(nmax_full, 1)

            def inverse(s):
                dve.wait_ge(exp_full, done(s))
                dve.wait_ge(pr_full, s + 1)
                dve.reciprocal(rinv[:], rsum[:]).then_inc(rinv_full, 1)

            def slot(c, h, last):
                s, more = c * H + h, not (last and h >= 14)
                if not (last and h == 15):
                    maxima(s + 1, (h + 1) % 2)
                if h == 14 and more:
                    x_split(x_uses(c))
                dve.wait_ge(T_act, s + 1)
                dve.tensor_tensor(PT[:, LO], T[:, :], PT[:, HI], ALU.subtract).then_inc(T_dve, 1)
                if more:
                    qk_split(qk_uses(c, h)[0:1], h % 2)
                if not (last and h == 15):
                    inverse(s + 1)
                if more:
                    qk_split(qk_uses(c, h)[1:2], h % 2, 1)
                dve.wait_ge(ot_hi, done(s))
                dve.tensor_tensor(OT[:, LO], PO[:, :], OT[:, HI], ALU.subtract).then_inc(ot_full, 1)
                if more:
                    v_split(v_use(c, h))
                if not last:
                    for at, stage_of in ((8, norm_stats), (9, norm_var), (10, norm_apply), (12, rms_apply)):
                        if h == at:
                            stage_of(c + 1)

            def chunk(c, last=False):
                for h in range(H):
                    slot(c, h, last)
                dve.wait_ge(T_full, (c + 1) * (H + 1))
                for u, bank in ((0, T), (1, PO)):
                    x = X[:, c * CT4 + 2 * u:c * CT4 + 2 * u + 2, :] if last else tokens(X, c, 2 * u, 2)
                    dve.tensor_tensor(x, bank[:, :].rearrange("p (a n) -> p a n", a=2), x, ALU.add).then_inc(x_sum, 1)

            norm_stats(0)
            norm_var(0)
            dve.wait_ge(x_saved, 16)
            norm_apply(0)
            for j, (_, dst) in enumerate(pieces):
                dve.wait_ge(w_hi, j + 1)
                dve.tensor_tensor(dst(LO), staging(j), dst(HI), ALU.subtract).then_inc(w_lo, 1)
            dve.wait_ge(tab_in, 3 * 16)
            dve.wait_ge(w_lo, len(pieces))
            rms_apply(0)
            x_split(x_uses(-1))
            for h in (14, 15):
                qk_split(qk_uses(-1, h), h % 2)
                v_split(v_use(-1, h))
            maxima(0, 0)
            dve.wait_ge(exp_full, done(0))
            dve.reciprocal(rinv[:], rsum[:]).then_inc(rinv_full, 1)
            dve.wait_ge(x_saved, 2 * 16)
            with dve.Fori(0, NC - 1) as c:
                chunk(c)
            chunk(NC - 1, last=True)

        @block.gpsimd
        def _(pool):
            start(pool, "pool")
            pool.memset(inv_dim[:], 1.0 / DIM)
            pool.memset(eps[:, 0, :], 1e-5)
            pool.memset(eps[:, 1, :], 1e-6)
            pool.memset(mhalf[:], -0.5).then_inc(var_full, 1)
            pool.wait_ge(var_full, 1)

            def ln_rstd(c):
                pool.wait_ge(mv_full, c + 1)
                pool.tensor_tensor(rstd[:], mv[:, :, 1], eps[:, 0, :], ALU.add).then_inc(var_full, 1)
                pool.wait_ge(var_full, 3 * c + 2)
                pool.tensor_tensor(rstd[:], rstd[:], mhalf[:], ALU.pow).then_inc(rstd_full, 1)

            def rms_rstd(c):
                pool.wait_ge(msq_full, 4 * c + 4)
                pool.tensor_tensor(rr[:], msq[:], inv_dim[:], ALU.mult).then_inc(var_full, 1)
                pool.wait_ge(var_full, 3 * c + 3)
                pool.tensor_tensor(rr[:], rr[:], eps[:, 1, :], ALU.add).then_inc(var_full, 1)
                pool.wait_ge(var_full, 3 * c + 4)
                pool.tensor_tensor(rr[:], rr[:], mhalf[:], ALU.pow).then_inc(rr_full, 1)

            def normalise(s, par):
                pool.wait_ge(rinv_full, done(s))
                pool.tensor_tensor(PR[par][:], PR[par][:], rinv[:, :, None].broadcast_to([P, CT4, P]), ALU.mult).then_inc(pr_full, 1)

            def chunk(c, last=False):
                for h in range(H):
                    if not (last and h == 15):
                        normalise(c * H + (h + 1), (h + 1) % 2)
                    if h == 9 and not last:
                        ln_rstd(c + 1)
                    if h == 11 and not last:
                        rms_rstd(c + 1)

            ln_rstd(0)
            rms_rstd(0)
            normalise(0, 0)
            with pool.Fori(0, NC - 1) as c:
                chunk(c)
            chunk(NC - 1, last=True)

        @block.tensor
        def _(pe):
            start(pe, "pe")

            def x_turn(uses, c):
                pe.wait_ge(xn_full, c + 1)
                for j, (bank, n) in enumerate(uses):
                    pe.wait_ge(J_dve[bank], n)
                    for t in range(CT4):
                        mm = pe.transpose(J[bank][:, t * P:(t + 1) * P], xn[:, t, j * P:(j + 1) * P], ident[:])
                    mm.then_inc(J_full[bank], 1)

            def qk_project(uses, h):
                for u, (bank, n) in enumerate(uses):
                    pe.wait_ge(J_dve[bank], n)
                    w = W[("WQ", "WK")[u]]
                    for j in range(KD):
                        mm = product(pe, J[bank][:, :], lambda a: w[:, a, j, h * HD:(h + 1) * HD], lambda a: HT[:, a, j, :],
                                     j == 0, j == KD - 1)
                    mm.then_inc(J_full[bank], 1)

            def v_project(v_use):
                (bank, n), pair, t = v_use
                pe.wait_ge(J_dve[bank], n)
                for u in range(2):
                    at = slice((t + u) * P, (t + u + 1) * P)
                    for j in range(KD):
                        mm = product(pe, J[bank][:, u * 2 * HD:(u + 1) * 2 * HD], lambda a: HT[:, a, j, at],
                                     lambda a: W["WV"][:, a, j, pair * 2 * HD:(pair + 1) * 2 * HD], j == 0, j == KD - 1)
                mm.then_inc(J_full[bank], 1)

            def scores(uses, s, par):
                for bank, n in uses:
                    pe.wait_ge(J_dve[bank], n + 1)
                for t in range(CT4):
                    mm = product(pe, S[par][:, t, :], lambda a: QT[par][:, a, t * P:(t + 1) * P],
                                 lambda a: KT[par][:, a, t * P:(t + 1) * P], True, True)
                mm.then_inc(S_full, 1)

            def slot(c, h, last):
                s, par, more = c * H + h, h % 2, not (last and h >= 14)
                if not (last and h == 15):
                    scores(qk_uses(c, h - 1), s + 1, 1 - par)
                if h == 14 and more:
                    x_turn(x_uses(c), c + 1)
                pe.wait_ge(pr_full, done(s))
                for t in range(CT4):
                    mm = pe.transpose(T[:, t * P:(t + 1) * P], PR[par][:, t, :], ident[:])
                mm.then_inc(T_full, 1)
                if h == 14 and more:
                    for bank, n in x_uses(c):
                        pe.wait_ge(J_dve[bank], n + 1)
                if more:
                    qk_project(qk_uses(c, h), (h + 2) % H)
                pe.wait_ge(T_dve, s + 1)
                pe.wait_ge(ot_full, s + 1)
                for t in range(CT4):
                    mm = product(pe, PO[:, t * P:(t + 1) * P], lambda a: V[h // 2 % 2][:, a, t, h % 2 * HD:(h % 2 + 1) * HD],
                                 lambda a: PT[:, a, t * P:(t + 1) * P], True, True)
                mm.then_inc(pv_done, 1)
                if more:
                    v_project(v_use(c, h))
                pe.wait_ge(ot_full, done(s))
                for j in range(KD):
                    mm = product(pe, ACC[j][:, :], lambda a: WO[:, a, h, j * P:(j + 1) * P], lambda a: OT[:, a, :], h == 0, h == H - 1)
                mm.then_inc(wo_done, 1)

            def chunk(c, last=False):
                for h in range(H):
                    slot(c, h, last)
                pe.wait_ge(out_hi, 2 * c + 2)
                for t in range(CT4):
                    for j in range(KD):
                        mm = pe.transpose((T, PO)[t // 2][:, (t % 2) * DIM + j * P:(t % 2) * DIM + (j + 1) * P],
                                          out_t[:, j, t * P:(t + 1) * P], ident[:])
                mm.then_inc(T_full, 1)
                pe.wait_ge(x_sum, 2 * c + 2)

            pe.wait_ge(tab_in, 3 * 16)
            x_turn(x_uses(-1), 0)
            pe.wait_ge(w_lo, len(pieces))
            for bank, n in x_uses(-1):
                pe.wait_ge(J_dve[bank], n + 1)
            for h in (14, 15):
                qk_project(qk_uses(-1, h), h - 14)
                v_project(v_use(-1, h))
            scores(qk_uses(-1, 14), 0, 0)
            with pe.Fori(0, NC - 1) as c:
                chunk(c)
            chunk(NC - 1, last=True)


EXPERTS, TOPK, INNER, SHARED = 16, 6, 176, 352
ROWS = EXPERTS * INNER
NE = (ROWS + SHARED + P - 1) // P


def mixture_of_experts(nc, x_kept, x2_kept, d, out, loads):
    with ExitStack() as ctx:
        k = Kit(nc, ctx, "me")
        sb, sem, sems = k.sb, k.sem, k.sems
        WG, WU = (sb(n, [P, 2, KD, NE * P], F32R) for n in ("WG", "WU"))
        WD = sb("WD", [P, 2, NE, DIM], F32R)
        WR = sb("WR", [P, KD, EXPERTS])
        SEL = sb("SEL", [64, NE, P], F32R)
        ident, ln2, tri = sb("ident", [P, P]), sb("ln2", [P, DIM]), sb("tri", [P, EXPERTS * EXPERTS])
        eps, mhalf, inv_dim = (sb(n, [P, CT4]) for n in ("eps", "mhalf", "inv_dim"))
        x2 = sb("x2", [P, CT4, DIM])
        msq, rr = sb("msq", [P, CT4]), sb("rr", [P, CT4])
        cw = sb("cw", [P, CT4, 32])
        sg, hu, hw = (sb(n, [P, CHUNK]) for n in ("sg", "hu", "hw"))
        NS = 7
        stage = stages(nc, "me", NS, 1024)
        xs, xn = (sb(n, [P, CT4, DIM]) for n in ("xs", "xn"))
        XF = sb("XF", [P, KD, CHUNK])
        HT = sb("HT", [P, 2, KD, CHUNK], F32R)
        HH = [sb(f"HH{j}", [P, 2, CHUNK], F32R) for j in range(2)]
        top, total, inv = sb("top", [P, CT4]), sb("total", [P, CT4]), sb("inv", [P, CT4])
        prob, pick, rank, ties = (sb(n, [P, CT4, EXPERTS]) for n in ("prob", "pick", "rank", "ties"))
        CWS = sb("CWS", [64, CHUNK], F32R)
        beats = xn[:].rearrange("p a (e f) -> p a e f", f=EXPERTS)
        out_t = xn[:].rearrange("p (k a) n -> p k (a n)", k=KD)
        G, U, C = ([k.ps(f"{n}{j}", [P, CHUNK]) for j in range(2)] for n in "GUC")
        ACC = [k.ps(f"ACC{j}", [P, CHUNK]) for j in range(KD)]

        tab_in, sel_in, w_hi, w_lo = sem("tab_in"), sem("sel_in"), sem("w_hi"), sem("w_lo")
        x2_in, xk_in, xs_full, res_full, stored = (sem(n) for n in ("x2_in", "xk_in", "xs_full", "res_full", "stored"))
        msq_full, rr_full, xn_full = (sem(n) for n in ("msq_full", "rr_full", "xn_full"))
        full = {r: sems(f"{r}_full") for r in "GUC"}
        x_copied = sem("x_copied")
        sg_full, hu_full, hw_full, hh_hi, hh_full, down_done = (
            sem(n) for n in ("sg_full", "hu_full", "hw_full", "hh_hi", "hh_full", "down_done"))
        top_full, prob_full, router, cws_hi, cws_full = (
            sem(n) for n in ("top_full", "prob_full", "router", "cws_hi", "cws_full"))
        out_hi, back_full, cw_set = sem("out_hi"), sem("back_full"), sem("cw_set")
        ht_hi, ht_full = sem("ht_hi"), sem("ht_full")
        LINKS = 12

        pieces = []
        for n, W, first in (("wg", WG, 0), ("wu", WU, 0)):
            v = d[n].rearrange("(k p) n -> p k n", p=P)
            pieces += [(v[:, c, u * 800:(u + 1) * 800], lambda a, W=W, c=c, u=u: W[:, a, c, u * 800:(u + 1) * 800])
                       for c in range(KD) for u in range(4)]
        v = d["wd"].rearrange("(e p) n -> p e n", p=P)
        pieces += [(v[:, u:min(u + 4, NE), :], lambda a, u=u: WD[:, a, u:min(u + 4, NE), :]) for u in range(0, NE, 4)]

        staged = loads.counts(len(pieces), NS)

        def staging(j):
            src = pieces[j][0]
            n = int(np.prod(src.shape[1:]))
            view = stage[j % NS][:, 0:n]
            return view.rearrange("p (a n) -> p a n", n=DIM) if len(src.shape) == 3 else view

        X_SLOT, LOGIT_SLOT = 14, 16
        plan = {r: [] for r in "GUC"}
        for e in [23, 24] + list(range(23)):
            if e == 23:
                plan["G"] += ["cw"]
            if e == X_SLOT:
                plan["G"] += ["x"]
                plan["U"] += ["x"]
            if e == LOGIT_SLOT:
                plan["G"] += ["logits"]
            for r in "GUC":
                plan[r] += [(e + 2) % NE]
        bank_of = {(r, name): n % 2 for r in "GUC" for n, name in enumerate(plan[r])}
        index_of = {(r, name): n // 2 for r in "GUC" for n, name in enumerate(plan[r])}
        uses_of = {r: [len(plan[r][b::2]) for b in range(2)] for r in "GUC"}
        ahead = {"G": ["x", "logits"], "U": ["x"], "C": []}

        def early(r, bank):
            return [name for name in ahead[r] if bank_of[r, name] == bank]

        def use(r, name, c):
            bank = bank_of[r, name]
            if isinstance(c, int) and c < 0:
                return bank, early(r, bank).index(name)
            skipped = 0
            if isinstance(c, int) and c == NC - 1:
                skipped = sum(m in ("x", "logits") for m in plan[r][bank:plan[r].index(name):2])
            return bank, c * uses_of[r][bank] + (index_of[r, name] + len(early(r, bank)) - skipped)

        def done(s):
            return s + 2

        def freed(r, name, c):
            if name == "x":
                return x_copied, 2 * (c + 1) + {"G": 1, "U": 2}[r]
            if name in ("logits", "cw"):
                return {"logits": (prob_full, c + 2), "cw": (cws_full, c + 1)}[name]
            return {"G": sg_full, "U": hu_full, "C": hw_full}[r], done(c * NE + name)

        def free(pe, r, name, c):
            bank, at = bank_of[r, name], plan[r].index(name)
            if isinstance(c, int) and c < 0:
                before = early(r, bank)[:early(r, bank).index(name)]
            elif at >= 2:
                before = [m for m in plan[r][bank:at:2] if not (m in ("x", "logits") and isinstance(c, int) and c == NC - 1)]
            elif isinstance(c, int) and c == 0:
                before, c = early(r, bank), -1
            else:
                before, c = plan[r][bank::2], c - 1
            if before:
                pe.wait_ge(*freed(r, before[-1], c))
            return bank

        def after(c, e):
            return (c + 1, e - NE) if e >= NE else (c, e)

        block = ctx.enter_context(nc.Block())

        @block.sync
        def _(sp):
            kept = [b.rearrange("(c t p) n -> p c t n", p=P, t=CT4) for b in (x2_kept, x_kept, out)]

            def rows(b, c):
                return kept[b][:, bass.ds(c, 1), :, :].rearrange("p c t n -> p (c t) n")

            sp.dma_start(x2[:], rows(0, 0)).then_inc(x2_in, 16)
            for dst, src in ((ident, d["ident"]), (ln2, d["ln2"].partition_broadcast(P)), (tri, d["tri"].partition_broadcast(P)),
                             (WR, d["wr"].rearrange("(k p) n -> p k n", p=P))):
                sp.dma_start(dst[:], src).then_inc(tab_in, 16)
            for j, (src, _) in enumerate(pieces):
                if j >= NS:
                    sp.wait_ge(w_lo, j - NS + 1)
                sp.dma_start(staging(j), src).then_inc(staged[j][0], 16)
            sp.wait_ge(w_lo, len(pieces))
            sp.dma_start(xs[:], rows(1, 0)).then_inc(xk_in, 16)
            with sp.Fori(0, NC - 1) as c:
                sp.wait_ge(xs_full, c + 1)
                sp.dma_start(x2[:], rows(0, c + 1)).then_inc(x2_in, 16)
                sp.wait_ge(res_full, 2 * c + 4)
                sp.dma_start(rows(2, c), xs[:]).then_inc(stored, 16)
                sp.wait_ge(stored, 16 * c + 16)
                sp.dma_start(xs[:], rows(1, c + 1)).then_inc(xk_in, 16)
            sp.wait_ge(res_full, 2 * NC + 2)
            sp.dma_start(rows(2, NC - 1), xs[:]).then_inc(stored, 16)
            sp.wait_ge(stored, 16 * NC)

        @block.scalar
        def _(act):
            act.sem_inc(sg_full, 1)
            act.sem_inc(hh_hi, 1)

            def squares(c, squared):
                act.wait_ge(x2_in, 16 * c + 16)
                for t in range(CT4):
                    act.activation(squared, x2[:, t, :], ACT.Square, accum_out=msq[:, t:t + 1]).then_inc(msq_full, 1)
                    act.wait_ge(msq_full, 4 * c + (t + 1))

            def x_copy(c):
                for j, (r, B) in enumerate((("G", G), ("U", U))):
                    bank, n = use(r, "x", c - 1)
                    act.wait_ge(full[r][bank], n + 1)
                    act.activation(XF[:, j, :], B[bank][:, :], ACT.Copy).then_inc(x_copied, 1)

            def x_split(c):
                for j in range(KD):
                    act.activation(HT[:, HI, j, :], XF[:, j, :], ACT.Copy).then_inc(ht_hi, 1)

            def route(c):
                bank, n = use("G", "logits", c - 1)
                act.wait_ge(top_full, c + 1)
                for t in range(CT4):
                    last = act.activation(prob[:, t, :], G[bank][:, t * EXPERTS:(t + 1) * EXPERTS], ACT.Exp, bias=top[:, t:t + 1],
                                          accum_out=total[:, t:t + 1])
                last.then_inc(prob_full, 1)

            def cw_split(c):
                bank, n = use("G", "cw", c)
                act.wait_ge(full["G"][bank], n + 1)
                act.activation(CWS[0:32, :], G[bank][0:32, :], ACT.Copy).then_inc(cws_hi, 1)

            def gate(c, e):
                bank, n = use("G", e, c)
                act.wait_ge(full["G"][bank], n + 1)
                act.wait_ge(hu_full, done(c * NE + (e - 1)))
                act.activation(sg[:], G[bank][:, :], ACT.Silu).then_inc(sg_full, 1)

            def high(c, e):
                act.wait_ge(down_done, done(c * NE + (e - 1 if e == 0 else e - 2)))
                act.wait_ge(hw_full, done(c * NE + e))
                act.activation(HH[e % 2][:, HI], hw[:], ACT.Copy).then_inc(hh_hi, 1)

            def chunk(c, last=False):
                for e in range(NE):
                    if e == X_SLOT + 1 and not last:
                        x_copy(c + 1)
                    if e == LOGIT_SLOT + 1 and not last:
                        route(c + 1)
                    if not (last and e == NE - 1):
                        gate(*after(c, e + 1))
                    if e == 23 and not last:
                        bank, n = use("U", NE - 1, c)
                        act.wait_ge(full["U"][bank], n + 1)
                        x_split(c + 1)
                        cw_split(c + 1)
                    if not (last and e == NE - 1):
                        high(*after(c, e + 1))
                    if e == 9 and not last:
                        act.wait_ge(back_full, c + 1)
                        squares(c + 1, xn[:, 0, :])
                act.wait_ge(down_done, done(c * NE + (NE - 1)))
                for j in range(KD):
                    act.activation(out_t[:, j, :], ACC[j][:, :], ACT.Copy).then_inc(out_hi, 1)

            squares(0, hu[:, 0:DIM])
            for j, (_, dst) in enumerate(pieces):
                act.wait_ge(*staged[j])
                act.activation(dst(HI), staging(j), ACT.Copy).then_inc(w_hi, 1)
            x_copy(0)
            for j in range(KD):
                act.wait_ge(x_copied, j + 1)
            x_split(0)
            route(0)
            cw_split(0)
            gate(0, 0)
            high(0, 0)
            with act.Fori(0, NC - 1) as c:
                chunk(c)
            chunk(NC - 1, last=True)

        @block.vector
        def _(dve):
            dve.sem_inc(hu_full, 1)
            dve.sem_inc(hw_full, 1)
            dve.sem_inc(res_full, 2)

            def rms_apply(c):
                dve.wait_ge(rr_full, 3 * c + 3)
                for t in range(CT4):
                    last = dve.scalar_tensor_tensor(xn[:, t, :], x2[:, t, :], rr[:, t:t + 1], ln2[:], ALU.mult, ALU.mult)
                last.then_inc(xn_full, 1)

            def x_split(c):
                for j in range(KD):
                    dve.wait_ge(ht_hi, 2 * c + (j + 1))
                    dve.tensor_tensor(HT[:, LO, j, :], XF[:, j, :], HT[:, HI, j, :], ALU.subtract).then_inc(ht_full, 1)

            def top_logit(c):
                bank, n = use("G", "logits", c - 1)
                dve.wait_ge(full["G"][bank], n + 1)
                dve.tensor_reduce(top[:], G[bank][:, 0:CT4 * EXPERTS].rearrange("p (t e) -> p t e", t=CT4), AX.X, ALU.max,
                                  negate=True).then_inc(top_full, 1)

            four = [P, CT4, EXPERTS, EXPERTS]
            other, own = prob[:, :, None, :].broadcast_to(four), prob[:, :, :, None].broadcast_to(four)

            def link(c, n, ins):
                ins.then_inc(router, 1)
                dve.wait_ge(router, LINKS * c + n)

            def route_rank(c):
                dve.wait_ge(prob_full, c + 1)
                link(c, 1, dve.reciprocal(inv[:], total[:]))
                link(c, 2, dve.tensor_tensor(prob[:], prob[:], inv[:, :, None].broadcast_to(four[:3]), ALU.mult))
                link(c, 3, dve.tensor_tensor(beats, other, own, ALU.is_gt))
                link(c, 4, dve.tensor_reduce(rank[:], beats, AX.X, ALU.add))

            def route_ties(c):
                link(c, 5, dve.tensor_tensor(beats, other, own, ALU.is_equal))
                link(c, 6, dve.tensor_tensor(beats, beats, tri[:, None, :].broadcast_to([P, CT4, EXPERTS * EXPERTS])
                                             .rearrange("p t (e f) -> p t e f", f=EXPERTS), ALU.mult))

            def route_weights(c):
                link(c, 7, dve.tensor_reduce(ties[:], beats, AX.X, ALU.add))
                link(c, 8, dve.tensor_tensor(rank[:], rank[:], ties[:], ALU.add))
                link(c, 9, dve.scalar_tensor_tensor(pick[:], rank[:], float(TOPK), prob[:], ALU.is_lt, ALU.mult))
                link(c, 10, dve.tensor_reduce(total[:], pick[:], AX.X, ALU.add))
                link(c, 11, dve.reciprocal(inv[:], total[:]))
                link(c, 12, dve.tensor_tensor(cw[:, :, 0:EXPERTS], pick[:], inv[:, :, None].broadcast_to(four[:3]), ALU.mult))

            def cw_split(c):
                dve.wait_ge(cws_hi, c + 1)
                dve.tensor_tensor(CWS[32:64, :], G[bank_of["G", "cw"]][0:32, :], CWS[0:32, :], ALU.subtract).then_inc(cws_full, 1)

            def scale(c, e):
                s = c * NE + e
                (bu, nu), (bc, n_c) = use("U", e, c), use("C", e, c)
                dve.wait_ge(full["U"][bu], nu + 1)
                dve.wait_ge(hw_full, done(c * NE + (e - 1)))
                dve.wait_ge(sg_full, done(s))
                dve.tensor_tensor(hu[:], U[bu][:, :], sg[:], ALU.mult).then_inc(hu_full, 1)
                dve.wait_ge(full["C"][bc], n_c + 1)
                dve.wait_ge(hh_full, done(c * NE + (e - 1)))
                dve.wait_ge(hu_full, done(s))
                dve.tensor_tensor(hw[:], C[bc][:, :], hu[:], ALU.mult).then_inc(hw_full, 1)

            def chunk(c, last=False):
                for e in range(NE):
                    if e == LOGIT_SLOT + 1 and not last:
                        top_logit(c + 1)
                    if e == 23 and not last:
                        x_split(c + 1)
                    if not (last and e == NE - 1):
                        scale(*after(c, e + 1))
                    if not last:
                        for at, stage_of in ((X_SLOT - 2, rms_apply), (LOGIT_SLOT + 2, route_rank), (LOGIT_SLOT + 3, route_ties),
                                             (LOGIT_SLOT + 4, route_weights), (23, cw_split)):
                            if e == at:
                                stage_of(c + 1)
                dve.wait_ge(back_full, c + 2)
                dve.wait_ge(xs_full, c + 1)
                for u in range(2):
                    rows = xs[:, 2 * u:2 * u + 2, :]
                    dve.tensor_tensor(rows, ACC[u][:, :].rearrange("p (a n) -> p a n", a=2), rows, ALU.add).then_inc(res_full, 1)

            for j, (_, dst) in enumerate(pieces):
                dve.wait_ge(w_hi, j + 1)
                dve.tensor_tensor(dst(LO), staging(j), dst(HI), ALU.subtract).then_inc(w_lo, 1)
            dve.wait_ge(w_lo, len(pieces))
            dve.wait_ge(cw_set, 2)
            rms_apply(0)
            for stage_of in (x_split, top_logit, route_rank, route_ties, route_weights, cw_split):
                stage_of(0)
            scale(0, 0)
            with dve.Fori(0, NC - 1) as c:
                chunk(c)
            chunk(NC - 1, last=True)

        @block.gpsimd
        def _(pool):
            pool.dma_start(SEL[:], d["sel_e"]).then_inc(sel_in, 16)
            pool.sem_inc(hh_full, 1)
            pool.memset(inv_dim[:], 1.0 / DIM)
            pool.memset(eps[:], 1e-6)
            pool.memset(mhalf[:], -0.5)
            pool.memset(cw[:], 0.0).then_inc(cw_set, 1)
            pool.wait_ge(cw_set, 1)
            pool.memset(cw[:, :, EXPERTS:EXPERTS + 1], 1.0).then_inc(cw_set, 1)

            def rms_rstd(c):
                pool.wait_ge(msq_full, 4 * c + 4)
                pool.tensor_tensor(rr[:], msq[:], inv_dim[:], ALU.mult).then_inc(rr_full, 1)
                pool.wait_ge(rr_full, 3 * c + 1)
                pool.tensor_tensor(rr[:], rr[:], eps[:], ALU.add).then_inc(rr_full, 1)
                pool.wait_ge(rr_full, 3 * c + 2)
                pool.tensor_tensor(rr[:], rr[:], mhalf[:], ALU.pow).then_inc(rr_full, 1)

            def low(c, e):
                pool.wait_ge(hh_hi, done(c * NE + e))
                pool.tensor_tensor(HH[e % 2][:, LO], hw[:], HH[e % 2][:, HI], ALU.subtract).then_inc(hh_full, 1)

            def chunk(c, last=False):
                for e in range(NE):
                    if not (last and e == NE - 1):
                        low(*after(c, e + 1))
                    if e == 4:
                        pool.wait_ge(x2_in, 16 * c + 16)
                        pool.wait_ge(xk_in, 16 * c + 16)
                        pool.tensor_tensor(xs[:], x2[:], xs[:], ALU.add).then_inc(xs_full, 1)
                    if e == 10 and not last:
                        rms_rstd(c + 1)

            rms_rstd(0)
            low(0, 0)
            with pool.Fori(0, NC - 1) as c:
                chunk(c)
            chunk(NC - 1, last=True)

        @block.tensor
        def _(pe):
            pe.sem_inc(down_done, 1)
            pe.sem_inc(back_full, 1)

            def x_turn(c):
                pe.wait_ge(xn_full, c + 1)
                for j, (r, B) in enumerate((("G", G), ("U", U))):
                    bank = free(pe, r, "x", c - 1)
                    for t in range(CT4):
                        mm = pe.transpose(B[bank][:, t * P:(t + 1) * P], xn[:, t, j * P:(j + 1) * P], ident[:])
                    mm.then_inc(full[r][bank], 1)

            def logits(c):
                bank = free(pe, "G", "logits", c - 1)
                pe.wait_ge(x_copied, 2 * c + 2)
                for t in range(CT4):
                    for j in range(KD):
                        mm = pe.matmul(G[bank][:, t * EXPERTS:(t + 1) * EXPERTS], XF[:, j, t * P:(t + 1) * P], WR[:, j, :],
                                       start=j == 0, stop=j == KD - 1)
                mm.then_inc(full["G"][bank], 1)

            def gates(c, e):
                if e == 0:
                    pe.wait_ge(ht_full, 2 * c + 2)
                for r, B, W in (("G", G, WG), ("U", U, WU)):
                    bank = free(pe, r, e, c)
                    for j in range(KD):
                        mm = product(pe, B[bank][:, :], lambda a: W[:, a, j, e * P:(e + 1) * P], lambda a: HT[:, a, j, :],
                                     j == 0, j == KD - 1)
                    mm.then_inc(full[r][bank], 1)

            def cw_turn(c):
                bank = free(pe, "G", "cw", c)
                pe.wait_ge(router, LINKS * c + LINKS)
                for t in range(CT4):
                    mm = pe.transpose(G[bank][0:32, t * P:(t + 1) * P], cw[:, t, :], ident[:])
                mm.then_inc(full["G"][bank], 1)

            def spread(c, e):
                if e == 0:
                    pe.wait_ge(cws_full, c + 1)
                bank = free(pe, "C", e, c)
                pe.matmul(C[bank][:, :], SEL[:, e, :], CWS[:, :], start=True, stop=True).then_inc(full["C"][bank], 1)

            def down(c, e):
                s = c * NE + e
                pe.wait_ge(hh_full, done(s))
                if e == 0:
                    pe.wait_ge(res_full, 2 * c + 2)
                for j in range(KD):
                    mm = product(pe, ACC[j][:, :], lambda a: WD[:, a, e, j * P:(j + 1) * P], lambda a: HH[e % 2][:, a, :],
                                 e == 0, e == NE - 1)
                mm.then_inc(down_done, 1)

            def chunk(c, last=False):
                for e in range(NE):
                    if not last:
                        if e == X_SLOT:
                            x_turn(c + 1)
                        if e == LOGIT_SLOT:
                            logits(c + 1)
                    if e == 23:
                        down(c, e)
                        if not last:
                            cw_turn(c + 1)
                    if not (last and e >= 23):
                        gates(*after(c, e + 2))
                        spread(*after(c, e + 2))
                    if e != 23:
                        down(c, e)
                pe.wait_ge(out_hi, 2 * c + 2)
                for t in range(CT4):
                    for j in range(KD):
                        mm = pe.transpose(ACC[t // 2][:, (t % 2) * DIM + j * P:(t % 2) * DIM + (j + 1) * P],
                                          out_t[:, j, t * P:(t + 1) * P], ident[:])
                mm.then_inc(back_full, 1)

            pe.wait_ge(tab_in, 4 * 16)
            pe.wait_ge(sel_in, 16)
            pe.wait_ge(w_lo, len(pieces))
            x_turn(0)
            logits(0)
            cw_turn(0)
            gates(0, 0)
            spread(0, 0)
            gates(0, 1)
            spread(0, 1)
            with pe.Fori(0, NC - 1) as c:
                chunk(c)
            chunk(NC - 1, last=True)


def rope_tables():
    inv = (1.0 / np.float32(10000.0) ** (np.arange(0, HD, 2, dtype=np.float32) / np.float32(HD))).astype(np.float32)
    angle = np.outer(np.arange(LEN, dtype=np.float32), inv).astype(np.float32)
    cos, sin = np.cos(angle), np.sin(angle)
    return (np.tile(np.concatenate([cos, cos], 1), (2, 1)).astype(np.float32),
            np.tile(np.concatenate([-sin, sin], 1), (2, 1)).astype(np.float32))


def selectors():
    unit = np.arange(NE * P).reshape(1, NE, P)
    return ((np.arange(64) % 32)[:, None, None] == np.minimum(unit // INNER, EXPERTS)).astype(np.float32)


def constants():
    cos, sin = rope_tables()
    q, key = np.arange(P)[:, None], np.arange(P)[None, :]
    return {
        "ident": np.eye(P, dtype=np.float32), "cos": cos, "sin": sin,
        "sel_bc": np.stack([np.where(np.arange(64)[:, None] % 32 == r, np.float32(1), np.float32(0)).repeat(P, 1)
                            for r in range(2 * DSTATE)], 1),
        "smask": np.where((key > q) | (key // LEN != q // LEN), np.float32(NEG), np.float32(0)),
        "tri": (np.arange(EXPERTS)[None, :] < np.arange(EXPERTS)[:, None]).astype(np.float32).reshape(-1),
        "sel_e": selectors(),
        "xmask": np.where(np.arange(LEN)[None, :] > q % LEN, np.float32(NEG), np.float32(0)),
    }


def layouts(a):
    def kv(wk, wv):
        both = np.stack([wk.reshape(KD, P, NG, HD), wv.reshape(KD, P, NG, HD)], axis=3)
        return both.transpose(1, 0, 2, 3, 4).reshape(P, -1)

    def units(routed, shared):
        return np.concatenate([routed.reshape(ROWS, DIM), shared, np.zeros((NE * P - ROWS - SHARED, DIM), np.float32)])

    return {
        "wg": units(a["L0_ffn_eg_w"], a["L0_ffn_sg_w"]).T, "wu": units(a["L0_ffn_eu_w"], a["L0_ffn_su_w"]).T,
        "wd": units(a["L0_ffn_ed_w"].transpose(0, 2, 1), a["L0_ffn_sd_w"].T), "wr": a["L0_ffn_gate_w"].T,
        "x": a["x"].reshape(BATCH * LEN, DIM),
        "ctxT": a["ctx_2048"].reshape(NT, 2 * CTX, KD, P).transpose(0, 3, 2, 1),
        "wq": a["L0_xattn_wq"], "wo": a["L0_xattn_wo"],
        "wkv": kv(a["L0_xattn_wk"], a["L0_xattn_wv"]), "wkvc": kv(a["L0_xattn_wk_ctx"], a["L0_xattn_wv_ctx"]),
        "xproj": a["L0_attn_x_proj_w"].T, "dtproj": a["L0_attn_dt_proj_w"].T, "dtbias": a["L0_attn_dt_proj_b"].reshape(KD, P).T,
        "alog": a["L0_attn_A_log"], "skip": a["L0_attn_D"].reshape(KD, P).T,
        "ffn_wq": a["L0_ffn_wq"], "ffn_wk": a["L0_ffn_wk"], "ffn_wv": a["L0_ffn_wv"], "ffn_wo": a["L0_ffn_wo"],
        "ln1": a["L0_ffn_ln1_w"], "ln2": a["L0_ffn_ln2_w"],
        "qnorm": a["L0_xattn_q_norm_w"], "knorm": a["L0_xattn_k_norm_w"],
    }


def perceiver_block(nc, d, out):
    x_kept, x2_kept = (nc.dram_tensor(n, (BATCH * LEN, DIM), F32, kind="Internal").ap() for n in ("x_kept", "x2_kept"))
    with ExitStack() as whole:
        loads = Staged(nc, whole, 8)
        with ExitStack() as ctx:
            X = ctx.enter_context(nc.sbuf_tensor("X", [P, NT, DIM], F32))
            cross_attention(nc, X, d["x"], d, loads)
            selective_scan(nc, X, d)
            self_attention(nc, X, x_kept, x2_kept, d, loads)
        mixture_of_experts(nc, x_kept, x2_kept, d, out, loads)


def kernel(**inputs):
    import concourse.bacc as bacc
    from concourse.bass_utils import run_bass_kernel_spmd as run

    nc = bacc.Bacc("TRN2", target_bir_lowering=False, num_devices=1)
    arrays = {n: np.ascontiguousarray(v) for n, v in {**layouts({n: np.asarray(v) for n, v in inputs.items()}), **constants()}.items()}
    d = {n: nc.dram_tensor(f"{n}_dram", v.shape, F32, kind="ExternalInput").ap() for n, v in arrays.items()}
    out = nc.dram_tensor("out_dram", (BATCH * LEN, DIM), F32, kind="ExternalOutput").ap()
    perceiver_block(nc, d, out)
    r = run(nc, [{f"{n}_dram": v for n, v in arrays.items()}], core_ids=[0])
    return r.results[0]["out_dram"].reshape(BATCH, LEN, DIM)
```
